# Optimizing a Trainium2 kernel written in Bass

```python
import numpy as np
import jax
import jax.numpy as jnp

def _softmax(x, axis=-1):
    return jax.nn.softmax(x, axis=axis)

def _gelu(x):
    return jax.nn.gelu(x, approximate=True)

def _silu(x):
    return jax.nn.silu(x)

def _sigmoid(x):
    return jax.nn.sigmoid(x)

def _layernorm(x, axis=-1, eps=1e-05):
    m = jnp.mean(x, axis=axis, keepdims=True)
    v = jnp.var(x, axis=axis, keepdims=True)
    return (x - m) / jnp.sqrt(v + eps)

def _scatter_add(tgt, idx, src, axis=0):
    return tgt.at[idx].add(src)

def _segment_sum(src, seg, n):
    return jax.ops.segment_sum(src, seg, n)
kernel_name = 'mk_xattn_ffn_d4_seqx_r8_d8e9e6'

def setup_inputs(seed: int=0):
    np.random.seed(seed)
    _w = jnp.asarray

    def _rec_inputs():
        import jax
        import jax.numpy as jnp
        _rk = jax.random.key(seed)
        x = -0.0003929 + 0.9999 * jax.random.normal(jax.random.fold_in(_rk, 1), (16, 128, 256), jnp.float32)
        _lenS = 128 - jax.random.randint(jax.random.fold_in(_rk, 7), (16,), 0, max(1, 128 // 4) + 1, jnp.int32)
        _lenS2 = 128 - jax.random.randint(jax.random.fold_in(_rk, 8), (16,), 0, max(1, 128 // 4) + 1, jnp.int32)
        _ctx_1024P = jax.random.normal(jax.random.fold_in(_rk, 11), (16, 16, 128), jnp.float32)
        _ctx_1024c = jax.random.dirichlet(jax.random.fold_in(_rk, 511), 0.3 * jnp.ones((16,), jnp.float32), (16, 128))
        _ctx_1024t = jnp.einsum('bsk,bkd->bsd', _ctx_1024c, _ctx_1024P)
        _ctx_1024t = _ctx_1024t * jax.lax.rsqrt(jnp.mean(jnp.square(_ctx_1024t)) + 1e-12) * 0.953939
        ctx_1024 = 0.000227908 + 0.99994 * (_ctx_1024t + 0.3 * jax.random.normal(jax.random.fold_in(_rk, 611), (16, 128, 128), jnp.float32))
        fside_BxSx2_0 = jax.random.uniform(jax.random.fold_in(_rk, 12), (16, 128, 2), jnp.float32, 0.0, 0.999707)
        return (x, ctx_1024, fside_BxSx2_0)
    x, ctx_1024, fside_BxSx2_0 = _rec_inputs()

    def _L0_xattn_setup():
        import jax, jax.numpy as jnp
        import numpy as np
        EPS = 1e-05

        def rmsnorm(x, g, eps=EPS):
            var = jnp.mean(jnp.square(x), axis=-1, keepdims=True)
            return x * jax.lax.rsqrt(var + eps) * g
        key = jax.random.key(seed)
        ks = jax.random.split(key, 8)
        B, Sq, Skv = (2, 512, 64)
        dim, cdim, H, D = (256, 128, 16, 128)
        inner = H * D
        s = lambda f: 1.0 / np.sqrt(f)
        return {'hidden_states': jax.random.normal(ks[0], (B, Sq, dim), jnp.float32), 'encoder_hidden_states': jax.random.normal(ks[1], (B, Skv, cdim), jnp.float32), 'Wq': jax.random.normal(ks[2], (dim, inner), jnp.float32) * s(dim), 'Wk': jax.random.normal(ks[3], (cdim, inner), jnp.float32) * s(cdim), 'Wv': jax.random.normal(ks[4], (cdim, inner), jnp.float32) * s(cdim), 'Wo': jax.random.normal(ks[5], (inner, dim), jnp.float32) * s(inner), 'gq': jnp.ones((D,), jnp.float32), 'gk': jnp.ones((D,), jnp.float32)}
    _L0_xattn_all = _L0_xattn_setup()
    _L0_xattn_in = {k: v for k, v in _L0_xattn_all.items() if k in ('Wq', 'Wk', 'Wv', 'Wo', 'gq', 'gk')}
    del _L0_xattn_all

    def _L0_ffn_setup():
        import jax, jax.numpy as jnp
        import numpy as np
        N_EXPERTS = 8
        TOP_K = 2
        D_MODEL = 256
        D_FF = 128
        BATCH, SEQ = (2, 256)

        def _trunc_normal(key, shape, fan_in):
            std = jnp.sqrt(1.0 / 3.0) / jnp.sqrt(float(fan_in))
            return jax.random.truncated_normal(key, -2.0, 2.0, shape, dtype=jnp.float32) * std
        key = jax.random.key(seed)
        kx, kr, k1, k2, k3 = jax.random.split(key, 5)
        x = jax.random.normal(kx, (BATCH, SEQ, D_MODEL), dtype=jnp.float32)
        router_w = jax.random.uniform(kr, (N_EXPERTS, D_MODEL), dtype=jnp.float32, minval=-1.0, maxval=1.0) / jnp.sqrt(float(D_MODEL))
        w1 = _trunc_normal(k1, (N_EXPERTS, D_MODEL, D_FF), D_MODEL)
        w2 = _trunc_normal(k2, (N_EXPERTS, D_MODEL, D_FF), D_MODEL)
        w3 = _trunc_normal(k3, (N_EXPERTS, D_FF, D_MODEL), D_FF)
        return {'x': x, 'router_w': router_w, 'w1': w1, 'w2': w2, 'w3': w3}
    _L0_ffn_all = _L0_ffn_setup()
    _L0_ffn_in = {k: v for k, v in _L0_ffn_all.items() if k in ('router_w', 'w1', 'w2', 'w3')}
    del _L0_ffn_all

    def _L1_xattn_setup():
        import jax, jax.numpy as jnp
        import numpy as np
        B, S1, S2, DCA = (2, 256, 128, 16)
        QDIM, KDIM, H = (256, 128, 16)
        HD = QDIM // H
        SCALE = HD ** (-0.5)
        EPS = 1e-06
        DCA_WEIGHT = 1.0

        def _ln(t, w, b):
            m = jnp.mean(t, axis=-1, keepdims=True)
            v = jnp.var(t, axis=-1, keepdims=True)
            return (t - m) * jax.lax.rsqrt(v + EPS) * w + b

        def _attn(q, k, v):
            s = jnp.einsum('bhqd,bhkd->bhqk', q, k) * SCALE
            p = jax.nn.softmax(s, axis=-1)
            return jnp.einsum('bhqk,bhkd->bhqd', p, v)
        key = jax.random.key(seed)
        ks = jax.random.split(key, 8)
        w = lambda k, shape: jax.random.normal(k, shape, jnp.float32) * 0.02
        return {'x': jax.random.normal(ks[0], (B, S1, QDIM), jnp.float32), 'y': jax.random.normal(ks[1], (B, S2 + DCA, KDIM), jnp.float32), 'Wq': w(ks[2], (QDIM, QDIM)), 'bq': jnp.zeros((QDIM,), jnp.float32), 'Wk': w(ks[3], (KDIM, QDIM)), 'bk': jnp.zeros((QDIM,), jnp.float32), 'Wv': w(ks[4], (KDIM, QDIM)), 'bv': jnp.zeros((QDIM,), jnp.float32), 'Wkv_dca': w(ks[5], (KDIM, 2 * QDIM)), 'bkv_dca': jnp.zeros((2 * QDIM,), jnp.float32), 'qn_w': jnp.ones((HD,), jnp.float32), 'qn_b': jnp.zeros((HD,), jnp.float32), 'kn_w': jnp.ones((HD,), jnp.float32), 'kn_b': jnp.zeros((HD,), jnp.float32), 'kn_dca_w': jnp.ones((HD,), jnp.float32), 'kn_dca_b': jnp.zeros((HD,), jnp.float32), 'Wo': w(ks[6], (QDIM, QDIM)), 'bo': jnp.zeros((QDIM,), jnp.float32)}
    _L1_xattn_all = _L1_xattn_setup()
    _L1_xattn_in = {k: v for k, v in _L1_xattn_all.items() if k in ('Wq', 'bq', 'Wk', 'bk', 'Wv', 'bv', 'Wkv_dca', 'bkv_dca', 'qn_w', 'qn_b', 'kn_w', 'kn_b', 'kn_dca_w', 'kn_dca_b', 'Wo', 'bo')}
    del _L1_xattn_all

    def _L1_ffn_setup():
        import jax, jax.numpy as jnp
        import numpy as np
        B, S, D = (2, 256, 256)
        MOE_D = 176
        E = 16
        K = 6
        ALPHA = 0.001

        def _moe_forward(x, gate_w, w_gate, w_up, w_down):
            b, s, d = x.shape
            T = b * s
            h = x.reshape(T, d)
            logits = h @ gate_w.T
            scores = jax.nn.softmax(logits.astype(jnp.float32), axis=-1)
            topk_w, topk_idx = jax.lax.top_k(scores, K)
            cw = jnp.zeros((T, E), jnp.float32)
            cw = cw.at[jnp.arange(T)[:, None], topk_idx].add(topk_w)
            y = jnp.zeros((T, d), x.dtype)
            for e in range(E):
                g = h @ w_gate[e].T
                u = h @ w_up[e].T
                out = jax.nn.silu(g) * u @ w_down[e].T
                y = y + cw[:, e:e + 1].astype(x.dtype) * out
            counts = jnp.sum(jax.nn.one_hot(topk_idx.reshape(b, s * K), E, dtype=jnp.float32), axis=1)
            ce = counts * (E / (s * K))
            scores_bse = scores.reshape(b, s, E)
            aux = jnp.mean(jnp.sum(ce * scores_bse.mean(axis=1), axis=1)) * ALPHA
            return (y.reshape(b, s, d), aux)
        key = jax.random.key(seed)
        ks = jax.random.split(key, 5)
        sd = 1.0 / np.sqrt(D)
        sm = 1.0 / np.sqrt(MOE_D)
        return {'x': jax.random.normal(ks[0], (B, S, D), jnp.float32), 'gate_w': jax.random.normal(ks[1], (E, D), jnp.float32) * sd, 'w_gate': jax.random.normal(ks[2], (E, MOE_D, D), jnp.float32) * sd, 'w_up': jax.random.normal(ks[3], (E, MOE_D, D), jnp.float32) * sd, 'w_down': jax.random.normal(ks[4], (E, D, MOE_D), jnp.float32) * sm}
    _L1_ffn_all = _L1_ffn_setup()
    _L1_ffn_in = {k: v for k, v in _L1_ffn_all.items() if k in ('gate_w', 'w_gate', 'w_up', 'w_down')}
    del _L1_ffn_all

    def _L2_xattn_setup():
        import jax, jax.numpy as jnp
        import numpy as np
        DIM = 256
        CTX_DIM = 128
        N_HEADS = 32
        HEAD_DIM = DIM // N_HEADS
        POS_DIM = 2
        B, N, CTXN = (2, 256, 256)
        ROPE_BASE = 10000.0

        def apply_axial_rope(x, pos):
            b, n, h, d = x.shape
            p = pos.shape[-1]
            dpa = d // p
            half = dpa // 2
            freqs = ROPE_BASE ** (-jnp.arange(half, dtype=x.dtype) / half)
            ang = pos[..., :, None] * freqs
            cos = jnp.cos(ang)[:, :, None, :, :]
            sin = jnp.sin(ang)[:, :, None, :, :]
            xr = x.reshape(b, n, h, p, half, 2)
            x1, x2 = (xr[..., 0], xr[..., 1])
            out = jnp.stack([x1 * cos - x2 * sin, x1 * sin + x2 * cos], axis=-1)
            return out.reshape(b, n, h, d)
        key = jax.random.key(seed)
        ks = jax.random.split(key, 8)
        x = jax.random.normal(ks[0], (B, N, DIM), jnp.float32)
        ctx = jax.random.normal(ks[1], (B, CTXN, CTX_DIM), jnp.float32)
        pos_map = jax.random.uniform(ks[2], (B, N, POS_DIM), jnp.float32)
        ctx_pos_map = jax.random.uniform(ks[3], (B, CTXN, POS_DIM), jnp.float32)
        Wq = jax.random.normal(ks[4], (DIM, DIM), jnp.float32) / np.sqrt(DIM)
        Wkv = jax.random.normal(ks[5], (CTX_DIM, 2 * DIM), jnp.float32) / np.sqrt(CTX_DIM)
        Wout = jax.random.normal(ks[6], (DIM, DIM), jnp.float32) / np.sqrt(DIM)
        bout = jnp.zeros((DIM,), jnp.float32)
        return {'x': x, 'ctx': ctx, 'pos_map': pos_map, 'ctx_pos_map': ctx_pos_map, 'Wq': Wq, 'Wkv': Wkv, 'Wout': Wout, 'bout': bout}
    _L2_xattn_all = _L2_xattn_setup()
    _L2_xattn_in = {k: v for k, v in _L2_xattn_all.items() if k in ('Wq', 'Wkv', 'Wout', 'bout')}
    del _L2_xattn_all

    def _L2_ffn_setup():
        import jax, jax.numpy as jnp
        import numpy as np
        EPS = 1e-07

        def per_token_quant_int8(x, eps=EPS):
            absmax = jnp.max(jnp.abs(x), axis=-1, keepdims=True)
            scale = jnp.maximum(absmax, eps) / 127.0
            q = jnp.clip(jnp.round(x / scale), -128, 127).astype(jnp.int8)
            return (q, scale)
        key = jax.random.key(seed)
        k1, k2, k3, k4 = jax.random.split(key, 4)
        B, S, IN, OUT = (4, 512, 256, 256)
        x = jax.random.normal(k1, (B, S, IN), dtype=jnp.float32)
        weight = jax.random.randint(k2, (OUT, IN), -127, 128, dtype=jnp.int32).astype(jnp.int8)
        w_scale = jax.random.uniform(k3, (OUT, 1), dtype=jnp.float32) * 0.01 + 0.0001
        bias = jax.random.normal(k4, (OUT,), dtype=jnp.float32)
        return {'x': x, 'weight': weight, 'w_scale': w_scale, 'bias': bias}
    _L2_ffn_all = _L2_ffn_setup()
    _L2_ffn_in = {k: v for k, v in _L2_ffn_all.items() if k in ('weight', 'w_scale', 'bias')}
    del _L2_ffn_all

    def _L3_xattn_setup():
        import jax, jax.numpy as jnp
        import numpy as np
        DIM = 256
        CTX_DIM = 128
        N_HEADS = 32
        HEAD_DIM = DIM // N_HEADS
        POS_DIM = 2
        B, N, CTXN = (2, 256, 256)
        ROPE_BASE = 10000.0

        def apply_axial_rope(x, pos):
            b, n, h, d = x.shape
            p = pos.shape[-1]
            dpa = d // p
            half = dpa // 2
            freqs = ROPE_BASE ** (-jnp.arange(half, dtype=x.dtype) / half)
            ang = pos[..., :, None] * freqs
            cos = jnp.cos(ang)[:, :, None, :, :]
            sin = jnp.sin(ang)[:, :, None, :, :]
            xr = x.reshape(b, n, h, p, half, 2)
            x1, x2 = (xr[..., 0], xr[..., 1])
            out = jnp.stack([x1 * cos - x2 * sin, x1 * sin + x2 * cos], axis=-1)
            return out.reshape(b, n, h, d)
        key = jax.random.key(seed)
        ks = jax.random.split(key, 8)
        x = jax.random.normal(ks[0], (B, N, DIM), jnp.float32)
        ctx = jax.random.normal(ks[1], (B, CTXN, CTX_DIM), jnp.float32)
        pos_map = jax.random.uniform(ks[2], (B, N, POS_DIM), jnp.float32)
        ctx_pos_map = jax.random.uniform(ks[3], (B, CTXN, POS_DIM), jnp.float32)
        Wq = jax.random.normal(ks[4], (DIM, DIM), jnp.float32) / np.sqrt(DIM)
        Wkv = jax.random.normal(ks[5], (CTX_DIM, 2 * DIM), jnp.float32) / np.sqrt(CTX_DIM)
        Wout = jax.random.normal(ks[6], (DIM, DIM), jnp.float32) / np.sqrt(DIM)
        bout = jnp.zeros((DIM,), jnp.float32)
        return {'x': x, 'ctx': ctx, 'pos_map': pos_map, 'ctx_pos_map': ctx_pos_map, 'Wq': Wq, 'Wkv': Wkv, 'Wout': Wout, 'bout': bout}
    _L3_xattn_all = _L3_xattn_setup()
    _L3_xattn_in = {k: v for k, v in _L3_xattn_all.items() if k in ('Wq', 'Wkv', 'Wout', 'bout')}
    del _L3_xattn_all

    def _L3_ffn_setup():
        import jax, jax.numpy as jnp
        import numpy as np
        from jax import lax
        TOP_K = 4
        ROUTED_SCALING = 1.0
        RENORMALIZE = True

        def _swiglu_ffn(x, wg, wu, wd):
            return jax.nn.silu(x @ wg.T) * (x @ wu.T) @ wd.T
        key = jax.random.key(seed)
        ks = jax.random.split(key, 9)
        H, I, E = (256, 128, 16)
        s = 0.02
        return {'hidden_states': jax.random.normal(ks[0], (2, 128, H), jnp.float32), 'gate_w': jax.random.normal(ks[1], (E, H), jnp.float32) * s, 'expert_bias': jax.random.normal(ks[2], (E,), jnp.float32) * s, 'w_gate': jax.random.normal(ks[3], (E, I, H), jnp.float32) * s, 'w_up': jax.random.normal(ks[4], (E, I, H), jnp.float32) * s, 'w_down': jax.random.normal(ks[5], (E, H, I), jnp.float32) * s, 'sw_gate': jax.random.normal(ks[6], (I, H), jnp.float32) * s, 'sw_up': jax.random.normal(ks[7], (I, H), jnp.float32) * s, 'sw_down': jax.random.normal(ks[8], (H, I), jnp.float32) * s}
    _L3_ffn_all = _L3_ffn_setup()
    _L3_ffn_in = {k: v for k, v in _L3_ffn_all.items() if k in ('gate_w', 'expert_bias', 'w_gate', 'w_up', 'w_down', 'sw_gate', 'sw_up', 'sw_down')}
    del _L3_ffn_all
    return {'x': x, 'ctx_1024': ctx_1024, 'fside_BxSx2_0': fside_BxSx2_0, 'L0_xattn_Wq': _L0_xattn_in['Wq'], 'L0_xattn_Wk': _L0_xattn_in['Wk'], 'L0_xattn_Wv': _L0_xattn_in['Wv'], 'L0_xattn_Wo': _L0_xattn_in['Wo'], 'L0_xattn_gq': _L0_xattn_in['gq'], 'L0_xattn_gk': _L0_xattn_in['gk'], 'L0_ffn_router_w': _L0_ffn_in['router_w'], 'L0_ffn_w1': _L0_ffn_in['w1'], 'L0_ffn_w2': _L0_ffn_in['w2'], 'L0_ffn_w3': _L0_ffn_in['w3'], 'L1_xattn_Wq': _L1_xattn_in['Wq'], 'L1_xattn_bq': _L1_xattn_in['bq'], 'L1_xattn_Wk': _L1_xattn_in['Wk'], 'L1_xattn_bk': _L1_xattn_in['bk'], 'L1_xattn_Wv': _L1_xattn_in['Wv'], 'L1_xattn_bv': _L1_xattn_in['bv'], 'L1_xattn_Wkv_dca': _L1_xattn_in['Wkv_dca'], 'L1_xattn_bkv_dca': _L1_xattn_in['bkv_dca'], 'L1_xattn_qn_w': _L1_xattn_in['qn_w'], 'L1_xattn_qn_b': _L1_xattn_in['qn_b'], 'L1_xattn_kn_w': _L1_xattn_in['kn_w'], 'L1_xattn_kn_b': _L1_xattn_in['kn_b'], 'L1_xattn_kn_dca_w': _L1_xattn_in['kn_dca_w'], 'L1_xattn_kn_dca_b': _L1_xattn_in['kn_dca_b'], 'L1_xattn_Wo': _L1_xattn_in['Wo'], 'L1_xattn_bo': _L1_xattn_in['bo'], 'L1_ffn_gate_w': _L1_ffn_in['gate_w'], 'L1_ffn_w_gate': _L1_ffn_in['w_gate'], 'L1_ffn_w_up': _L1_ffn_in['w_up'], 'L1_ffn_w_down': _L1_ffn_in['w_down'], 'L2_xattn_Wq': _L2_xattn_in['Wq'], 'L2_xattn_Wkv': _L2_xattn_in['Wkv'], 'L2_xattn_Wout': _L2_xattn_in['Wout'], 'L2_xattn_bout': _L2_xattn_in['bout'], 'L2_ffn_weight': _L2_ffn_in['weight'], 'L2_ffn_w_scale': _L2_ffn_in['w_scale'], 'L2_ffn_bias': _L2_ffn_in['bias'], 'L3_xattn_Wq': _L3_xattn_in['Wq'], 'L3_xattn_Wkv': _L3_xattn_in['Wkv'], 'L3_xattn_Wout': _L3_xattn_in['Wout'], 'L3_xattn_bout': _L3_xattn_in['bout'], 'L3_ffn_gate_w': _L3_ffn_in['gate_w'], 'L3_ffn_expert_bias': _L3_ffn_in['expert_bias'], 'L3_ffn_w_gate': _L3_ffn_in['w_gate'], 'L3_ffn_w_up': _L3_ffn_in['w_up'], 'L3_ffn_w_down': _L3_ffn_in['w_down'], 'L3_ffn_sw_gate': _L3_ffn_in['sw_gate'], 'L3_ffn_sw_up': _L3_ffn_in['sw_up'], 'L3_ffn_sw_down': _L3_ffn_in['sw_down']}

def reference(x, ctx_1024, fside_BxSx2_0, L0_xattn_Wq, L0_xattn_Wk, L0_xattn_Wv, L0_xattn_Wo, L0_xattn_gq, L0_xattn_gk, L0_ffn_router_w, L0_ffn_w1, L0_ffn_w2, L0_ffn_w3, L1_xattn_Wq, L1_xattn_bq, L1_xattn_Wk, L1_xattn_bk, L1_xattn_Wv, L1_xattn_bv, L1_xattn_Wkv_dca, L1_xattn_bkv_dca, L1_xattn_qn_w, L1_xattn_qn_b, L1_xattn_kn_w, L1_xattn_kn_b, L1_xattn_kn_dca_w, L1_xattn_kn_dca_b, L1_xattn_Wo, L1_xattn_bo, L1_ffn_gate_w, L1_ffn_w_gate, L1_ffn_w_up, L1_ffn_w_down, L2_xattn_Wq, L2_xattn_Wkv, L2_xattn_Wout, L2_xattn_bout, L2_ffn_weight, L2_ffn_w_scale, L2_ffn_bias, L3_xattn_Wq, L3_xattn_Wkv, L3_xattn_Wout, L3_xattn_bout, L3_ffn_gate_w, L3_ffn_expert_bias, L3_ffn_w_gate, L3_ffn_w_up, L3_ffn_w_down, L3_ffn_sw_gate, L3_ffn_sw_up, L3_ffn_sw_down):
    import jax
    import jax.numpy as jnp

    def _L0_xattn_ref(hidden_states, encoder_hidden_states, Wq, Wk, Wv, Wo, gq, gk):
        import jax, jax.numpy as jnp
        import numpy as np
        EPS = 1e-05

        def rmsnorm(x, g, eps=EPS):
            var = jnp.mean(jnp.square(x), axis=-1, keepdims=True)
            return x * jax.lax.rsqrt(var + eps) * g
        B, Sq, _ = hidden_states.shape
        Skv = encoder_hidden_states.shape[1]
        D = gq.shape[0]
        H = Wq.shape[1] // D
        scale = 1.0 / np.sqrt(D)
        q = (hidden_states @ Wq).reshape(B, Sq, H, D)
        k = (encoder_hidden_states @ Wk).reshape(B, Skv, H, D)
        v = (encoder_hidden_states @ Wv).reshape(B, Skv, H, D)
        q = rmsnorm(q, gq)
        k = rmsnorm(k, gk)
        scores = jnp.einsum('bqhd,bkhd->bhqk', q, k) * scale
        attn = jax.nn.softmax(scores, axis=-1)
        out = jnp.einsum('bhqk,bkhd->bqhd', attn, v)
        out = out.reshape(B, Sq, H * D)
        return out @ Wo

    def _L0_ffn_ref(x, router_w, w1, w2, w3):
        import jax, jax.numpy as jnp
        import numpy as np
        N_EXPERTS = 8
        TOP_K = 2
        D_MODEL = 256
        D_FF = 128
        BATCH, SEQ = (2, 256)

        def _trunc_normal(key, shape, fan_in):
            std = jnp.sqrt(1.0 / 3.0) / jnp.sqrt(float(fan_in))
            return jax.random.truncated_normal(key, -2.0, 2.0, shape, dtype=jnp.float32) * std
        B, S, D = x.shape
        xf = x.reshape(-1, D)
        n_tokens = xf.shape[0]
        logits = xf @ router_w.T
        topk_vals, topk_idx = jax.lax.top_k(logits, TOP_K)
        topk_weights = jax.nn.softmax(topk_vals, axis=-1)
        gate = jax.nn.silu(jnp.einsum('nd,edf->enf', xf, w1))
        value = jnp.einsum('nd,edf->enf', xf, w2)
        expert_out = jnp.einsum('enf,efd->end', gate * value, w3)
        tok = jnp.arange(n_tokens)[:, None]
        selected = expert_out[topk_idx, tok]
        out = jnp.sum(selected * topk_weights[..., None], axis=1)
        return out.reshape(B, S, D)

    def _L1_xattn_ref(x, y, Wq, bq, Wk, bk, Wv, bv, Wkv_dca, bkv_dca, qn_w, qn_b, kn_w, kn_b, kn_dca_w, kn_dca_b, Wo, bo):
        import jax, jax.numpy as jnp
        import numpy as np
        B, S1, S2, DCA = (2, 256, 128, 16)
        QDIM, KDIM, H = (256, 128, 16)
        HD = QDIM // H
        SCALE = HD ** (-0.5)
        EPS = 1e-06
        DCA_WEIGHT = 1.0

        def _ln(t, w, b):
            m = jnp.mean(t, axis=-1, keepdims=True)
            v = jnp.var(t, axis=-1, keepdims=True)
            return (t - m) * jax.lax.rsqrt(v + EPS) * w + b

        def _attn(q, k, v):
            s = jnp.einsum('bhqd,bhkd->bhqk', q, k) * SCALE
            p = jax.nn.softmax(s, axis=-1)
            return jnp.einsum('bhqk,bhkd->bhqd', p, v)
        b, s1, _ = x.shape
        y_dca = y[:, -DCA:, :]
        y_main = y[:, :-DCA, :]
        kv_dca = (y_dca @ Wkv_dca + bkv_dca).reshape(b, DCA, 2, H, HD)
        k_dca = _ln(kv_dca[:, :, 0], kn_dca_w, kn_dca_b)
        v_dca = kv_dca[:, :, 1]
        s2 = y_main.shape[1]
        q = _ln((x @ Wq + bq).reshape(b, s1, H, HD), qn_w, qn_b)
        kv = jnp.concatenate([y_main @ Wk + bk, y_main @ Wv + bv], axis=-1)
        kv = kv.reshape(b, s2, H, 2 * HD)
        k = _ln(kv[..., :HD], kn_w, kn_b)
        v = kv[..., HD:]
        qT = q.transpose(0, 2, 1, 3)
        ctx = _attn(qT, k.transpose(0, 2, 1, 3), v.transpose(0, 2, 1, 3))
        ctx = ctx.transpose(0, 2, 1, 3).reshape(b, s1, QDIM)
        ctx_dca = _attn(qT, k_dca.transpose(0, 2, 1, 3), v_dca.transpose(0, 2, 1, 3))
        ctx_dca = ctx_dca.transpose(0, 2, 1, 3).reshape(b, s1, QDIM)
        ctx = ctx + DCA_WEIGHT * ctx_dca
        return ctx @ Wo + bo

    def _L1_ffn_ref(x, gate_w, w_gate, w_up, w_down):
        import jax, jax.numpy as jnp
        import numpy as np
        B, S, D = (2, 256, 256)
        MOE_D = 176
        E = 16
        K = 6
        ALPHA = 0.001

        def _moe_forward(x, gate_w, w_gate, w_up, w_down):
            b, s, d = x.shape
            T = b * s
            h = x.reshape(T, d)
            logits = h @ gate_w.T
            scores = jax.nn.softmax(logits.astype(jnp.float32), axis=-1)
            topk_w, topk_idx = jax.lax.top_k(scores, K)
            cw = jnp.zeros((T, E), jnp.float32)
            cw = cw.at[jnp.arange(T)[:, None], topk_idx].add(topk_w)
            y = jnp.zeros((T, d), x.dtype)
            for e in range(E):
                g = h @ w_gate[e].T
                u = h @ w_up[e].T
                out = jax.nn.silu(g) * u @ w_down[e].T
                y = y + cw[:, e:e + 1].astype(x.dtype) * out
            counts = jnp.sum(jax.nn.one_hot(topk_idx.reshape(b, s * K), E, dtype=jnp.float32), axis=1)
            ce = counts * (E / (s * K))
            scores_bse = scores.reshape(b, s, E)
            aux = jnp.mean(jnp.sum(ce * scores_bse.mean(axis=1), axis=1)) * ALPHA
            return (y.reshape(b, s, d), aux)
        y, _aux = _moe_forward(x, gate_w, w_gate, w_up, w_down)
        return y

    def _L2_xattn_ref(x, ctx, pos_map, ctx_pos_map, Wq, Wkv, Wout, bout):
        import jax, jax.numpy as jnp
        import numpy as np
        DIM = 256
        CTX_DIM = 128
        N_HEADS = 32
        HEAD_DIM = DIM // N_HEADS
        POS_DIM = 2
        B, N, CTXN = (2, 256, 256)
        ROPE_BASE = 10000.0

        def apply_axial_rope(x, pos):
            b, n, h, d = x.shape
            p = pos.shape[-1]
            dpa = d // p
            half = dpa // 2
            freqs = ROPE_BASE ** (-jnp.arange(half, dtype=x.dtype) / half)
            ang = pos[..., :, None] * freqs
            cos = jnp.cos(ang)[:, :, None, :, :]
            sin = jnp.sin(ang)[:, :, None, :, :]
            xr = x.reshape(b, n, h, p, half, 2)
            x1, x2 = (xr[..., 0], xr[..., 1])
            out = jnp.stack([x1 * cos - x2 * sin, x1 * sin + x2 * cos], axis=-1)
            return out.reshape(b, n, h, d)
        b, n, _ = x.shape
        ctx_n = ctx.shape[1]
        q = (x @ Wq).reshape(b, n, N_HEADS, HEAD_DIM)
        k, v = jnp.split(ctx @ Wkv, 2, axis=-1)
        k = k.reshape(b, ctx_n, N_HEADS, HEAD_DIM)
        v = v.reshape(b, ctx_n, N_HEADS, HEAD_DIM)
        q = apply_axial_rope(q, pos_map)
        k = apply_axial_rope(k, ctx_pos_map)
        scale = 1.0 / np.sqrt(HEAD_DIM).astype(np.float32)
        logits = jnp.einsum('bqhd,bkhd->bhqk', q, k) * scale
        w = jax.nn.softmax(logits, axis=-1)
        attn = jnp.einsum('bhqk,bkhd->bqhd', w, v)
        attn = attn.reshape(b, n, N_HEADS * HEAD_DIM)
        return attn @ Wout + bout

    def _L2_ffn_ref(x, weight, w_scale, bias):
        import jax, jax.numpy as jnp
        import numpy as np
        EPS = 1e-07

        def per_token_quant_int8(x, eps=EPS):
            absmax = jnp.max(jnp.abs(x), axis=-1, keepdims=True)
            scale = jnp.maximum(absmax, eps) / 127.0
            q = jnp.clip(jnp.round(x / scale), -128, 127).astype(jnp.int8)
            return (q, scale)
        q, in_scale = per_token_quant_int8(x)
        acc = jnp.einsum('bsk,nk->bsn', q, weight, preferred_element_type=jnp.int32)
        out = acc.astype(jnp.float32) * in_scale * w_scale[:, 0] + bias
        return out.astype(jnp.float16)

    def _L3_xattn_ref(x, ctx, pos_map, ctx_pos_map, Wq, Wkv, Wout, bout):
        import jax, jax.numpy as jnp
        import numpy as np
        DIM = 256
        CTX_DIM = 128
        N_HEADS = 32
        HEAD_DIM = DIM // N_HEADS
        POS_DIM = 2
        B, N, CTXN = (2, 256, 256)
        ROPE_BASE = 10000.0

        def apply_axial_rope(x, pos):
            b, n, h, d = x.shape
            p = pos.shape[-1]
            dpa = d // p
            half = dpa // 2
            freqs = ROPE_BASE ** (-jnp.arange(half, dtype=x.dtype) / half)
            ang = pos[..., :, None] * freqs
            cos = jnp.cos(ang)[:, :, None, :, :]
            sin = jnp.sin(ang)[:, :, None, :, :]
            xr = x.reshape(b, n, h, p, half, 2)
            x1, x2 = (xr[..., 0], xr[..., 1])
            out = jnp.stack([x1 * cos - x2 * sin, x1 * sin + x2 * cos], axis=-1)
            return out.reshape(b, n, h, d)
        b, n, _ = x.shape
        ctx_n = ctx.shape[1]
        q = (x @ Wq).reshape(b, n, N_HEADS, HEAD_DIM)
        k, v = jnp.split(ctx @ Wkv, 2, axis=-1)
        k = k.reshape(b, ctx_n, N_HEADS, HEAD_DIM)
        v = v.reshape(b, ctx_n, N_HEADS, HEAD_DIM)
        q = apply_axial_rope(q, pos_map)
        k = apply_axial_rope(k, ctx_pos_map)
        scale = 1.0 / np.sqrt(HEAD_DIM).astype(np.float32)
        logits = jnp.einsum('bqhd,bkhd->bhqk', q, k) * scale
        w = jax.nn.softmax(logits, axis=-1)
        attn = jnp.einsum('bhqk,bkhd->bqhd', w, v)
        attn = attn.reshape(b, n, N_HEADS * HEAD_DIM)
        return attn @ Wout + bout

    def _L3_ffn_ref(hidden_states, gate_w, expert_bias, w_gate, w_up, w_down, sw_gate, sw_up, sw_down):
        import jax, jax.numpy as jnp
        import numpy as np
        from jax import lax
        TOP_K = 4
        ROUTED_SCALING = 1.0
        RENORMALIZE = True

        def _swiglu_ffn(x, wg, wu, wd):
            return jax.nn.silu(x @ wg.T) * (x @ wu.T) @ wd.T
        orig_shape = hidden_states.shape
        H = orig_shape[-1]
        x = hidden_states.reshape(-1, H)
        T = x.shape[0]
        logits = x.astype(jnp.float32) @ gate_w.T
        scores = jax.nn.sigmoid(logits)
        _, topk_idx = lax.top_k(scores + expert_bias[None, :], TOP_K)
        topk_w = jnp.take_along_axis(scores, topk_idx, axis=-1)
        if RENORMALIZE:
            topk_w = topk_w / jnp.sum(topk_w, axis=-1, keepdims=True)
        topk_w = topk_w * ROUTED_SCALING
        E = gate_w.shape[0]
        combine = jnp.zeros((T, E), dtype=x.dtype).at[jnp.arange(T)[:, None], topk_idx].set(topk_w.astype(x.dtype))

        def step(acc, ws):
            wg, wu, wd, cw = ws
            return (acc + cw[:, None] * _swiglu_ffn(x, wg, wu, wd), None)
        routed, _ = lax.scan(step, jnp.zeros_like(x), (w_gate, w_up, w_down, combine.T))
        shared = _swiglu_ffn(x, sw_gate, sw_up, sw_down)
        return (routed + shared).reshape(orig_shape)
    x = x + _L0_xattn_ref(_layernorm(x, axis=-1), ctx_1024, L0_xattn_Wq, L0_xattn_Wk, L0_xattn_Wv, L0_xattn_Wo, L0_xattn_gq, L0_xattn_gk)
    x = x + _L0_ffn_ref(_layernorm(x, axis=-1), L0_ffn_router_w, L0_ffn_w1, L0_ffn_w2, L0_ffn_w3)
    x = x + _L1_xattn_ref(_layernorm(x, axis=-1), ctx_1024, L1_xattn_Wq, L1_xattn_bq, L1_xattn_Wk, L1_xattn_bk, L1_xattn_Wv, L1_xattn_bv, L1_xattn_Wkv_dca, L1_xattn_bkv_dca, L1_xattn_qn_w, L1_xattn_qn_b, L1_xattn_kn_w, L1_xattn_kn_b, L1_xattn_kn_dca_w, L1_xattn_kn_dca_b, L1_xattn_Wo, L1_xattn_bo)
    x = x + _L1_ffn_ref(_layernorm(x, axis=-1), L1_ffn_gate_w, L1_ffn_w_gate, L1_ffn_w_up, L1_ffn_w_down)
    x = x + _L2_xattn_ref(_layernorm(x, axis=-1), ctx_1024, fside_BxSx2_0, fside_BxSx2_0, L2_xattn_Wq, L2_xattn_Wkv, L2_xattn_Wout, L2_xattn_bout)
    x = x + _L2_ffn_ref(_layernorm(x, axis=-1), L2_ffn_weight, L2_ffn_w_scale, L2_ffn_bias)
    x = x + _L3_xattn_ref(_layernorm(x, axis=-1), ctx_1024, fside_BxSx2_0, fside_BxSx2_0, L3_xattn_Wq, L3_xattn_Wkv, L3_xattn_Wout, L3_xattn_bout)
    x = x + _L3_ffn_ref(_layernorm(x, axis=-1), L3_ffn_gate_w, L3_ffn_expert_bias, L3_ffn_w_gate, L3_ffn_w_up, L3_ffn_w_down, L3_ffn_sw_gate, L3_ffn_sw_up, L3_ffn_sw_down)
    return x

_drawn_inputs = setup_inputs


def setup_inputs(seed=0):
    import zlib

    import numpy as np

    out = dict(_drawn_inputs(seed))
    spreads = {'L0_xattn_gq': (1.0, 0.2),
     'L0_xattn_gk': (1.0, 0.2),
     'L1_xattn_bq': (0.0, 0.65),
     'L1_xattn_bk': (0.0, 0.358),
     'L1_xattn_bv': (0.0, 0.369),
     'L1_xattn_bkv_dca': (0.0, 0.1),
     'L1_xattn_qn_w': (1.0, 0.6),
     'L1_xattn_qn_b': (0.0, 0.8),
     'L1_xattn_kn_w': (1.0, 0.6),
     'L1_xattn_kn_b': (0.0, 0.8),
     'L1_xattn_kn_dca_w': (1.0, 0.6),
     'L1_xattn_kn_dca_b': (0.0, 0.8),
     'L1_xattn_bo': (0.0, 0.1),
     'L2_xattn_bout': (0.0, 0.1),
     'L3_xattn_bout': (0.0, 0.588)}
    factors = {'L3_ffn_gate_w': 8.0,
     'L3_ffn_expert_bias': 8.0,
     'L3_ffn_w_gate': 8.0,
     'L3_ffn_w_up': 8.0,
     'L3_ffn_w_down': 8.0,
     'L3_ffn_sw_gate': 8.0,
     'L3_ffn_sw_up': 8.0,
     'L3_ffn_sw_down': 8.0}
    for name, (base, spread) in spreads.items():
        noise = np.random.default_rng([zlib.crc32(name.encode()), seed]).standard_normal(out[name].shape)
        drawn = base * np.exp(spread * noise) if base else spread * noise
        out[name] = jnp.asarray(drawn.astype(out[name].dtype))
    for name, factor in factors.items():
        out[name] = (out[name] * factor).astype(out[name].dtype)
    return out
```

```python
import concourse.bass as bass
from concourse import mybir
from contextlib import ExitStack

F32 = mybir.dt.float32
BF16 = mybir.dt.bfloat16
F16 = mybir.dt.float16
I8 = mybir.dt.int8
ALU = mybir.AluOpType
ACT = mybir.ActivationFunctionType
AX = mybir.AxisListType
ds = bass.ds

P = 128
B = 16
DM = 256
KC = DM // P
CD = 128
GT = 4
NG = B // GT
LN_EPS = 1e-5
MAGIC = 12582912.0
TWO_PI = (6.28125, 1.9350051879882812e-3, 3.019916050561733e-7)
PI_LOW = 3.1415925


def bc(ap, axis, n):
    a = ap.unsqueeze(axis)
    shape = list(a.shape)
    shape[axis] = n
    return a.to_broadcast(shape)


def wait(eng, sem, n):
    if isinstance(n, int) and n <= 0:
        return
    eng.wait_ge(sem, n)


class Core:

    def __init__(self, nc, dram, stack):
        self.nc, self.dram, self.stack = nc, dram, stack
        self.passing, self.used = ExitStack(), []

    def sb(self, name, shape, dt=F32, stack=None):
        return (stack or self.stack).enter_context(self.nc.sbuf_tensor(name, shape, dt))

    def ps(self, name, shape, dt=F32, stack=None):
        return (stack or self.stack).enter_context(self.nc.psum_tensor(name, shape, dt))

    def sem(self, name, lasting=False):
        s = (self.stack if lasting else self.passing).enter_context(self.nc.semaphore(name))
        if not lasting:
            self.used.append(s)
        return s

    def recycle(self):
        with self.nc.Block() as block:
            @block.gpsimd
            def _(pool):
                for s in self.used:
                    pool.sem_clear(s)
        self.used = []
        self.passing.close()


def load_everything_small(c):
    nc, d = c.nc, c.dram
    c.x = c.sb("x", [P, B, DM])
    c.xT = c.sb("xT", [P, KC, B * P])
    c.ident = c.sb("ident", [P, P])
    c.ident_b = c.sb("ident_b", [P, P], BF16)
    c.mask8 = c.sb("mask8", [P, 4])
    c.mask16 = c.sb("mask16", [P, 4])
    c.mask_seg = c.sb("mask_seg", [P, 2])
    c.sel_seg = c.sb("sel_seg", [2, P])
    c.ones_row = c.sb("ones_row", [1, P])
    c.neg_half = c.sb("neg_half", [P, 32])
    c.pos = c.sb("pos", [P, B, 2])
    c.g0 = c.sb("g0", [P, 2])
    c.gqk = c.sb("gqk", [P, 1])
    w = c.w = {}
    w["L0q"] = c.sb("w_L0q", [P, KC, 2048])
    w["L0k"] = c.sb("w_L0k", [P, 2048])
    w["L0v"] = c.sb("w_L0v", [P, 2048])
    w["L0o"] = c.sb("w_L0o", [P, 16, DM])
    w["L1q"] = c.sb("w_L1q", [P, KC, DM])
    w["L1k"] = c.sb("w_L1k", [P, DM])
    w["L1v"] = c.sb("w_L1v", [P, DM])
    w["L1d"] = c.sb("w_L1d", [P, 2 * DM])
    w["L1o"] = c.sb("w_L1o", [P, KC, DM])
    w["L1bq"] = c.sb("w_L1bq", [1, DM])
    w["L1bkv"] = c.sb("w_L1bkv", [2, 2 * DM])
    w["L1bo"] = c.sb("w_L1bo", [1, DM])
    w["L1nw"] = c.sb("w_L1nw", [P, 2, 16])
    w["L1nb"] = c.sb("w_L1nb", [P, 2, 16])
    for m in ("L2", "L3"):
        w[m + "q"] = c.sb(f"w_{m}q", [P, KC, DM])
        w[m + "kv"] = c.sb(f"w_{m}kv", [P, 2 * DM])
        w[m + "o"] = c.sb(f"w_{m}o", [P, KC, DM])
        w[m + "bo"] = c.sb(f"w_{m}bo", [1, DM])
    w["fq8"] = c.sb("w_fq8", [P, KC, DM // 4], mybir.dt.int32)
    w["fsc"] = c.sb("w_fsc", [P, DM])
    w["fb"] = c.sb("w_fb", [P, DM])
    c.s_first = c.sem("first_loads", True)
    c.s_late = c.sem("late_loads", True)

    def row(a):
        return a.rearrange("(o n) -> o n", o=1)

    def down(a, p=P):
        return row(a).to_broadcast([p, a.shape[0]])

    first = [
        (c.x[:], d["x"].rearrange("b p d -> p b d")),
        (c.ident[:], d["c_ident"]),
        (c.neg_half[:], d["c_neg_half"]),
        (w["L0q"][:], d["L0_xattn_Wq"].rearrange("(k p) n -> p k n", p=P)),
        (w["L0k"][:], d["L0_xattn_Wk"]),
        (w["L0v"][:], d["L0_xattn_Wv"]),
        (c.g0[:, 0:1], d["L0_xattn_gq"].rearrange("(n o) -> n o", o=1)),
        (c.g0[:, 1:2], d["L0_xattn_gk"].rearrange("(n o) -> n o", o=1)),
        (w["L0o"][:], d["L0_xattn_Wo"].rearrange("(h p) n -> p h n", p=P)),
    ]
    seg = P - 16
    late = [
        (c.mask8[:], d["c_mask8"]), (c.mask16[:], d["c_mask16"]),
        (c.mask_seg[:], d["c_mask_seg"]), (c.sel_seg[:], d["c_sel_seg"]),
        (c.ones_row[:], d["c_ones"]),
        (c.pos[:], d["fside_BxSx2_0"].rearrange("b p a -> p b a")),
        (w["L1q"][:], d["L1_xattn_Wq"].rearrange("(k p) n -> p k n", p=P)),
        (w["L1k"][:], d["L1_k"]), (w["L1v"][:], d["L1_v"]),
        (w["L1d"][:], d["L1_xattn_Wkv_dca"]),
        (w["L1o"][:], d["L1_xattn_Wo"].rearrange("(k p) n -> p k n", p=P)),
        (w["L1bq"][:], row(d["L1_xattn_bq"])), (w["L1bo"][:], row(d["L1_xattn_bo"])),
        (w["L1bkv"][0:1, 0:DM], row(d["L1_k_bias"])),
        (w["L1bkv"][0:1, DM:], row(d["L1_v_bias"])),
        (w["L1bkv"][1:2, :], row(d["L1_xattn_bkv_dca"])),
        (w["L1nw"][:, 0, :], down(d["L1_xattn_qn_w"])), (w["L1nb"][:, 0, :], down(d["L1_xattn_qn_b"])),
        (w["L1nw"][0:seg, 1, :], down(d["L1_xattn_kn_w"], seg)),
        (w["L1nb"][0:seg, 1, :], down(d["L1_xattn_kn_b"], seg)),
        (w["L1nw"][seg:, 1, :], down(d["L1_xattn_kn_dca_w"], 16)),
        (w["L1nb"][seg:, 1, :], down(d["L1_xattn_kn_dca_b"], 16)),
        (w["fq8"][:], d["L2_ffn_weight"].rearrange("(k p) n -> p k n", p=P)),
        (w["fsc"][:], down(d["L2_ffn_w_scale"].rearrange("n o -> (n o)"))),
        (w["fb"][:], down(d["L2_ffn_bias"])),
    ]
    for m in ("L2", "L3"):
        late += [
            (w[m + "q"][:], d[m + "_xattn_Wq"].rearrange("(k p) n -> p k n", p=P)),
            (w[m + "kv"][:], d[m + "_xattn_Wkv"]),
            (w[m + "o"][:], d[m + "_xattn_Wout"].rearrange("(k p) n -> p k n", p=P)),
            (w[m + "bo"][:], row(d[m + "_xattn_bout"])),
        ]
    c.n_first, c.n_late = 16 * len(first), 16 * len(late)
    c.first, c.late = first, late


class TileNorm:

    def __init__(self, c, name, stack):
        self.c = c
        self.stats = c.sb(name + "_stats", [P, 6], F32, stack)
        self.mv = c.sb(name + "_mv", [P, 2], F32, stack)
        self.hold = c.sb(name + "_hold", [P, 1], F32, stack)
        self.ve = c.sb(name + "_ve", [P, 1], F32, stack)
        self.rstd = c.sb(name + "_rstd", [P, 1], F32, stack)
        self.xn = c.sb(name + "_xn", [P, DM], F32, stack)
        self.s_st = c.sem(name + "_stats")
        self.s_rs = c.sem(name + "_rstd")
        self.s_xn = c.sem(name + "_normed")

    def dve_stats(self, dve, b, n=None):
        n = b if n is None else n
        v = self.c.nc.vector
        wait(dve, self.s_xn, n)
        v.bn_stats(self.stats[:], self.c.x[:, ds(b, 1), :].rearrange("p a d -> p (a d)")).then_inc(self.s_st, 1)
        wait(dve, self.s_st, n * 3 + 1)
        v.memset(self.hold[:], 0.0)
        v.bn_aggr(self.mv[:], self.stats[:]).then_inc(self.s_st, 1)
        wait(dve, self.s_st, n * 3 + 2)
        v.tensor_scalar(self.ve[:], self.mv[:, 1:2], LN_EPS, None, ALU.add).then_inc(self.s_st, 1)

    def pool_rstd(self, pool, n):
        wait(pool, self.s_st, n * 3 + 3)
        self.c.nc.gpsimd.tensor_tensor(self.rstd[:], self.ve[:], self.c.neg_half[:, 0:1], ALU.pow).then_inc(self.s_rs, 1)

    def dve_apply(self, dve, b, s_read, n_read, n=None):
        n = b if n is None else n
        wait(dve, self.s_rs, n + 1)
        wait(dve, s_read, n_read)
        self.c.nc.vector.tensor_scalar(self.xn[:], self.c.x[:, ds(b, 1), :].rearrange("p a d -> p (a d)"),
                                       self.mv[:, 0:1], self.rstd[:], ALU.subtract, ALU.mult).then_inc(self.s_xn, 1)


def l0_attention(c):
    nc, w = c.nc, c.w
    NH, HG = 16, 4
    G = NH // HG
    W = HG * P
    SCALE = P ** -0.5
    with ExitStack() as st:
        ln = TileNorm(c, "l0a", st)
        xT = c.sb("l0_xT", [P, KC, P], F32, st)
        ctx = c.sb("l0_ctx", [P, 2, P], F32, st)
        sq = c.sb("l0_sq", [P, 2 * HG, P], F32, st)
        ss = c.sb("l0_ss", [P, 2 * HG], F32, st)
        ms = c.sb("l0_ms", [P, 2 * HG], F32, st)
        rs = c.sb("l0_rs", [P, 2 * HG], F32, st)
        qk = c.sb("l0_qk", [P, 2 * HG, P], F32, st)
        qT = c.sb("l0_qT", [P, 2, HG, P], F32, st)
        kT = c.sb("l0_kT", [P, 2, HG, P], F32, st)
        v = c.sb("l0_v", [P, 2, HG, P], F32, st)
        mx = c.sb("l0_mx", [P, HG], F32, st)
        df = c.sb("l0_df", [P, HG, P], F32, st)
        pr = c.sb("l0_pr", [P, HG, P], F32, st)
        sm = c.sb("l0_sm", [P, HG], F32, st)
        rl = c.sb("l0_rl", [P, HG], F32, st)
        pn = c.sb("l0_pn", [P, HG, P], F32, st)
        pT = c.sb("l0_pT", [P, HG, P], F32, st)
        oT = c.sb("l0_oT", [P, HG, P], F32, st)
        psQK = c.ps("l0_psQK", [P, 2 * HG, P], F32, st)
        psQT = c.ps("l0_psQT", [P, 2 * HG, P], F32, st)
        psV = c.ps("l0_psV", [P, HG, P], F32, st)
        psS = c.ps("l0_psS", [P, HG, P], F32, st)
        psP = c.ps("l0_psP", [P, HG, P], F32, st)
        psY = c.ps("l0_psY", [P, 512], F32, st)
        S = lambda n: c.sem("l0_" + n)
        s_ctx, s_g = S("ctx"), S("gqk")
        s_xt, s_xT = S("x_transposed"), S("xT_copied")
        s_qk, s_v, s_vc = S("qk_made"), S("v_made"), S("v_copied")
        s_sq, s_ss, s_ms, s_rs, s_qn = S("squares"), S("sums"), S("means"), S("rrms"), S("qk_normed")
        s_qt, s_qT, s_kT = S("qk_transposed"), S("qT_copied"), S("kT_copied")
        s_s, s_mx, s_df, s_e = S("scores"), S("maxima"), S("shifted"), S("exps")
        s_sm, s_rl, s_pn = S("exp_sums"), S("inverse_sums"), S("probs")
        s_pt, s_pT, s_o, s_oT = S("probs_transposed"), S("probs_T_copied"), S("out_made"), S("out_copied")
        s_y, s_x = S("projected"), S("x_updated")

        def pe_A(pe, b):
            wait(pe, ln.s_xn, b + 1)
            wait(pe, s_pT, b * G - 1)
            for k in range(KC):
                last = nc.tensor.transpose(psP[:, k, :], ln.xn[:, k * P:(k + 1) * P], c.ident[:])
            last.then_inc(s_xt, 1)

        def pe_F(pe, b, g):
            n = b * G + g
            wait(pe, s_xT, b + 1)
            wait(pe, s_ctx, b * 16 + 16)
            wait(pe, s_qn, n)
            for k in range(KC):
                nc.tensor.matmul(psQK[:, 0:HG, :], xT[:, k, :], w["L0q"][:, k, g * W:(g + 1) * W],
                                 start=k == 0, stop=k == KC - 1)
            nc.tensor.matmul(psQK[:, HG:, :], cx(b), w["L0k"][:, g * W:(g + 1) * W],
                             start=True, stop=True).then_inc(s_qk, 1)
            wait(pe, s_oT, n - 1)
            nc.tensor.matmul(psV[:], cx(b), w["L0v"][:, g * W:(g + 1) * W],
                             start=True, stop=True).then_inc(s_v, 1)

        def cx(b):
            return ctx[:, 0, :]

        def pe_FT(pe, b, g):
            n = b * G + g
            wait(pe, s_qn, n + 1)
            wait(pe, s_kT, n)
            for h in range(2 * HG):
                last = nc.tensor.transpose(psQT[:, h, :], qk[:, h, :], c.ident[:])
            last.then_inc(s_qt, 1)

        def pe_S(pe, b, g):
            n = b * G + g
            wait(pe, s_kT, n + 1)
            wait(pe, s_df, n)
            for h in range(HG):
                last = nc.tensor.matmul(psS[:, h, :], qT[:, g % 2, h, :], kT[:, g % 2, h, :], start=True, stop=True)
            last.then_inc(s_s, 1)

        def pe_T(pe, b, g, more):
            n = b * G + g
            wait(pe, s_pn, n + 1)
            wait(pe, s_pT, n)
            if g == G - 1 and more:
                wait(pe, s_xT, b + 2)
            for h in range(HG):
                last = nc.tensor.transpose(psP[:, h, :], pn[:, h, :], c.ident[:])
            last.then_inc(s_pt, 1)

        def pe_O(pe, b, g, go):
            n = b * G + g
            wait(pe, s_pT, n + 1)
            wait(pe, s_vc, n + (2 if go else 1))
            for h in range(HG):
                last = nc.tensor.matmul(psV[:, h, :], v[:, g % 2, h, :], pT[:, h, :], start=True, stop=True)
            last.then_inc(s_o, 1)

        def pe_Y(pe, b, g):
            n = b * G + g
            wait(pe, s_oT, n + 1)
            if g == 0:
                wait(pe, s_x, b)
            for h in range(HG):
                last = nc.tensor.matmul(psY[:, 0:DM], oT[:, h, :], w["L0o"][:, g * HG + h, :],
                                        start=g == 0 and h == 0, stop=g == G - 1 and h == HG - 1)
            if g == G - 1:
                last.then_inc(s_y, 1)
            else:
                last.then_inc(s_ypart, 1)
        s_ypart = S("projected_part")

        def dve_F(dve, b, g):
            n = b * G + g
            wait(dve, s_sq, n + 1)
            nc.vector.tensor_reduce(ss[:], sq[:], AX.X, ALU.add).then_inc(s_ss, 1)
            wait(dve, s_ss, n + 1)
            nc.vector.tensor_scalar(ms[:], ss[:], 1.0 / P, 1e-5, ALU.mult, ALU.add).then_inc(s_ms, 1)
            wait(dve, s_rs, n + 1)
            wait(dve, s_qt, n)
            nc.vector.tensor_tensor(qk[:], psQK[:], bc(rs[:], 2, P), ALU.mult).then_inc(s_qn, 1)

        def dve_T1(dve, b, g):
            n = b * G + g
            wait(dve, s_s, n + 1)
            nc.vector.tensor_reduce(mx[:], psS[:], AX.X, ALU.max).then_inc(s_mx, 1)
            wait(dve, s_mx, n + 1)
            wait(dve, s_e, n)
            nc.vector.tensor_tensor(df[:], psS[:], bc(mx[:], 2, P), ALU.subtract).then_inc(s_df, 1)

        def dve_T2(dve, b, g):
            n = b * G + g
            wait(dve, s_e, n + 1)
            nc.vector.tensor_reduce(sm[:], pr[:], AX.X, ALU.add).then_inc(s_sm, 1)
            wait(dve, s_sm, n + 1)
            nc.vector.reciprocal(rl[:], sm[:]).then_inc(s_rl, 1)
            wait(dve, s_rl, n + 1)
            wait(dve, s_pt, n)
            nc.vector.tensor_tensor(pn[:], pr[:], bc(rl[:], 2, P), ALU.mult).then_inc(s_pn, 1)

        def dve_X(dve, b):
            wait(dve, s_y, b + 1)
            xb = c.x[:, ds(b, 1), :].rearrange("p a d -> p (a d)")
            nc.vector.tensor_tensor(xb, xb, psY[:, 0:DM], ALU.add).then_inc(s_x, 1)

        def act_A(act, b):
            wait(act, s_xt, b + 1)
            wait(act, s_v, b * G)
            nc.scalar.copy(xT[:], psP[:, 0:KC, :]).then_inc(s_xT, 1)

        def act_F1(act, b, g):
            n = b * G + g
            wait(act, s_qk, n + 1)
            wait(act, s_ss, n)
            nc.scalar.activation(sq[:], psQK[:], ACT.Square).then_inc(s_sq, 1)
            wait(act, s_v, n + 1)
            wait(act, s_o, n - 1)
            nc.scalar.copy(v[:, g % 2], psV[:]).then_inc(s_vc, 1)

        def act_F2(act, b, g):
            n = b * G + g
            wait(act, s_qt, n + 1)
            nc.scalar.copy(qT[:, g % 2], psQT[:, 0:HG, :]).then_inc(s_qT, 1)
            nc.scalar.activation(kT[:, g % 2], psQT[:, HG:, :], ACT.Copy, scale=c.gqk[:]).then_inc(s_kT, 1)

        def act_T1(act, b, g):
            n = b * G + g
            wait(act, s_df, n + 1)
            wait(act, s_pn, n)
            nc.scalar.activation(pr[:], df[:], ACT.Exp, scale=SCALE).then_inc(s_e, 1)

        with nc.Block() as block:
            @block.sync
            def _(sp):
                for n, (dst, src) in enumerate(c.first):
                    sp.dma_start(dst, src).then_inc(c.s_first, 16)
                    if n == 2:
                        sp.dma_start(ctx[:, 0, :], c.dram["ctxT"][0]).then_inc(s_ctx, 16)
                for dst, src in c.late:
                    sp.dma_start(dst, src).then_inc(c.s_late, 16)
                with sp.Fori(0, B - 1) as b:
                    wait(sp, s_v, b * G + G)
                    sp.dma_start(ctx[:, 0:1, :], c.dram["ctxT"][ds(b + 1, 1)].rearrange("a p d -> p a d")).then_inc(s_ctx, 16)

            def run(first_step, body, loop):
                first_step()
                with loop(0, B - 1) as b:
                    body(b, True)
                body(B - 1, False)

            @block.tensor
            def _(pe):
                pe.wait_ge(c.s_first, c.n_first)

                def first():
                    pe_A(pe, 0)
                    pe_F(pe, 0, 0)
                    pe_FT(pe, 0, 0)
                    pe_S(pe, 0, 0)

                def body(b, more):
                    for g in range(G):
                        nb, ng = (b, g + 1) if g < G - 1 else (b + 1, 0)
                        go = more or g < G - 1
                        if go:
                            pe_F(pe, nb, ng)
                        pe_T(pe, b, g, more)
                        if go:
                            pe_FT(pe, nb, ng)
                        pe_O(pe, b, g, go)
                        if go:
                            pe_S(pe, nb, ng)
                        if g == G - 2 and more:
                            pe_A(pe, b + 1)
                        pe_Y(pe, b, g)
                run(first, body, pe.Fori)

            @block.vector
            def _(dve):
                dve.wait_ge(c.s_first, c.n_first)
                nc.vector.tensor_tensor(c.gqk[:], c.g0[:, 0:1], c.g0[:, 1:2], ALU.mult).then_inc(s_g, 1)

                def first():
                    ln.dve_stats(dve, 0)
                    ln.dve_apply(dve, 0, s_xt, 0)
                    dve_F(dve, 0, 0)
                    dve_T1(dve, 0, 0)

                def body(b, more):
                    for g in range(G):
                        nb, ng = (b, g + 1) if g < G - 1 else (b + 1, 0)
                        go = more or g < G - 1
                        dve_T2(dve, b, g)
                        if go:
                            dve_F(dve, nb, ng)
                            if more and g == 0:
                                ln.dve_stats(dve, b + 1)
                            if more and g == 1:
                                ln.dve_apply(dve, b + 1, s_xt, b + 1)
                            dve_T1(dve, nb, ng)
                        if g == G - 1:
                            dve_X(dve, b)
                run(first, body, dve.Fori)

            @block.gpsimd
            def _(pool):
                def rms(b, g):
                    n = b * G + g
                    wait(pool, s_ms, n + 1)
                    wait(pool, s_qn, n)
                    nc.gpsimd.tensor_tensor(rs[:], ms[:], c.neg_half[:, 0:2 * HG], ALU.pow).then_inc(s_rs, 1)

                def first():
                    pool.wait_ge(c.s_first, c.n_first)
                    ln.pool_rstd(pool, 0)
                    rms(0, 0)

                def body(b, more):
                    for g in range(G):
                        nb, ng = (b, g + 1) if g < G - 1 else (b + 1, 0)
                        if more or g < G - 1:
                            rms(nb, ng)
                            if more and g == 0:
                                ln.pool_rstd(pool, b + 1)
                run(first, body, pool.Fori)

            @block.scalar
            def _(act):
                act.wait_ge(s_g, 1)
                nc.scalar.copy(c.ident_b[:], c.ident[:])

                def first():
                    act_A(act, 0)
                    act_F1(act, 0, 0)
                    act_F2(act, 0, 0)
                    act_T1(act, 0, 0)

                def body(b, more):
                    for g in range(G):
                        nb, ng = (b, g + 1) if g < G - 1 else (b + 1, 0)
                        go = more or g < G - 1
                        if go:
                            act_F1(act, nb, ng)
                        wait(act, s_pt, b * G + g + 1)
                        wait(act, s_o, b * G + g)
                        nc.scalar.copy(pT[:], psP[:]).then_inc(s_pT, 1)
                        if go:
                            act_F2(act, nb, ng)
                        wait(act, s_o, b * G + g + 1)
                        if g == 0:
                            wait(act, s_y, b)
                        else:
                            wait(act, s_ypart, b * (G - 1) + g)
                        nc.scalar.copy(oT[:], psV[:]).then_inc(s_oT, 1)
                        if more and g == G - 2:
                            act_A(act, b + 1)
                        if go:
                            act_T1(act, nb, ng)
                run(first, body, act.Fori)


def small_attention(c, name):
    nc, w = c.nc, c.w
    L1 = name == "L1"
    HD = 16 if L1 else 8
    NH = DM // HD
    HG = 4
    G = NH // HG
    RT = HG * HD
    SEG = P - 16
    VW = 2 * (HD + 1) if L1 else HD + 1
    SCALE = HD ** -0.5
    NT = 1 if L1 else 2
    NO = 2 if L1 else 1
    HO = NH // NO
    mask = c.mask16 if L1 else c.mask8
    with ExitStack() as st:
        sb = lambda n, shape: c.sb(f"{name}_{n}", shape, F32, st)
        ps = lambda n, shape: c.ps(f"{name}_{n}", shape, F32, st)
        S = lambda n: c.sem(f"{name}_{n}")
        ln = TileNorm(c, name + "a", st)
        xT = sb("xT", [P, KC, P])
        ctx = sb("ctx", [P, 2, P])
        t1 = sb("t1", [P, 2 * DM])
        t2 = sb("t2", [P, 2 * DM])
        qk = sb("qk", [P, 2 * DM])
        kT = sb("kT", [P, KC, P])
        qT = [sb(f"qT{p}", [P, KC, P]) for p in range(2)]
        kbd = [sb(f"kbd{p}", [P, KC, HG, P]) for p in range(2)]
        vx = [sb(f"vx{p}", [P, NH, VW]) for p in range(2)]
        mx = sb("mx", [P, 2, HG, 2])
        df = sb("df", [P, 2, HG, P])
        pr = sb("pr", [P, 2, HG, P])
        pT = sb("pT", [P, 2, HG, P])
        rl = sb("rl", [P, NH, 2])
        o = sb("o", [P, DM])
        o2 = sb("o2", [P, DM]) if L1 else None
        oT = sb("oT", [P, KC, P])
        n32 = sb("n32", [P, 4, 32]) if L1 else None
        psS = [ps(f"psS{p}", [P, HG, P]) for p in range(2)]
        psP = [ps(f"psP{p}", [P, HG, P]) for p in range(NT)]
        psO = [ps(f"psO{p}", [P, 512]) for p in range(NO)]
        psT = ps("psT", [P, 4, P])
        psA = ps("psA", [P, 512])
        psV = ps("psV", [P, 512])
        s_ctx, s_pre = S("ctx"), S("prepared")
        s_xt, s_xT, s_qk, s_v, s_vc = S("x_transposed"), S("xT_copied"), S("qk_made"), S("v_made"), S("v_copied")
        s_ch, s_n, s_qn = S("qk_chain"), S("qk_rstd"), S("qk_ready")
        s_qt, s_qT, s_kT, s_kb = S("qk_transposed"), S("qT_copied"), S("kT_copied"), S("keys_diagonal")
        s_s, s_mx, s_df, s_e = S("scores"), S("maxima"), S("shifted"), S("exps")
        s_pt, s_pT, s_o = S("probs_transposed"), S("probs_T_copied"), S("out_made")
        s_rl, s_on, s_ot, s_oT, s_y, s_x = (S("inverse_sums"), S("out_normed"), S("out_transposed"),
                                            S("out_T_copied"), S("projected"), S("x_updated"))
        CH = 6 if L1 else 3
        OC = 2 if L1 else 1
        ND = 2 if L1 else 1
        PRE = 4 if L1 else 2

        def pe_A1(pe, b):
            wait(pe, ln.s_xn, b + 1)
            wait(pe, s_qn, b)
            for k in range(KC):
                last = nc.tensor.transpose(psA[:, k * P:(k + 1) * P], ln.xn[:, k * P:(k + 1) * P], c.ident[:])
            last.then_inc(s_xt, 1)

        def act_A1(act, b):
            wait(act, s_xt, b + 1)
            wait(act, s_qk, b)
            nc.scalar.copy(xT[:], psA[:, 0:KC * P].rearrange("p (k n) -> p k n", k=KC)).then_inc(s_xT, 1)

        def pe_A2(pe, b):
            wait(pe, s_xT, b + 1)
            wait(pe, s_ctx, (b + 1) * 16 * ND)
            wq = w[name + "q"]
            mm = nc.tensor.matmul
            for k in range(KC):
                mm(psA[:, 0:DM], xT[:, k, :], wq[:, k, :], start=k == 0, stop=k == KC - 1 and not L1)
            if L1:
                mm(psA[:, 0:DM], c.ones_row[:], w["L1bq"][:], start=False, stop=True)
                mm(psA[:, DM:], ctx[:, 0, :], w["L1k"][:], start=True, stop=False)
                mm(psA[:, DM:], ctx[:, 1, :], w["L1d"][:, 0:DM], start=False, stop=False)
                mm(psA[:, DM:], c.sel_seg[:], w["L1bkv"][:, 0:DM], start=False, stop=True).then_inc(s_qk, 1)
            else:
                mm(psA[:, DM:], ctx[:, 0, :], w[name + "kv"][:, 0:DM], start=True, stop=True).then_inc(s_qk, 1)
            wait(pe, s_vc, b * (2 if L1 else 1))
            wait(pe, s_x, b - (2 if L1 else 1))
            if L1:
                mm(psV[:, 0:DM], ctx[:, 0, :], w["L1v"][:], start=True, stop=False)
                mm(psV[:, 0:DM], ctx[:, 1, :], w["L1d"][:, DM:], start=False, stop=False)
                mm(psV[:, 0:DM], c.sel_seg[:], w["L1bkv"][:, DM:], start=False, stop=True).then_inc(s_v, 1)
            else:
                mm(psV[:, 0:DM], ctx[:, 0, :], w[name + "kv"][:, DM:], start=True, stop=True).then_inc(s_v, 1)

        def act_A2(act, b, p):
            wait(act, s_v, b + 1)
            wait(act, s_o, (b - 1) * G)
            vs = psV[:, 0:DM].rearrange("p (h d) -> p h d", d=HD)
            if L1:
                nc.scalar.activation(vx[p][:, :, 0:HD], vs, ACT.Copy, scale=c.mask_seg[:, 0:1]).then_inc(s_vc, 1)
                nc.scalar.activation(vx[p][:, :, HD + 1:2 * HD + 1], vs, ACT.Copy, scale=c.mask_seg[:, 1:2]).then_inc(s_vc, 1)
            else:
                nc.scalar.copy(vx[p][:, :, 0:HD], vs).then_inc(s_vc, 1)

        def dve_A2(dve, b):
            v = nc.vector
            wait(dve, s_qk, b + 1)
            wait(dve, s_qt, b)

            def link(ins, n):
                ins.then_inc(s_ch, 1)
                dve.wait_ge(s_ch, b * CH + n)
            if L1:
                h3 = lambda a: a.rearrange("p (h d) -> p h d", d=HD)
                link(v.tensor_reduce(n32[:, 0, :], h3(psA[:]), AX.X, ALU.add), 1)
                link(v.tensor_scalar(n32[:, 1, :], n32[:, 0, :], 1.0 / HD, None, ALU.mult), 2)
                link(v.tensor_tensor(h3(t1[:]), h3(psA[:]), bc(n32[:, 1, :], 2, HD), ALU.subtract), 3)
                link(v.tensor_tensor(t2[:], t1[:], t1[:], ALU.mult), 4)
                link(v.tensor_reduce(n32[:, 2, :], h3(t2[:]), AX.X, ALU.add), 5)
                v.tensor_scalar(n32[:, 2, :], n32[:, 2, :], 1.0 / HD, 1e-6, ALU.mult, ALU.add).then_inc(s_ch, 1)
            else:
                f = lambda a: a.rearrange("p (h r) -> p h r", r=8)
                cb = bc(c.cos2[:, ds(b, 1), :].rearrange("p a r -> p (a r)"), 1, 64)
                v.tensor_tensor(f(t1[:]), f(psA[:]), cb, ALU.mult).then_inc(s_ch, 1)
                for i in range(2):
                    sbc = bc(c.sin2[:, ds(b, 1), i:8:2].rearrange("p a r -> p (a r)"), 1, 64)
                    last = v.tensor_tensor(f(t2[:])[:, :, i:8:2], f(psA[:])[:, :, 1 - i:8:2], sbc, ALU.mult)
                    last.then_inc(s_ch, 1)
                dve.wait_ge(s_ch, b * CH + 3)
                v.tensor_tensor(qk[:], t1[:], t2[:], ALU.add).then_inc(s_qn, 1)

        def pool_A2(pool, b):
            if L1:
                wait(pool, s_ch, b * CH + 6)
                nc.gpsimd.tensor_tensor(n32[:, 3, :], n32[:, 2, :], c.neg_half[:], ALU.pow).then_inc(s_n, 1)

        def dve_A2b(dve, b):
            if L1:
                v = nc.vector
                s4 = lambda a: a.rearrange("p (s h d) -> p s h d", s=2, d=HD)
                wait(dve, s_n, b + 1)
                h3 = lambda a: a.rearrange("p (h d) -> p h d", d=HD)
                v.tensor_tensor(h3(t2[:]), h3(t1[:]), bc(n32[:, 3, :], 2, HD), ALU.mult).then_inc(s_nm, 1)
                dve.wait_ge(s_nm, b * 2 + 1)
                v.tensor_tensor(s4(t1[:]), s4(t2[:]), bc(w["L1nw"][:], 2, 16), ALU.mult).then_inc(s_nm, 1)
                dve.wait_ge(s_nm, b * 2 + 2)
                wait(dve, s_qt, b)
                v.tensor_tensor(s4(qk[:]), s4(t1[:]), bc(w["L1nb"][:], 2, 16), ALU.add).then_inc(s_qn, 1)
        s_nm = S("qk_norm_links")

        def pe_A3(pe, b):
            wait(pe, s_qn, b + 1)
            wait(pe, s_oT, b - 1)
            wait(pe, s_kT, b)
            for k in range(4):
                last = nc.tensor.transpose(psT[:, k, :], qk[:, k * P:(k + 1) * P], c.ident[:])
            last.then_inc(s_qt, 1)

        def act_A3(act, b, p):
            wait(act, s_qt, b + 1)
            wait(act, s_s, (b - 1) * G)
            nc.scalar.copy(qT[p][:], psT[:, 0:KC, :]).then_inc(s_qT, 1)
            wait(act, s_kb, b)
            nc.scalar.copy(kT[:], psT[:, KC:, :]).then_inc(s_kT, 1)

        def pool_A3(pool, b, p):
            wait(pool, s_kT, b + 1)
            wait(pool, s_s, (b - 1) * G)
            for k in range(KC):
                last = nc.gpsimd.tensor_tensor(kbd[p][:, k], bc(kT[:, k, :], 1, HG), bc(mask[:], 2, P), ALU.mult)
            last.then_inc(s_kb, 1)

        def pe_S(pe, b, g, p):
            n = b * G + g
            if g == 0:
                wait(pe, s_kb, b + 1)
            wait(pe, s_df, (n - 1) * (2 if L1 else 1))
            k, r = (g * RT) // P, (g * RT) % P
            nc.tensor.matmul(psS[g % 2][:], qT[p][r:r + RT, k, :], kbd[p][r:r + RT, k], start=True, stop=True).then_inc(s_s, 1)

        def dve_S(dve, b, g):
            n = b * G + g
            v = nc.vector
            wait(dve, s_s, n + 1)
            q = g % 2
            wait(dve, s_e, n - 1)
            if L1:
                v.tensor_reduce(mx[:, q, :, 0], psS[q][:, :, 0:SEG], AX.X, ALU.max).then_inc(s_mx, 1)
                v.tensor_reduce(mx[:, q, :, 1], psS[q][:, :, SEG:], AX.X, ALU.max).then_inc(s_mx, 1)
                dve.wait_ge(s_mx, n * 2 + 2)
                v.tensor_tensor(df[:, q, :, 0:SEG], psS[q][:, :, 0:SEG], bc(mx[:, q, :, 0], 2, SEG), ALU.subtract).then_inc(s_df, 1)
                v.tensor_tensor(df[:, q, :, SEG:], psS[q][:, :, SEG:], bc(mx[:, q, :, 1], 2, P - SEG), ALU.subtract).then_inc(s_df, 1)
            else:
                v.tensor_reduce(mx[:, q, :, 0], psS[q][:], AX.X, ALU.max).then_inc(s_mx, 1)
                dve.wait_ge(s_mx, n + 1)
                v.tensor_tensor(df[:, q], psS[q][:], bc(mx[:, q, :, 0], 2, P), ALU.subtract).then_inc(s_df, 1)

        def act_S(act, b, g):
            n = b * G + g
            wait(act, s_df, (n + 1) * (2 if L1 else 1))
            wait(act, s_pt, n - 1)
            nc.scalar.activation(pr[:, g % 2], df[:, g % 2], ACT.Exp, scale=SCALE).then_inc(s_e, 1)

        def pe_T(pe, b, g):
            n = b * G + g
            wait(pe, s_e, n + 1)
            wait(pe, s_pT, n + 1 - NT)
            for h in range(HG):
                last = nc.tensor.transpose(psP[g % NT][:, h, :], pr[:, g % 2, h, :], c.ident[:])
            last.then_inc(s_pt, 1)

        def act_T(act, b, g):
            n = b * G + g
            wait(act, s_pt, n + 1)
            wait(act, s_o, n - 1)
            nc.scalar.copy(pT[:, g % 2], psP[g % NT][:]).then_inc(s_pT, 1)

        def pe_O(pe, b, g, p):
            n = b * G + g
            wait(pe, s_pT, n + 1)
            if g == 0:
                wait(pe, s_vc, (b + 1) * (2 if L1 else 1))
                wait(pe, s_on, b)
            for j in range(HG):
                h = g * HG + j
                last = nc.tensor.matmul(psO[h // HO][:, (h % HO) * VW:(h % HO + 1) * VW], pT[:, g % 2, j, :],
                                        vx[p][:, h, :], start=True, stop=True)
            last.then_inc(s_o, 1)

        def dve_E1(dve, b):
            v = nc.vector
            wait(dve, s_o, (b + 1) * G)
            wait(dve, s_ot, b)
            if L1:
                for i in range(NO):
                    po = psO[i][:, 0:HO * VW].rearrange("p (h s d) -> p h s d", h=HO, s=2)
                    v.reciprocal(rl[:, i * HO:(i + 1) * HO, :], po[:, :, :, HD]).then_inc(s_rl, 1)
                dve.wait_ge(s_rl, b * 2 + 2)
                for i in range(NO):
                    po = psO[i][:, 0:HO * VW].rearrange("p (h s d) -> p h s d", h=HO, s=2)
                    hs = slice(i * HO, (i + 1) * HO)
                    for s, dst in ((0, o2), (1, t2x)):
                        d3 = dst[:].rearrange("p (h d) -> p h d", d=HD)[:, hs, :]
                        v.tensor_tensor(d3, po[:, :, s, 0:HD], bc(rl[:, hs, s], 2, HD), ALU.mult).then_inc(s_os, 1)
                dve.wait_ge(s_os, b * 4 + 4)
                v.tensor_tensor(o[:], o2[:], t2x[:], ALU.add).then_inc(s_on, 1)
            else:
                po = psO[0][:, 0:NH * VW].rearrange("p (h d) -> p h d", h=NH)
                v.reciprocal(rl[:, :, 0], po[:, :, HD]).then_inc(s_rl, 1)
                dve.wait_ge(s_rl, b + 1)
                v.tensor_tensor(o[:].rearrange("p (h d) -> p h d", d=HD), po[:, :, 0:HD], bc(rl[:, :, 0], 2, HD),
                                ALU.mult).then_inc(s_on, 1)
        t2x = sb("o3", [P, DM]) if L1 else None
        s_os = S("segments_divided")

        def pe_E1(pe, b):
            wait(pe, s_on, b + 1)
            wait(pe, s_kT, b + 1)
            for k in range(KC):
                last = nc.tensor.transpose(psT[:, k, :], o[:, k * P:(k + 1) * P], c.ident[:])
            last.then_inc(s_ot, 1)

        def act_E1(act, b):
            wait(act, s_ot, b + 1)
            wait(act, s_y, b)
            nc.scalar.copy(oT[:], psT[:, 0:KC, :]).then_inc(s_oT, 1)

        def pe_E2(pe, b, last=False):
            wait(pe, s_oT, b + 1)
            wait(pe, s_x, b)
            if not last:
                wait(pe, s_vc, (b + 3) * 2 if L1 else b + 2)
            ypart = psV[:, DM:]
            for k in range(KC):
                nc.tensor.matmul(ypart, oT[:, k, :], w[name + "o"][:, k, :], start=k == 0, stop=False)
            nc.tensor.matmul(ypart, c.ones_row[:], w[name + "bo"][:], start=False, stop=True).then_inc(s_y, 1)

        def dve_E2(dve, b):
            wait(dve, s_y, b + 1)
            xb = c.x[:, ds(b, 1), :].rearrange("p a d -> p (a d)")
            nc.vector.tensor_tensor(xb, xb, psV[:, DM:], ALU.add).then_inc(s_x, 1)

        def schedule(body, loop):
            body(0, 0, True, False)
            with loop(0, B // 2 - 1) as j:
                body(j * 2 + 1, 1, True, True)
                body(j * 2 + 2, 0, True, True)
            body(B - 1, 1, False, True)

        def steps(b, p, more):
            for g in range(G):
                yield g, ((b, g + 1, p) if g < G - 1 else (b + 1, 0, 1 - p) if more else None)

        E1, E2 = 1, 2
        A1, A2, A3 = (0, 1, 2) if L1 else (1, 3, 5)

        with nc.Block() as block:
            @block.sync
            def _(sp):
                def load(b):
                    src = c.dram["ctxT"][ds(b, 1)].rearrange("a p d -> p (a d)")
                    if L1:
                        sp.dma_start(ctx[:, 0, 0:SEG], src[:, 0:SEG]).then_inc(s_ctx, 16)
                        sp.dma_start(ctx[:, 1, SEG:], src[:, SEG:]).then_inc(s_ctx, 16)
                    else:
                        sp.dma_start(ctx[:, 0, :], src).then_inc(s_ctx, 16)
                if L1:
                    sp.wait_ge(s_pre, PRE)
                load(0)
                with sp.Fori(0, B - 1) as b:
                    wait(sp, s_v, b + 1)
                    load(b + 1)

            @block.tensor
            def _(pe):
                pe.wait_ge(c.s_late, c.n_late)
                pe.wait_ge(s_pre, PRE)
                pe_A1(pe, 0)
                pe_A2(pe, 0)
                pe_A3(pe, 0)
                pe_S(pe, 0, 0, 0)

                def body(b, p, more, end):
                    for g, nxt in steps(b, p, more):
                        if nxt:
                            pe_S(pe, *nxt)
                        pe_T(pe, b, g)
                        if g:
                            pe_O(pe, b, g - 1, p)
                        elif end:
                            pe_O(pe, b - 1, G - 1, 1 - p)
                        if more and g == A1:
                            pe_A1(pe, b + 1)
                        if end and g == E1:
                            pe_E1(pe, b - 1)
                        if end and g == E2:
                            pe_E2(pe, b - 1, not more)
                        if more and g == A2:
                            pe_A2(pe, b + 1)
                        if more and g == A3:
                            pe_A3(pe, b + 1)
                schedule(body, pe.Fori)
                pe_O(pe, B - 1, G - 1, 1)
                pe_E1(pe, B - 1)
                pe_E2(pe, B - 1, True)

            @block.vector
            def _(dve):
                v = nc.vector
                if L1:
                    v.memset(ctx[:], 0.0).then_inc(s_pre, 1)
                for p in range(2):
                    v.memset(vx[p][:], 1.0).then_inc(s_pre, 1)
                dve.wait_ge(c.s_late, c.n_late)
                if L1:
                    dve.wait_ge(s_pre, 3)
                    for p in range(2):
                        for i in range(2):
                            last = v.tensor_copy(vx[p][:, :, i * (HD + 1) + HD], c.mask_seg[:, i:i + 1].to_broadcast([P, NH]))
                    last.then_inc(s_pre, 1)
                ln.dve_stats(dve, 0)
                ln.dve_apply(dve, 0, s_xt, 0)
                dve_A2(dve, 0)
                dve_A2b(dve, 0)
                dve_S(dve, 0, 0)

                def body(b, p, more, end):
                    for g, nxt in steps(b, p, more):
                        if more and g == 0:
                            ln.dve_stats(dve, b + 1)
                        if nxt and g < G - 1:
                            dve_S(dve, nxt[0], nxt[1])
                        if more and g == 0:
                            ln.dve_apply(dve, b + 1, s_xt, b + 1)
                        if end and g == 0:
                            dve_E1(dve, b - 1)
                        if more and g == A2:
                            dve_A2(dve, b + 1)
                            dve_A2b(dve, b + 1)
                        if end and g == E2:
                            dve_E2(dve, b - 1)
                        if nxt and g == G - 1:
                            dve_S(dve, nxt[0], nxt[1])
                schedule(body, dve.Fori)
                dve_E1(dve, B - 1)
                dve_E2(dve, B - 1)

            @block.gpsimd
            def _(pool):
                pool.wait_ge(c.s_late, c.n_late)
                ln.pool_rstd(pool, 0)
                pool_A2(pool, 0)
                pool_A3(pool, 0, 0)

                def body(b, p, more, end):
                    if more:
                        ln.pool_rstd(pool, b + 1)
                        pool_A2(pool, b + 1)
                        pool_A3(pool, b + 1, 1 - p)
                schedule(body, pool.Fori)

            @block.scalar
            def _(act):
                act_A1(act, 0)
                act.wait_ge(s_pre, PRE)
                act_A2(act, 0, 0)
                act_A3(act, 0, 0)
                act_S(act, 0, 0)

                def body(b, p, more, end):
                    for g, nxt in steps(b, p, more):
                        act_T(act, b, g)
                        if more and g == A1:
                            act_A1(act, b + 1)
                        if end and g == E1:
                            act_E1(act, b - 1)
                        if more and g == A2:
                            act_A2(act, b + 1, 1 - p)
                        if more and g == A3:
                            act_A3(act, b + 1, 1 - p)
                        if nxt:
                            act_S(act, nxt[0], nxt[1])
                schedule(body, act.Fori)
                act_E1(act, B - 1)


def rotation_tables(c):
    nc = c.nc
    FREQ = (1.0, 0.01)
    c.cos2 = c.sb("cos2", [P, B, 8])
    c.sin2 = c.sb("sin2", [P, B, 8])
    with ExitStack() as st:
        ang = c.sb("rt_ang", [P, B * 4], F32, st)
        kk = c.sb("rt_k", [P, B * 4], F32, st)
        kr = c.sb("rt_kr", [P, B * 4], F32, st)
        red = [c.sb(f"rt_red{i}", [P, B * 4], F32, st) for i in range(4)]
        ab = c.sb("rt_abs", [P, B * 4], F32, st)
        sn = c.sb("rt_sin", [P, B * 4], F32, st)
        cs = c.sb("rt_cos", [P, B * 4], F32, st)
        half_pi = c.sb("rt_half_pi", [P, 1], F32, st)
        s_ch, s_red, s_act = c.sem("rt_chain"), c.sem("rt_reduced"), c.sem("rt_functions")
        with nc.Block() as block:
            @block.vector
            def _(dve):
                v = nc.vector
                n = 0

                def link(ins):
                    nonlocal n
                    n += 1
                    ins.then_inc(s_ch, 1)
                    dve.wait_ge(s_ch, n)
                v.memset(half_pi[:], 1.5707963267948966).then_inc(s_red, 1)
                dve.wait_ge(c.s_late, c.n_late)
                pos = c.pos[:].rearrange("p b a -> p (b a)")
                a3 = ang[:].rearrange("p (q f) -> p q f", f=2)
                for i, f in enumerate(FREQ):
                    link(v.tensor_scalar(a3[:, :, i], pos, f, None, ALU.mult))
                link(v.tensor_scalar(kk[:], ang[:], 0.15915494309189535, MAGIC, ALU.mult, ALU.add))
                link(v.tensor_scalar(kr[:], kk[:], -MAGIC, None, ALU.add))
                src = ang
                for i, part in enumerate(TWO_PI):
                    link(v.scalar_tensor_tensor(red[i][:], kr[:], -part, src[:], ALU.mult, ALU.add))
                    src = red[i]
                v.tensor_scalar(red[3][:], src[:], PI_LOW, -PI_LOW, ALU.min, ALU.max).then_inc(s_red, 1)
                dve.wait_ge(s_act, 3)
                for i, sign in ((0, -1.0), (1, 1.0)):
                    s8 = c.sin2[:].rearrange("p b (r i) -> p (b r) i", i=2)
                    c8 = c.cos2[:].rearrange("p b (r i) -> p (b r) i", i=2)
                    v.tensor_scalar(s8[:, :, i], sn[:], sign, None, ALU.mult)
                    v.tensor_copy(c8[:, :, i], cs[:])

            @block.scalar
            def _(act):
                act.wait_ge(s_red, 2)
                nc.scalar.activation(sn[:], red[3][:], ACT.Sin).then_inc(s_act, 1)
                nc.scalar.activation(ab[:], red[3][:], ACT.Abs).then_inc(s_act, 1)
                act.wait_ge(s_act, 2)
                nc.scalar.activation(cs[:], ab[:], ACT.Sin, bias=half_pi[:], scale=-1.0).then_inc(s_act, 1)


def moe(c, name, E, TOP, EX, chunks, downs, shared=False):
    nc, d = c.nc, c.dram
    pack = d[name + "_pack"]
    U, WP = pack.shape[0], pack.shape[2]
    FT = chunks[-1][0] + chunks[-1][1]
    NCH = len(chunks)
    ES = E + (1 if shared else 0)
    BP = 2 * EX
    with ExitStack() as st:
        sb = lambda n, shape: c.sb(f"{name}moe_{n}", shape, F32, st)
        ps = lambda n, shape: c.ps(f"{name}moe_{n}", shape, F32, st)
        S = lambda n: c.sem(f"{name}moe_{n}")
        lns = [TileNorm(c, f"{name}moe{p}", st) for p in range(2)]
        wr = sb("router", [P, KC, E])
        bias = sb("bias", [P, E])
        xb = [sb(f"xb{p}", [P, KC, P]) for p in range(2)]
        lg = sb("lg", [P, B, E])
        val = sb("val", [P, B, E])
        key = sb("key", [P, B, E])
        tmp = sb("tmp", [P, B, E])
        col = sb("col", [P, B])
        rank = sb("rank", [P, B, E])
        cw = sb("cw", [P, ES, B])
        cmp_ = sb("cmp", [P, B, E, E])
        wt = [sb(f"w{p}", [P, WP]) for p in range(2)]
        cwe = [sb(f"cwe{p}", [P, EX, B]) for p in range(2)]
        sg = [sb(f"sg{p}", [P, 512]) for p in range(2)]
        h = [[sb(f"h{p}_{i}", [P, 512]) for i in range(NCH)] for p in range(2)]
        psG = [ps(f"psG{p}", [P, 512]) for p in range(2)]
        psU = [ps(f"psU{p}", [P, 512]) for p in range(2)]
        psY = [ps(f"psY{p}", [P, 2, DM]) for p in range(4)]
        s_r, s_w = S("router_loaded"), [S(f"weights_loaded{p}") for p in range(2)]
        s_xt, s_xb, s_lg, s_lc, s_xT = (S("x_transposed"), S("xb_copied"), S("logits_made"),
                                        S("logits_copied"), S("xT_copied"))
        s_ch, s_d, s_e, s_cw, s_ce = (S("gate_chain"), S("gate_shifted"), S("gate_exps"),
                                      S("gates_done"), S("unit_gates"))
        s_g, s_u, s_sg, s_h, s_y, s_x = (S("gate_made"), S("up_made"), S("silu_done"), S("hidden_done"),
                                         S("down_made"), S("x_added"))

        def gate_w(p, k, ch):
            o, m = chunks[ch]
            return wt[p][:, k * FT + o:k * FT + o + m]

        def up_w(p, k, ch):
            o, m = chunks[ch]
            return wt[p][:, (KC + k) * FT + o:(KC + k) * FT + o + m]

        def down_w(p, ch):
            return wt[p][:, 2 * KC * FT + ch * DM:2 * KC * FT + (ch + 1) * DM]

        def tiles(body, loop):
            for p in range(2):
                body(p, p, 0)
            with loop(1, B // 2) as j:
                for p in range(2):
                    body(j * 2 + p, p, j)

        def units(body, loop):
            body(0, 0, True)
            pairs = (U - 2) // 2
            with loop(0, pairs) as j:
                body(j * 2 + 1, 1, True)
                body(j * 2 + 2, 0, True)
            for u in range(2 * pairs + 1, U):
                body(u, u % 2, u < U - 1)

        def steps(u, p, more):
            for q in range(NG):
                yield q, ((u, q + 1, p) if q < NG - 1 else (u + 1, 0, 1 - p) if more else None)

        with nc.Block() as block:
            @block.sync
            def _(sp):
                sp.dma_start(wr[:], d[name + "_router"].rearrange("(k p) e -> p k e", p=P)).then_inc(s_r, 16)
                if shared:
                    sp.dma_start(bias[:], d[name + "_bias"].rearrange("(o e) -> o e", o=1).to_broadcast([P, E])).then_inc(s_r, 16)
                for p in range(2):
                    sp.dma_start(wt[p][:], pack[p]).then_inc(s_w[p], 16)

                def load(u, p):
                    wait(sp, s_y, (u - 1) * (NG * BP))
                    sp.dma_start(wt[p][:], pack[ds(u, 1)].rearrange("a p n -> p (a n)")).then_inc(s_w[p], 16)
                with sp.Fori(1, U // 2) as j:
                    load(j * 2, 0)
                    load(j * 2 + 1, 1)
                if U % 2:
                    load(U - 1, 0)

            @block.tensor
            def _(pe):
                pe.wait_ge(s_r, 16 + 16 * shared)

                def tile(i, p, n):
                    wait(pe, lns[p].s_xn, n + 1)
                    wait(pe, s_xb, i - 1)
                    for k in range(KC):
                        last = nc.tensor.transpose(psG[p][:, k * P:(k + 1) * P], lns[p].xn[:, k * P:(k + 1) * P], c.ident[:])
                    last.then_inc(s_xt, 1)
                    wait(pe, s_xb, i + 1)
                    wait(pe, s_lc, i - 1)
                    for k in range(KC):
                        last = nc.tensor.matmul(psU[p][:, 0:E], xb[p][:, k, :], wr[:, k, :], start=k == 0, stop=k == KC - 1)
                    last.then_inc(s_lg, 1)
                tiles(tile, pe.Fori)
                pe.wait_ge(s_xT, B)
                pe.wait_ge(s_lc, B)

                def gate_up(u, q, p):
                    if q == 0:
                        wait(pe, s_w[p], (u - p) * 8 + 16)
                    for ch in range(NCH):
                        m = (u * NG + q) * NCH + ch
                        i, rows = (q * NCH + ch) % 2, chunks[ch][1]
                        wait(pe, s_h, m - 1)
                        for ww, dst, s in ((gate_w, psG, s_g), (up_w, psU, s_u)):
                            for k in range(KC):
                                last = nc.tensor.matmul(dst[i][0:rows, :], ww(p, k, ch), c.xT[:, k, q * 512:(q + 1) * 512],
                                                        start=k == 0, stop=k == KC - 1)
                            last.then_inc(s, 1)

                def down(u, q, p):
                    n = u * NG + q
                    wait(pe, s_h, (n + 1) * NCH)
                    for j in range(BP):
                        r = n * BP + j
                        wait(pe, s_x, (r - 3) * 2)
                        for i in range(2):
                            t, e = 2 * (j // EX) + i, j % EX
                            for k, (ch, r0, rn) in enumerate(downs[e]):
                                last = nc.tensor.matmul(psY[(q * BP + j) % 4][:, i, :],
                                                        h[q % 2][ch][r0:r0 + rn, t * P:(t + 1) * P],
                                                        down_w(p, ch)[r0:r0 + rn, :],
                                                        start=k == 0, stop=k == len(downs[e]) - 1)
                        last.then_inc(s_y, 1)
                gate_up(0, 0, 0)

                def unit(u, p, more):
                    for q, nxt in steps(u, p, more):
                        if nxt:
                            gate_up(*nxt)
                        down(u, q, p)
                units(unit, pe.Fori)

            @block.vector
            def _(dve):
                v = nc.vector
                v.memset(cmp_[:], 0.0).then_inc(s_ch, 1)
                if shared:
                    v.memset(cw[:, E:, :], 1.0).then_inc(s_cw, 1)

                def stats(p, n):
                    lns[p].dve_stats(dve, n * 2 + p, n)

                def apply(p, n):
                    lns[p].dve_apply(dve, n * 2 + p, s_xt, (n - 1) * 2 + p + 1, n)
                stats(0, 0)
                stats(1, 0)
                apply(0, 0)
                with dve.Fori(1, B // 2) as j:
                    stats(0, j)
                    lns[1].dve_apply(dve, j * 2 - 1, s_xt, (j - 1) * 2, j - 1)
                    stats(1, j)
                    apply(0, j)
                apply(1, B // 2 - 1)

                dve.wait_ge(s_lc, B)
                n = 1

                def link(ins):
                    nonlocal n
                    n += 1
                    ins.then_inc(s_ch, 1)
                    dve.wait_ge(s_ch, n)
                if shared:
                    dve.wait_ge(s_e, 1)
                    link(v.tensor_scalar(tmp[:], key[:], 1.0, None, ALU.add))
                    link(v.reciprocal(val[:], tmp[:]))
                    dve.wait_ge(s_r, 32)
                    link(v.tensor_tensor(key[:], val[:], bc(bias[:], 1, B), ALU.add))
                    ranked = key
                else:
                    link(v.tensor_reduce(col[:], lg[:], AX.X, ALU.max))
                    v.tensor_tensor(tmp[:], lg[:], bc(col[:], 2, E), ALU.subtract).then_inc(s_d, 1)
                    dve.wait_ge(s_e, 1)
                    ranked = lg
                    if name == "L1":
                        link(v.tensor_reduce(col[:], key[:], AX.X, ALU.add))
                        link(v.reciprocal(col[:], col[:]))
                        link(v.tensor_tensor(val[:], key[:], bc(col[:], 2, E), ALU.mult))
                        ranked = val
                dve.wait_ge(s_ch, 1)
                for j in range(E):
                    kj = ranked[:, :, j]
                    if j > 0:
                        last = v.tensor_tensor(cmp_[:, :, 0:j, j], bc(kj, 2, j), ranked[:, :, 0:j], ALU.is_gt)
                    if j < E - 1:
                        last = v.tensor_tensor(cmp_[:, :, j + 1:, j], bc(kj, 2, E - 1 - j), ranked[:, :, j + 1:], ALU.is_ge)
                link(last)
                link(v.tensor_reduce(rank[:], cmp_[:], AX.X, ALU.add))
                link(v.tensor_scalar(rank[:], rank[:], float(TOP), None, ALU.is_lt))
                vals = key if name == "L0" else val
                cwt = cw[:, 0:E, :].rearrange("p e b -> p b e")
                if name == "L1":
                    v.tensor_tensor(cwt, vals[:], rank[:], ALU.mult).then_inc(s_cw, 1)
                else:
                    link(v.tensor_tensor(tmp[:], vals[:], rank[:], ALU.mult))
                    link(v.tensor_reduce(col[:], tmp[:], AX.X, ALU.add))
                    link(v.reciprocal(col[:], col[:]))
                    v.tensor_tensor(cwt, tmp[:], bc(col[:], 2, E), ALU.mult).then_inc(s_cw, 1)

                def hidden(u, q, p):
                    nn = u * NG + q
                    for ch in range(NCH):
                        m = nn * NCH + ch
                        i, rows = (q * NCH + ch) % 2, chunks[ch][1]
                        wait(dve, s_u, m + 1)
                        wait(dve, s_sg, m + 1)
                        wait(dve, s_y, (nn - 1) * BP)
                        v.tensor_tensor(h[q % 2][ch][0:rows, :], sg[i][0:rows, :], psU[i][0:rows, :], ALU.mult).then_inc(s_h, 1)

                def add(u, q, p):
                    nn = u * NG + q
                    if q == 0:
                        wait(dve, s_ce, u + 1)
                    for j in range(BP):
                        r = nn * BP + j
                        wait(dve, s_y, r + 1)
                        for i in range(2):
                            t, e = 4 * q + 2 * (j // EX) + i, j % EX
                            if i == 0 and (e or j == 0):
                                wait(dve, s_x, r * 2)
                            v.scalar_tensor_tensor(c.x[:, t, :], psY[(q * BP + j) % 4][:, i, :],
                                                   cwe[p][:, e, t:t + 1], c.x[:, t, :], ALU.mult, ALU.add).then_inc(s_x, 1)
                hidden(0, 0, 0)

                def unit(u, p, more):
                    for q, nxt in steps(u, p, more):
                        if nxt:
                            hidden(*nxt)
                        add(u, q, p)
                units(unit, dve.Fori)

            @block.gpsimd
            def _(pool):
                def tile(i, p, n):
                    lns[p].pool_rstd(pool, n)

                def copy(i, p):
                    wait(pool, s_xb, i + 1)
                    nc.gpsimd.tensor_copy(c.xT[:, :, ds(i * P, P)], xb[p][:]).then_inc(s_xT, 1)
                tile(0, 0, 0)
                tile(1, 1, 0)
                with pool.Fori(1, B // 2) as j:
                    copy(j * 2 - 2, 0)
                    lns[0].pool_rstd(pool, j)
                    copy(j * 2 - 1, 1)
                    lns[1].pool_rstd(pool, j)
                copy(B - 2, 0)
                copy(B - 1, 1)
                pool.wait_ge(s_cw, 1 + shared)

                def gates(u, p):
                    wait(pool, s_x, (u - 1) * (NG * BP * 2))
                    nc.gpsimd.tensor_copy(cwe[p][:], cw[:, ds(u * EX, EX), :]).then_inc(s_ce, 1)
                gates(0, 0)
                with pool.Fori(0, (U - 1) // 2) as j:
                    gates(j * 2 + 1, 1)
                    gates(j * 2 + 2, 0)
                if U % 2 == 0:
                    gates(U - 1, 1)

            @block.scalar
            def _(act):
                def tile(i, p, n):
                    wait(act, s_xt, i + 1)
                    wait(act, s_lg, i - 1)
                    wait(act, s_xT, i - 1)
                    nc.scalar.copy(xb[p][:], psG[p][:, 0:DM].rearrange("p (k n) -> p k n", k=KC)).then_inc(s_xb, 1)
                    wait(act, s_lg, i + 1)
                    nc.scalar.copy(lg[:, ds(i, 1), :], psU[p][:, 0:E].rearrange("p (a e) -> p a e", a=1)).then_inc(s_lc, 1)
                tiles(tile, act.Fori)
                if shared:
                    act.wait_ge(s_lc, B)
                    nc.scalar.activation(key[:], lg[:], ACT.Exp, scale=-1.0).then_inc(s_e, 1)
                else:
                    act.wait_ge(s_d, 1)
                    nc.scalar.activation(key[:], tmp[:], ACT.Exp).then_inc(s_e, 1)

                def silu(u, q, p):
                    for ch in range(NCH):
                        m = (u * NG + q) * NCH + ch
                        i, rows = (q * NCH + ch) % 2, chunks[ch][1]
                        wait(act, s_g, m + 1)
                        wait(act, s_h, m - 1)
                        nc.scalar.activation(sg[i][0:rows, :], psG[i][0:rows, :], ACT.Silu).then_inc(s_sg, 1)
                silu(0, 0, 0)

                def unit(u, p, more):
                    for q, nxt in steps(u, p, more):
                        if nxt:
                            silu(*nxt)
                units(unit, act.Fori)



def quantized_linear(c):
    nc, w = c.nc, c.w
    with ExitStack() as st:
        sb = lambda n, shape, dt=F32: c.sb(f"q8_{n}", shape, dt, st)
        S = lambda n: c.sem("q8_" + n)
        lns = [TileNorm(c, f"q8f{p}", st) for p in range(2)]
        wb = sb("wb", [P, KC, DM], BF16)
        am = sb("am", [P, 2])
        sc = [sb(f"sc{p}", [P, 1]) for p in range(2)]
        isc = sb("isc", [P, 2])
        r1 = sb("r1", [P, DM])
        r2 = sb("r2", [P, DM])
        xq = [sb(f"xq{p}", [P, DM], BF16) for p in range(2)]
        xqT = [sb(f"xqT{p}", [P, KC, P], BF16) for p in range(2)]
        y1 = sb("y1", [P, DM])
        y2 = sb("y2", [P, DM], F16)
        psT = [c.ps(f"q8_psT{p}", [P, KC, P], BF16, st) for p in range(2)]
        psY = [c.ps(f"q8_psY{p}", [P, 512], F32, st) for p in range(2)]
        s_w, s_ch, s_xq, s_xt, s_xT, s_acc, s_y, s_x = (S("weights"), S("chain"), S("quantized"), S("transposed"),
                                                        S("transposed_copied"), S("accumulated"), S("scaled"), S("x_added"))
        CH = 5

        with nc.Block() as block:
            @block.vector
            def _(dve):
                v = nc.vector
                dve.wait_ge(c.s_late, c.n_late)
                v.tensor_copy(wb[:].rearrange("p k n -> p (k n)"),
                              w["fq8"][:].rearrange("p k n -> p (k n)").bitcast(I8)).then_inc(s_w, 1)

                def front(i, p, n):
                    lns[p].dve_stats(dve, i, n)
                    lns[p].dve_apply(dve, i, s_ch, i * CH, n)

                    def link(ins, k):
                        ins.then_inc(s_ch, 1)
                        dve.wait_ge(s_ch, i * CH + k)
                    dve.wait_ge(lns[p].s_xn, n + 1)
                    link(v.tensor_reduce(am[:, 0:1], lns[p].xn[:], AX.X, ALU.max, apply_absolute_value=True), 1)
                    wait(dve, s_x, i - 1)
                    link(v.tensor_scalar(sc[p][:], am[:, 0:1], 1e-7, 1.0 / 127.0, ALU.max, ALU.mult), 2)
                    link(v.reciprocal(isc[:, 0:1], sc[p][:]), 3)
                    link(v.tensor_scalar(r1[:], lns[p].xn[:], isc[:, 0:1], MAGIC, ALU.mult, ALU.add), 4)
                    link(v.tensor_scalar(r2[:], r1[:], -MAGIC, 127.0, ALU.add, ALU.min), 5)
                    wait(dve, s_xt, i - 1)
                    v.tensor_scalar(xq[p][:], r2[:], -128.0, None, ALU.max).then_inc(s_xq, 1)

                def back(i, p):
                    wait(dve, s_acc, i + 1)
                    v.scalar_tensor_tensor(y1[:], psY[p][:, 0:DM], sc[p][:], w["fsc"][:], ALU.mult, ALU.mult).then_inc(s_y, 1)
                    wait(dve, s_y, i * 2 + 1)
                    v.tensor_tensor(y2[:], y1[:], w["fb"][:], ALU.add).then_inc(s_y, 1)
                    wait(dve, s_y, i * 2 + 2)
                    xi = c.x[:, ds(i, 1), :].rearrange("p a d -> p (a d)")
                    v.tensor_tensor(xi, xi, y2[:], ALU.add).then_inc(s_x, 1)
                front(0, 0, 0)
                front(1, 1, 0)
                back(0, 0)
                with dve.Fori(1, B // 2) as j:
                    front(j * 2, 0, j)
                    back(j * 2 - 1, 1)
                    front(j * 2 + 1, 1, j)
                    back(j * 2, 0)
                back(B - 1, 1)

            @block.gpsimd
            def _(pool):
                with pool.Fori(0, B // 2) as j:
                    lns[0].pool_rstd(pool, j)
                    lns[1].pool_rstd(pool, j)

            def pairs(body, loop):
                for p in range(2):
                    body(p, p)
                with loop(1, B // 2) as j:
                    for p in range(2):
                        body(j * 2 + p, p)

            @block.tensor
            def _(pe):
                pe.wait_ge(s_w, 1)
                pe.wait_ge(c.s_late, c.n_late)

                def tile(i, p):
                    wait(pe, s_xq, i + 1)
                    wait(pe, s_xT, i - 1)
                    for k in range(KC):
                        last = nc.tensor.transpose(psT[p][:, k, :], xq[p][:, k * P:(k + 1) * P], c.ident_b[:])
                    last.then_inc(s_xt, 1)
                    wait(pe, s_xT, i + 1)
                    wait(pe, s_y, (i - 1) * 2)
                    for k in range(KC):
                        last = nc.tensor.matmul(psY[p][:, 0:DM], xqT[p][:, k, :], wb[:, k, :], start=k == 0, stop=k == KC - 1)
                    last.then_inc(s_acc, 1)
                pairs(tile, pe.Fori)

            @block.scalar
            def _(act):
                def tile(i, p):
                    wait(act, s_xt, i + 1)
                    wait(act, s_acc, i - 1)
                    nc.scalar.copy(xqT[p][:], psT[p][:]).then_inc(s_xT, 1)
                pairs(tile, act.Fori)


def store(c, out):
    s_out = c.sem("stored")
    with c.nc.Block() as block:
        @block.sync
        def _(sp):
            sp.wait_ge(c.s_late, c.n_late)
            sp.dma_start(out.rearrange("b p d -> p b d"), c.x[:]).then_inc(s_out, 16)
            sp.wait_ge(s_out, 16)


STOP = 8


def build(nc, dram, out):
    with ExitStack() as stack:
        c = Core(nc, dram, stack)
        load_everything_small(c)
        whole = [(0, P)]
        rest = 176 - P
        parts = [
            lambda: l0_attention(c),
            lambda: moe(c, "L0", 8, 2, 1, whole, [[(0, 0, P)]]),
            lambda: small_attention(c, "L1"),
            lambda: moe(c, "L1", 16, 6, 2, [(0, P), (P, P), (2 * P, 64 + rest)],
                        [[(0, 0, P), (2, 0, rest)], [(1, 0, P), (2, 64, rest)]]),
            lambda: (c.recycle(), rotation_tables(c), small_attention(c, "L2")),
            lambda: quantized_linear(c),
            lambda: small_attention(c, "L3"),
            lambda: moe(c, "L3", 16, 4, 1, whole, [[(0, 0, P)]], shared=True),
        ]
        for part in parts[:STOP]:
            part()
        store(c, out)
        c.passing.close()


_SHAPE = (B, P, DM)


def kernel(**inputs):
    import numpy as np
    import concourse.bacc as bacc
    from concourse.bass_utils import run_bass_kernel_spmd

    a = {k: np.asarray(v) for k, v in inputs.items()}

    def packed(g, u, dn):
        n = g.shape[0]
        cut = lambda m: m.reshape(n, KC, P, m.shape[2]).transpose(0, 2, 1, 3).reshape(n, P, -1)
        return np.concatenate([cut(g), cut(u), dn.reshape(n, P, -1)], axis=2)

    t = lambda m: m.transpose(0, 2, 1)
    d = {k: a[k] for k in a if "_xattn_" in k or k in ("x", "fside_BxSx2_0", "L2_ffn_w_scale", "L2_ffn_bias")}
    d["ctxT"] = t(a["ctx_1024"])
    d["L2_ffn_weight"] = np.ascontiguousarray(a["L2_ffn_weight"].T).view(np.int32)
    d["L0_router"] = a["L0_ffn_router_w"].T
    d["L0_pack"] = packed(a["L0_ffn_w1"], a["L0_ffn_w2"], a["L0_ffn_w3"])
    d["L1_router"] = a["L1_ffn_gate_w"].T

    def pairs(m):
        m = m.reshape(8, 2, DM, 176)
        gap = np.zeros((8, DM, 16), m.dtype)
        return np.concatenate([m[:, 0, :, :P], m[:, 1, :, :P], m[:, 0, :, P:], gap, m[:, 1, :, P:]], axis=2)
    dn = pairs(a["L1_ffn_w_down"])
    dn = np.concatenate([dn, np.zeros((8, DM, 16), dn.dtype)], axis=2)
    dn = dn.reshape(8, DM, 3, P).transpose(0, 3, 2, 1)
    d["L1_pack"] = packed(pairs(t(a["L1_ffn_w_gate"])), pairs(t(a["L1_ffn_w_up"])), dn)
    heads = np.concatenate([a["L1_xattn_Wk"], a["L1_xattn_Wv"]], axis=1).reshape(CD, 16, 2, 16)
    biases = np.concatenate([a["L1_xattn_bk"], a["L1_xattn_bv"]]).reshape(16, 2, 16)
    for i, n in enumerate(("L1_k", "L1_v")):
        d[n], d[n + "_bias"] = heads[:, :, i].reshape(CD, DM), biases[:, i].reshape(DM)
    d["L3_router"] = a["L3_ffn_gate_w"].T
    d["L3_bias"] = a["L3_ffn_expert_bias"]
    both = lambda e, s: np.concatenate([t(a["L3_ffn_" + e]), t(a["L3_ffn_" + s][None])])
    d["L3_pack"] = packed(both("w_gate", "sw_gate"), both("w_up", "sw_up"), both("w_down", "sw_down"))
    p = np.arange(P)
    f = np.float32
    d["c_ident"] = np.eye(P, dtype=f)
    d["c_neg_half"] = np.full((P, 32), -0.5, f)
    d["c_ones"] = np.ones((1, P), f)
    d["c_mask8"] = ((p[:, None] // 8) % 4 == np.arange(4)).astype(f)
    d["c_mask16"] = ((p[:, None] // 16) % 4 == np.arange(4)).astype(f)
    seg = np.stack([p < P - 16, p >= P - 16], axis=1).astype(f)
    d["c_mask_seg"] = seg
    d["c_sel_seg"] = seg.T

    nc = bacc.Bacc("TRN2", target_bir_lowering=False, num_devices=1)
    arrays, dram = {}, {}
    for name, m in d.items():
        m = np.ascontiguousarray(m)
        arrays["in_" + name] = m
        dram[name] = nc.dram_tensor("in_" + name, m.shape, mybir.dt.from_np(m.dtype), kind="ExternalInput").ap()
    out = nc.dram_tensor("out", _SHAPE, F32, kind="ExternalOutput").ap()
    build(nc, dram, out)
    r = run_bass_kernel_spmd(nc, [arrays], core_ids=[0])
    return r.results[0]["out"]
```

```python
import concourse.bass as bass
from concourse import mybir
from contextlib import ExitStack

F32 = mybir.dt.float32
BF16 = mybir.dt.bfloat16
F16 = mybir.dt.float16
F32R = mybir.dt.float32r
I32 = mybir.dt.int32
I8 = mybir.dt.int8
ALU = mybir.AluOpType
ACT = mybir.ActivationFunctionType
AX = mybir.AxisListType
ds = bass.ds

P = 128
B = 16
DM = 256
KC = DM // P
CD = 128
GT = 4
NG = B // GT
LN_EPS = 1e-5
MAGIC = 12582912.0
TWO_PI = (6.28125, 1.9350051879882812e-3, 3.019916050561733e-7)
PI_LOW = 3.1415925
HIGH_BITS = -4096


def bc(ap, axis, n):
    a = ap.unsqueeze(axis)
    shape = list(a.shape)
    shape[axis] = n
    return a.to_broadcast(shape)


def wait(eng, sem, n):
    if isinstance(n, int) and n <= 0:
        return
    eng.wait_ge(sem, n)


class Core:

    def __init__(self, nc, dram, stack):
        self.nc, self.dram, self.stack = nc, dram, stack
        self.passing, self.used = ExitStack(), []
        self.layer0 = ExitStack()

    def sb(self, name, shape, dt=F32, stack=None):
        return (stack or self.stack).enter_context(self.nc.sbuf_tensor(name, shape, dt))

    def ps(self, name, shape, dt=F32, stack=None):
        return (stack or self.stack).enter_context(self.nc.psum_tensor(name, shape, dt))

    def sem(self, name, lasting=False):
        s = (self.stack if lasting else self.passing).enter_context(self.nc.semaphore(name))
        if not lasting:
            self.used.append(s)
        return s

    def passing_over(self):
        old = self.used, self.passing
        self.used, self.passing = [], ExitStack()
        return old


def load_everything_small(c):
    nc, d = c.nc, c.dram
    c.x = c.sb("x", [P, B, DM])
    c.ident = c.sb("ident", [P, P])
    c.ident_b = c.sb("ident_b", [P, P], BF16)
    c.mask8 = c.sb("mask8", [P, 4])
    c.mask16 = c.sb("mask16", [P, 4])
    c.mask_seg = c.sb("mask_seg", [P, 2])
    c.sel_seg = c.sb("sel_seg", [2, P])
    c.ones_row = c.sb("ones_row", [1, P])
    c.neg_half = c.sb("neg_half", [P, 32])
    c.pos = c.sb("pos", [P, B, 2])
    c.g0 = c.sb("g0", [P, 2])
    c.gqk = c.sb("gqk", [P, 1])
    w = c.w = {}
    w["L1q"] = c.sb("w_L1q", [P, KC, DM])
    w["L1k"] = c.sb("w_L1k", [P, DM])
    w["L1v"] = c.sb("w_L1v", [P, DM])
    w["L1d"] = c.sb("w_L1d", [P, 2 * DM])
    w["L1o"] = c.sb("w_L1o", [P, 4, DM])
    w["L1bq"] = c.sb("w_L1bq", [1, DM])
    w["L1bkv"] = c.sb("w_L1bkv", [2, 2 * DM])
    w["L1bo"] = c.sb("w_L1bo", [1, DM])
    w["L1nw"] = c.sb("w_L1nw", [P, 2, 16])
    w["L1nb"] = c.sb("w_L1nb", [P, 2, 16])
    for m in ("L2", "L3"):
        w[m + "q"] = c.sb(f"w_{m}q", [P, KC, DM])
        w[m + "kv"] = c.sb(f"w_{m}kv", [P, 2 * DM])
        w[m + "o"] = c.sb(f"w_{m}o", [P, KC, DM])
        w[m + "bo"] = c.sb(f"w_{m}bo", [1, DM])
    w["fq8"] = c.sb("w_fq8", [P, KC, DM // 4], mybir.dt.int32)
    w["fsc"] = c.sb("w_fsc", [P, DM])
    w["fb"] = c.sb("w_fb", [P, DM])
    w["L0h"] = c.sb("w_L0h", [P, 4, 3072], F32R, c.layer0)
    w["L0l"] = c.sb("w_L0l", [P, 4, 3072], F32R, c.layer0)
    c.s_first = c.sem("first_loads", True)
    c.s_late = c.sem("late_loads", True)

    def row(a):
        return a.rearrange("(o n) -> o n", o=1)

    def down(a, p=P):
        return row(a).to_broadcast([p, a.shape[0]])

    first = [
        (c.s_first, c.x[:], d["x"].rearrange("b p d -> p b d")),
        (c.s_first, c.ident[:], d["c_ident"]),
        (c.s_first, c.neg_half[:], d["c_neg_half"]),
        (c.s_first, c.g0[:, 0:1], d["L0_xattn_gq"].rearrange("(n o) -> n o", o=1)),
        (c.s_first, c.g0[:, 1:2], d["L0_xattn_gk"].rearrange("(n o) -> n o", o=1)),
    ]
    seg = P - 16
    late = [
        (c.mask8[:], d["c_mask8"]), (c.mask16[:], d["c_mask16"]),
        (c.mask_seg[:], d["c_mask_seg"]), (c.sel_seg[:], d["c_sel_seg"]),
        (c.ones_row[:], d["c_ones"]),
        (c.pos[:], d["fside_BxSx2_0"].rearrange("b p a -> p b a")),
        (w["L1q"][:], d["L1_xattn_Wq"].rearrange("(k p) n -> p k n", p=P)),
        (w["L1k"][:], d["L1_k"]), (w["L1v"][:], d["L1_v"]),
        (w["L1d"][:], d["L1_xattn_Wkv_dca"]),
        (w["L1o"][:], d["L1_o"].rearrange("(k p) n -> p k n", p=P)),
        (w["L1bq"][:], row(d["L1_xattn_bq"])), (w["L1bo"][:], row(d["L1_xattn_bo"])),
        (w["L1bkv"][0:1, 0:DM], row(d["L1_k_bias"])),
        (w["L1bkv"][0:1, DM:], row(d["L1_v_bias"])),
        (w["L1bkv"][1:2, :], row(d["L1_xattn_bkv_dca"])),
        (w["L1nw"][:, 0, :], down(d["L1_xattn_qn_w"])), (w["L1nb"][:, 0, :], down(d["L1_xattn_qn_b"])),
        (w["L1nw"][0:seg, 1, :], down(d["L1_xattn_kn_w"], seg)),
        (w["L1nb"][0:seg, 1, :], down(d["L1_xattn_kn_b"], seg)),
        (w["L1nw"][seg:, 1, :], down(d["L1_xattn_kn_dca_w"], 16)),
        (w["L1nb"][seg:, 1, :], down(d["L1_xattn_kn_dca_b"], 16)),
        (w["fq8"][:], d["L2_ffn_weight"].rearrange("(k p) n -> p k n", p=P)),
        (w["fsc"][:], down(d["L2_ffn_w_scale"].rearrange("n o -> (n o)"))),
        (w["fb"][:], down(d["L2_ffn_bias"])),
    ]
    for m in ("L2", "L3"):
        late += [
            (w[m + "q"][:], d[m + "_xattn_Wq"].rearrange("(k p) n -> p k n", p=P)),
            (w[m + "kv"][:], d[m + "_xattn_Wkv"]),
            (w[m + "o"][:], d[m + "_xattn_Wout"].rearrange("(k p) n -> p k n", p=P)),
            (w[m + "bo"][:], row(d[m + "_xattn_bout"])),
        ]
    c.n_first, c.n_late = 16 * 5, 16 * len(late)
    c.first, c.late = first, late


class TileNorm:

    def __init__(self, c, name, stack):
        self.c = c
        self.stats = c.sb(name + "_stats", [P, 6], F32, stack)
        self.mv = c.sb(name + "_mv", [P, 2], F32, stack)
        self.hold = c.sb(name + "_hold", [P, 1], F32, stack)
        self.ve = c.sb(name + "_ve", [P, 1], F32, stack)
        self.rstd = c.sb(name + "_rstd", [P, 1], F32, stack)
        self.xn = c.sb(name + "_xn", [P, DM], F32, stack)
        self.s_st = c.sem(name + "_stats")
        self.s_rs = c.sem(name + "_rstd")
        self.s_xn = c.sem(name + "_normed")

    def dve_stats(self, dve, b, n=None):
        n = b if n is None else n
        v = self.c.nc.vector
        wait(dve, self.s_xn, n)
        v.bn_stats(self.stats[:], self.c.x[:, ds(b, 1), :].rearrange("p a d -> p (a d)")).then_inc(self.s_st, 1)
        wait(dve, self.s_st, n * 3 + 1)
        v.memset(self.hold[:], 0.0)
        v.bn_aggr(self.mv[:], self.stats[:]).then_inc(self.s_st, 1)
        wait(dve, self.s_st, n * 3 + 2)
        v.tensor_scalar(self.ve[:], self.mv[:, 1:2], LN_EPS, None, ALU.add).then_inc(self.s_st, 1)

    def pool_rstd(self, pool, n):
        wait(pool, self.s_st, n * 3 + 3)
        self.c.nc.gpsimd.tensor_tensor(self.rstd[:], self.ve[:], self.c.neg_half[:, 0:1], ALU.pow).then_inc(self.s_rs, 1)

    def dve_apply(self, dve, b, s_read, n_read, n=None):
        n = b if n is None else n
        wait(dve, self.s_rs, n + 1)
        wait(dve, s_read, n_read)
        self.c.nc.vector.tensor_scalar(self.xn[:], self.c.x[:, ds(b, 1), :].rearrange("p a d -> p (a d)"),
                                       self.mv[:, 0:1], self.rstd[:], ALU.subtract, ALU.mult).then_inc(self.s_xn, 1)


class GroupNorm:
    N = 4
    GROUPS = B // N

    def __init__(self, c, name, stack):
        self.c = c
        self.stats = c.sb(name + "_stats", [P, self.N, 6], F32, stack)
        self.mv = c.sb(name + "_mv", [P, self.N, 2], F32, stack)
        self.mean = c.sb(name + "_mean", [P, B], F32, stack)
        self.hold = c.sb(name + "_hold", [P, 1], F32, stack)
        self.ve = c.sb(name + "_ve", [P, B], F32, stack)
        self.rstd = c.sb(name + "_rstd", [P, B], F32, stack)
        self.xn = [c.sb(f"{name}_xn{p}", [P, DM], F32, stack) for p in range(2)]
        self.s_st = c.sem(name + "_stats")
        self.s_rs = c.sem(name + "_rstd")
        self.s_xn = c.sem(name + "_normed")

    def tile(self, a, i):
        return a[:, ds(i, 1), :].rearrange("p a d -> p (a d)")

    def dve_stats(self, dve, g):
        v = self.c.nc.vector
        wait(dve, self.s_st, g * 4)
        for t in range(self.N):
            last = v.bn_stats(self.stats[:, t, :], self.tile(self.c.x, g * self.N + t))
        last.then_inc(self.s_st, 1)
        wait(dve, self.s_st, g * 4 + 1)
        v.memset(self.hold[:], 0.0)
        for t in range(self.N):
            last = v.bn_aggr(self.mv[:, t, :], self.stats[:, t, :])
        last.then_inc(self.s_st, 1)
        wait(dve, self.s_st, g * 4 + 2)
        v.tensor_copy(self.mean[:, ds(g * self.N, self.N)], self.mv[:, :, 0]).then_inc(self.s_st, 1)
        v.tensor_scalar(self.ve[:, ds(g * self.N, self.N)], self.mv[:, :, 1], LN_EPS, None, ALU.add).then_inc(self.s_st, 1)

    def pool_rstd(self, pool, g):
        wait(pool, self.s_st, g * 4 + 4)
        self.c.nc.gpsimd.tensor_tensor(self.rstd[:, ds(g * self.N, self.N)], self.ve[:, ds(g * self.N, self.N)],
                                       self.c.neg_half[:, 0:self.N], ALU.pow).then_inc(self.s_rs, 1)

    def dve_apply(self, dve, g, t, s_read):
        i = g * self.N + t
        if t == 0:
            wait(dve, self.s_rs, g + 1)
        wait(dve, s_read, i - 1)
        self.c.nc.vector.tensor_scalar(self.xn[t % 2][:], self.tile(self.c.x, i), self.mean[:, ds(i, 1)],
                                       self.rstd[:, ds(i, 1)], ALU.subtract, ALU.mult).then_inc(self.s_xn, 1)

    def groups(self, body, loop):
        body(0, True)
        with loop(1, self.GROUPS - 1) as g:
            body(g, True)
        body(self.GROUPS - 1, False)


def batch_schedule(body, loop):
    for b in range(3):
        body(b, b % 2)
    with loop(1, (B - 4) // 2) as j:
        body(j * 2 + 1, 1)
        body(j * 2 + 2, 0)
    for b in range(B - 3, B):
        body(b, b % 2)


def exists(b):
    return not isinstance(b, int) or 0 <= b < B


def l0_attention(c):
    nc, w = c.nc, c.w
    NH, HG = 16, 4
    G = NH // HG
    W = HG * P
    SCALE = P ** -0.5
    with ExitStack() as st:
        ln = TileNorm(c, "l0a", st)
        xf = [c.sb(f"l0_xf{p}", [P, KC + 1, P], F32, st) for p in range(2)]
        xm = c.sb("l0_xm", [P, KC + 1, P], F32, st)
        xh = [c.sb(f"l0_xh{p}", [P, KC + 1, P], F32R, st) for p in range(2)]
        xl = [c.sb(f"l0_xl{p}", [P, KC + 1, P], F32R, st) for p in range(2)]
        sq = c.sb("l0_sq", [P, 2 * HG, P], F32, st)
        ss = c.sb("l0_ss", [P, 2 * HG], F32, st)
        ms = c.sb("l0_ms", [P, 2 * HG], F32, st)
        rs = c.sb("l0_rs", [P, 2 * HG], F32, st)
        qk = c.sb("l0_qk", [P, 2 * HG, P], F32, st)
        qT = c.sb("l0_qT", [P, 2, HG, P], F32, st)
        kT = c.sb("l0_kT", [P, 2, HG, P], F32, st)
        v = c.sb("l0_v", [P, G, HG, P], F32, st)
        mx = c.sb("l0_mx", [P, HG], F32, st)
        df = c.sb("l0_df", [P, HG, P], F32, st)
        pr = c.sb("l0_pr", [P, HG, P], F32, st)
        sm = c.sb("l0_sm", [P, HG], F32, st)
        rl = c.sb("l0_rl", [P, HG], F32, st)
        buffers = c.sb("l0_buffers", [P, 4, W], F32, st)
        pn, pT, of, om = (buffers[:, i, :].rearrange("p (h n) -> p h n", h=HG) for i in range(4))
        oh = c.sb("l0_oh", [P, HG, P], F32R, st)
        ol = c.sb("l0_ol", [P, HG, P], F32R, st)
        psQK = c.ps("l0_psQK", [P, 2 * HG, P], F32, st)
        psQT = c.ps("l0_psQT", [P, 2 * HG, P], F32, st)
        psV = c.ps("l0_psV", [P, HG, P], F32, st)
        psS = c.ps("l0_psS", [P, HG, P], F32, st)
        psP = c.ps("l0_psP", [P, HG, P], F32, st)
        psY = c.ps("l0_psY", [P, 512], F32, st)
        S = lambda n: c.sem("l0_" + n)
        s_ctx, s_g = [S(f"ctx{p}") for p in range(2)], S("gqk")
        s_xt, s_xT = S("x_transposed"), S("xT_copied")
        s_qk, s_v, s_vc = S("qk_made"), S("v_made"), S("v_copied")
        s_sq, s_ss, s_ms, s_rs, s_qn = S("squares"), S("sums"), S("means"), S("rrms"), S("qk_normed")
        s_qt, s_qT, s_kT = S("qk_transposed"), S("qT_copied"), S("kT_copied")
        s_s, s_mx, s_df, s_e = S("scores"), S("maxima"), S("shifted"), S("exps")
        s_sm, s_rl, s_pn = S("exp_sums"), S("inverse_sums"), S("probs")
        s_pt, s_pT, s_o, s_oT = S("probs_transposed"), S("probs_T_copied"), S("out_made"), S("out_copied")
        s_y, s_x = S("projected"), S("x_updated")

        s_ypart = S("projected_part")
        s_xm, s_xh, s_xl = S("x_masked"), S("x_high"), S("x_low")
        s_om, s_oh, s_ol = S("out_masked"), S("out_high"), S("out_low")
        s_wm, s_wl, s_wh, s_raw = S("weights_masked"), S("weights_low"), S("weights_high"), [S(f"weights_loaded{p}") for p in range(4)]
        NP = 4
        PW = 6 * W // NP
        raw = [c.sb(f"l0_raw{p}", [P, PW], F32, st)[:] for p in range(2)]
        raw += [buffers[:].rearrange("p i n -> p (i n)")[:, p * PW:(p + 1) * PW] for p in range(2)]
        wm = c.sb("l0_wm", [P, PW], F32, st)
        wh, wl = w["L0h"], w["L0l"]
        FP = 4 * W
        PASSES = (0, 0), (1, 0), (0, 1)

        def dve_W(dve, g):
            v = nc.vector
            for i in range(NP):
                n = g * NP + i
                dve.wait_ge(s_raw[n % 4], (n // 4 + 1) * 16)
                wait(dve, s_wh, n)
                wait(dve, s_wl, n)
                v.tensor_scalar(wm[:].bitcast(I32), raw[n % 4].bitcast(I32), HIGH_BITS, None, ALU.bitwise_and).then_inc(s_wm, 1)
                dve.wait_ge(s_wm, n + 1)
                v.tensor_tensor(wl[:, g, i * PW:(i + 1) * PW], raw[n % 4], wm[:], ALU.subtract).then_inc(s_wl, 1)

        def act_W(act, g):
            for i in range(NP):
                act.wait_ge(s_wm, g * NP + i + 1)
                nc.scalar.copy(wh[:, g, i * PW:(i + 1) * PW], wm[:]).then_inc(s_wh, 1)

        def dve_XM(dve, b, p):
            wait(dve, s_xT, b + 1)
            wait(dve, s_ctx[p], (b - p) * 8 + 16)
            wait(dve, s_xh, b)
            wait(dve, s_xl, b)
            nc.vector.tensor_scalar(xm[:].bitcast(I32), xf[p][:].bitcast(I32), HIGH_BITS, None, ALU.bitwise_and).then_inc(s_xm, 1)

        def act_XH(act, b, p):
            wait(act, s_xm, b + 1)
            wait(act, s_v, (b - 1) * G)
            nc.scalar.copy(xh[p][:], xm[:]).then_inc(s_xh, 1)

        def pool_XL(pool, b, p):
            wait(pool, s_xm, b + 1)
            wait(pool, s_v, (b - 1) * G)
            nc.gpsimd.tensor_tensor(xl[p][:], xf[p][:], xm[:], ALU.subtract).then_inc(s_xl, 1)

        def dve_OM(dve, b, g, p):
            n = b * G + g
            wait(dve, s_oT, n + 1)
            wait(dve, s_oh, n)
            wait(dve, s_ol, n)
            nc.vector.tensor_scalar(om.bitcast(I32), of.bitcast(I32), HIGH_BITS, None, ALU.bitwise_and).then_inc(s_om, 1)

        def out_used(eng, b, g):
            if g == 0:
                wait(eng, s_y, b)
            else:
                wait(eng, s_ypart, b * (G - 1) + g)

        def act_OH(act, b, g, p):
            wait(act, s_om, b * G + g + 1)
            out_used(act, b, g)
            nc.scalar.copy(oh[:], om[:]).then_inc(s_oh, 1)

        def pool_OL(pool, b, g, p):
            wait(pool, s_om, b * G + g + 1)
            out_used(pool, b, g)
            nc.gpsimd.tensor_tensor(ol[:], of[:], om[:], ALU.subtract).then_inc(s_ol, 1)

        def pe_A(pe, b):
            wait(pe, ln.s_xn, b + 1)
            wait(pe, s_pT, b * G - G)
            for k in range(KC):
                last = nc.tensor.transpose(psP[:, k, :], ln.xn[:, k * P:(k + 1) * P], c.ident[:])
            last.then_inc(s_xt, 1)

        def pe_F(pe, b, g, p):
            n = b * G + g
            wait(pe, s_xh, b + 1)
            wait(pe, s_xl, b + 1)
            if isinstance(b, int) and b == 0:
                wait(pe, s_wh, g * NP + 3)
                wait(pe, s_wl, g * NP + 3)
            wait(pe, s_qn, n)
            x, ww = (xh[p], xl[p]), (wh, wl)
            parts = [(k, i, j) for k in range(KC) for i, j in PASSES]
            for m, (k, i, j) in enumerate(parts):
                nc.tensor.matmul(psQK[:, 0:HG, :], x[i][:, k, :], ww[j][:, g, k * W:(k + 1) * W],
                                 start=m == 0, stop=m == len(parts) - 1)
            for m, (i, j) in enumerate(PASSES):
                last = nc.tensor.matmul(psQK[:, HG:, :], x[i][:, KC, :], ww[j][:, g, KC * W:(KC + 1) * W],
                                        start=m == 0, stop=m == 2)
            last.then_inc(s_qk, 1)
            wait(pe, s_oT, n - 3)
            wait(pe, s_vc, n)
            for m, (i, j) in enumerate(PASSES):
                last = nc.tensor.matmul(psV[:], x[i][:, KC, :], ww[j][:, g, (KC + 1) * W:(KC + 2) * W],
                                        start=m == 0, stop=m == 2)
            last.then_inc(s_v, 1)

        def pe_FT(pe, b, g, p):
            n = b * G + g
            wait(pe, s_qn, n + 1)
            wait(pe, s_kT, n)
            for h in range(2 * HG):
                last = nc.tensor.transpose(psQT[:, h, :], qk[:, h, :], c.ident[:])
            last.then_inc(s_qt, 1)

        def pe_S(pe, b, g, p):
            n = b * G + g
            wait(pe, s_kT, n + 1)
            wait(pe, s_df, n)
            for h in range(HG):
                last = nc.tensor.matmul(psS[:, h, :], qT[:, g % 2, h, :], kT[:, g % 2, h, :], start=True, stop=True)
            last.then_inc(s_s, 1)

        def pe_T(pe, b, g):
            n = b * G + g
            wait(pe, s_pn, n + 1)
            wait(pe, s_pT, n)
            if g == 0 and exists(b + 1):
                wait(pe, s_xT, b + 2)
            for h in range(HG):
                last = nc.tensor.transpose(psP[:, h, :], pn[:, h, :], c.ident[:])
            last.then_inc(s_pt, 1)

        def pe_O(pe, b, g):
            n = b * G + g
            wait(pe, s_pT, n + 1)
            wait(pe, s_vc, min(n + 4, B * G) if isinstance(n, int) else n + 4)
            for h in range(HG):
                last = nc.tensor.matmul(psV[:, h, :], v[:, g, h, :], pT[:, h, :], start=True, stop=True)
            last.then_inc(s_o, 1)

        def pe_Y(pe, b, g, p):
            n = b * G + g
            wait(pe, s_oh, n + 1)
            wait(pe, s_ol, n + 1)
            if isinstance(b, int) and b == 0:
                wait(pe, s_wh, g * NP + NP)
                wait(pe, s_wl, g * NP + NP)
            if g == 0:
                wait(pe, s_x, b)
            o, ww = (oh, ol), (wh, wl)
            parts = [(h, i, j) for h in range(HG) for i, j in PASSES]
            for m, (h, i, j) in enumerate(parts):
                last = nc.tensor.matmul(psY[:, 0:DM], o[i][:, h, :], ww[j][:, g, FP + h * DM:FP + (h + 1) * DM],
                                        start=g == 0 and m == 0, stop=g == G - 1 and m == len(parts) - 1)
            last.then_inc(s_y if g == G - 1 else s_ypart, 1)

        def dve_F1(dve, b, g, p):
            n = b * G + g
            wait(dve, s_sq, n + 1)
            nc.vector.tensor_reduce(ss[:], sq[:], AX.X, ALU.add).then_inc(s_ss, 1)
            wait(dve, s_ss, n + 1)
            nc.vector.tensor_scalar(ms[:], ss[:], 1.0 / P, 1e-5, ALU.mult, ALU.add).then_inc(s_ms, 1)

        def dve_F2(dve, b, g, p):
            n = b * G + g
            wait(dve, s_rs, n + 1)
            wait(dve, s_qt, n)
            nc.vector.tensor_tensor(qk[:], psQK[:], bc(rs[:], 2, P), ALU.mult).then_inc(s_qn, 1)

        def dve_S(dve, b, g, p):
            n = b * G + g
            wait(dve, s_s, n + 1)
            nc.vector.tensor_reduce(mx[:], psS[:], AX.X, ALU.max).then_inc(s_mx, 1)
            wait(dve, s_mx, n + 1)
            wait(dve, s_e, n)
            nc.vector.tensor_tensor(df[:], psS[:], bc(mx[:], 2, P), ALU.subtract).then_inc(s_df, 1)

        def dve_T(dve, b, g):
            n = b * G + g
            wait(dve, s_e, n + 1)
            nc.vector.tensor_reduce(sm[:], pr[:], AX.X, ALU.add).then_inc(s_sm, 1)
            wait(dve, s_sm, n + 1)
            nc.vector.reciprocal(rl[:], sm[:]).then_inc(s_rl, 1)
            wait(dve, s_rl, n + 1)
            wait(dve, s_pt, n)
            nc.vector.tensor_tensor(pn[:], pr[:], bc(rl[:], 2, P), ALU.mult).then_inc(s_pn, 1)

        def dve_X(dve, b):
            wait(dve, s_y, b + 1)
            xb = c.x[:, ds(b, 1), :].rearrange("p a d -> p (a d)")
            nc.vector.tensor_tensor(xb, xb, psY[:, 0:DM], ALU.add).then_inc(s_x, 1)

        def act_A(act, b, p):
            wait(act, s_xt, b + 1)
            wait(act, s_xl, b - 1)
            nc.scalar.copy(xf[p][:, 0:KC, :], psP[:, 0:KC, :]).then_inc(s_xT, 1)

        def act_F(act, b, g, p):
            n = b * G + g
            wait(act, s_qk, n + 1)
            wait(act, s_ss, n)
            nc.scalar.activation(sq[:], psQK[:], ACT.Square).then_inc(s_sq, 1)

        def act_V(act, b, g, p):
            n = b * G + g
            wait(act, s_v, n + 1)
            wait(act, s_o, n - 3)
            nc.scalar.copy(v[:, g], psV[:]).then_inc(s_vc, 1)

        def act_FT(act, b, g, p):
            n = b * G + g
            wait(act, s_qt, n + 1)
            wait(act, s_s, n - 1)
            nc.scalar.copy(qT[:, g % 2], psQT[:, 0:HG, :]).then_inc(s_qT, 1)
            nc.scalar.activation(kT[:, g % 2], psQT[:, HG:, :], ACT.Copy, scale=c.gqk[:]).then_inc(s_kT, 1)

        def act_S(act, b, g, p):
            n = b * G + g
            wait(act, s_df, n + 1)
            wait(act, s_pn, n)
            nc.scalar.activation(pr[:], df[:], ACT.Exp, scale=SCALE).then_inc(s_e, 1)

        def act_T(act, b, g):
            n = b * G + g
            wait(act, s_pt, n + 1)
            wait(act, s_o, n)
            nc.scalar.copy(pT[:], psP[:]).then_inc(s_pT, 1)

        def act_O(act, b, g):
            wait(act, s_o, b * G + g + 1)
            wait(act, s_ol, b * G + g)
            nc.scalar.copy(of[:], psV[:]).then_inc(s_oT, 1)

        def at(fn, eng, b, g, p, ahead):
            e, gg = divmod(g + ahead, G)
            if exists(b + e):
                fn(eng, b + e, gg, p ^ (e & 1))

        with nc.Block() as block:
            @block.sync
            def _(sp):
                for n, (sem, dst, src) in enumerate(c.first):
                    sp.dma_start(dst, src).then_inc(sem, 16)
                    if n == 2:
                        sp.dma_start(xf[0][:, KC, :], c.dram["ctxT"][0]).then_inc(s_ctx[0], 16)
                        sp.dma_start(xf[1][:, KC, :], c.dram["ctxT"][1]).then_inc(s_ctx[1], 16)
                for n in range(NP * G):
                    wait(sp, s_wl, n - 3)
                    g, i = divmod(n, NP)
                    sp.dma_start(raw[n % 4], c.dram["L0_attn"][:, g, i * PW:(i + 1) * PW]).then_inc(s_raw[n % 4], 16)
                for dst, src in c.late:
                    sp.dma_start(dst, src).then_inc(c.s_late, 16)
                with sp.Fori(0, (B - 2) // 2) as j:
                    for p in range(2):
                        wait(sp, s_xl, j * 2 + p + 1)
                        sp.dma_start(xf[p][:, KC:, :], c.dram["ctxT"][ds(j * 2 + p + 2, 1)].rearrange("a p d -> p a d")).then_inc(s_ctx[p], 16)

            @block.tensor
            def _(pe):
                pe.wait_ge(c.s_first, c.n_first)
                pe_A(pe, 0)
                pe_F(pe, 0, 0, 0)
                pe_FT(pe, 0, 0, 0)
                pe_F(pe, 0, 1, 0)
                pe_FT(pe, 0, 1, 0)
                pe_F(pe, 0, 2, 0)
                pe_S(pe, 0, 0, 0)

                def body(b, p):
                    for g in range(G):
                        at(pe_S, pe, b, g, p, 1)
                        if g == 0 and exists(b + 1):
                            pe_A(pe, b + 1)
                        pe_T(pe, b, g)
                        at(pe_F, pe, b, g, p, 3)
                        at(pe_FT, pe, b, g, p, 2)
                        at(pe_Y, pe, b, g, p, -1)
                        pe_O(pe, b, g)
                batch_schedule(body, pe.Fori)
                pe_Y(pe, B - 1, G - 1, 1)

            @block.vector
            def _(dve):
                dve.wait_ge(c.s_first, c.n_first)
                nc.vector.tensor_tensor(c.gqk[:], c.g0[:, 0:1], c.g0[:, 1:2], ALU.mult).then_inc(s_g, 1)
                ln.dve_stats(dve, 0)
                ln.dve_apply(dve, 0, s_xt, 0)
                dve_W(dve, 0)
                dve_XM(dve, 0, 0)
                dve_W(dve, 1)
                dve_F1(dve, 0, 0, 0)
                dve_F2(dve, 0, 0, 0)
                dve_W(dve, 2)
                ln.dve_stats(dve, 1)
                ln.dve_apply(dve, 1, s_xt, 1)
                dve_F1(dve, 0, 1, 0)
                dve_F2(dve, 0, 1, 0)
                dve_W(dve, 3)
                dve_S(dve, 0, 0, 0)
                dve_F1(dve, 0, 2, 0)
                dve.wait_ge(s_wl, NP * G)

                def body(b, p):
                    for g in range(G):
                        dve_T(dve, b, g)
                        at(dve_F2, dve, b, g, p, 2)
                        at(dve_OM, dve, b, g, p, -1)
                        at(dve_S, dve, b, g, p, 1)
                        if g == 0 and exists(b + 1):
                            dve_XM(dve, b + 1, p ^ 1)
                        if g == 1 and exists(b - 1):
                            dve_X(dve, b - 1)
                        if exists(b + 2):
                            if g == 1:
                                ln.dve_stats(dve, b + 2)
                            if g == 2:
                                ln.dve_apply(dve, b + 2, s_xt, b + 2)
                        at(dve_F1, dve, b, g, p, 3)
                batch_schedule(body, dve.Fori)
                dve_OM(dve, B - 1, G - 1, 1)
                dve_X(dve, B - 1)

            @block.gpsimd
            def _(pool):
                def rms(pool, b, g, p):
                    n = b * G + g
                    wait(pool, s_ms, n + 1)
                    wait(pool, s_qn, n)
                    nc.gpsimd.tensor_tensor(rs[:], ms[:], c.neg_half[:, 0:2 * HG], ALU.pow).then_inc(s_rs, 1)
                pool.wait_ge(c.s_first, c.n_first)
                ln.pool_rstd(pool, 0)
                pool_XL(pool, 0, 0)
                rms(pool, 0, 0, 0)
                ln.pool_rstd(pool, 1)
                rms(pool, 0, 1, 0)
                rms(pool, 0, 2, 0)

                def body(b, p):
                    for g in range(G):
                        at(pool_OL, pool, b, g, p, -1)
                        if g == 0 and exists(b + 1):
                            pool_XL(pool, b + 1, p ^ 1)
                        if g == 1 and exists(b + 2):
                            ln.pool_rstd(pool, b + 2)
                        at(rms, pool, b, g, p, 3)
                batch_schedule(body, pool.Fori)
                pool_OL(pool, B - 1, G - 1, 1)

            @block.scalar
            def _(act):
                act.wait_ge(s_g, 1)
                nc.scalar.copy(c.ident_b[:], c.ident[:])
                act_A(act, 0, 0)
                act_W(act, 0)
                act_XH(act, 0, 0)
                act_W(act, 1)
                act_F(act, 0, 0, 0)
                act_V(act, 0, 0, 0)
                act_FT(act, 0, 0, 0)
                act_W(act, 2)
                act_F(act, 0, 1, 0)
                act_V(act, 0, 1, 0)
                act_FT(act, 0, 1, 0)
                act_W(act, 3)
                act_F(act, 0, 2, 0)
                act_V(act, 0, 2, 0)
                act_S(act, 0, 0, 0)

                def body(b, p):
                    for g in range(G):
                        if g == 0 and exists(b + 1):
                            act_A(act, b + 1, p ^ 1)
                        act_T(act, b, g)
                        at(act_S, act, b, g, p, 1)
                        at(act_F, act, b, g, p, 3)
                        at(act_OH, act, b, g, p, -1)
                        at(act_V, act, b, g, p, 3)
                        at(act_FT, act, b, g, p, 2)
                        if g == 0 and exists(b + 1):
                            act_XH(act, b + 1, p ^ 1)
                        act_O(act, b, g)
                batch_schedule(body, act.Fori)
                act_OH(act, B - 1, G - 1, 1)


def small_attention(c, name):
    nc, w = c.nc, c.w
    L1 = name == "L1"
    HD = 16 if L1 else 8
    NH = DM // HD
    HG = 4
    G = NH // HG
    RT = HG * HD
    SEG = P - 16
    HV = (2 if L1 else 1) * HD
    HALF = P // 2
    HR = HALF // HV
    NR = NH // HR
    PER = 2 * HR * P
    SCALE = HD ** -0.5
    mask = c.mask16 if L1 else c.mask8
    with ExitStack() as st:
        sb = lambda n, shape: c.sb(f"{name}_{n}", shape, F32, st)
        ps = lambda n, shape: c.ps(f"{name}_{n}", shape, F32, st)
        S = lambda n: c.sem(f"{name}_{n}")
        ln = TileNorm(c, name + "a", st)
        xT = sb("xT", [P, KC, P])
        ctx = sb("ctx", [P, 2, 2, P])
        t1 = sb("t1", [P, 2 * DM])
        t2 = sb("t2", [P, 2 * DM])
        qk = sb("qk", [P, 2 * DM])
        kT = sb("kT", [P, KC, P]) if L1 else None
        qT = [sb(f"qT{p}", [P, KC, P]) for p in range(2)] if L1 else None
        kbd = [sb(f"kbd{p}", [P, KC, HG, P]) for p in range(2)] if L1 else None
        if not L1:
            qkT = sb("qkT", [P, 2 * KC, P])
            qkTm = sb("qkTm", [P, 2 * KC, P])
            low = [c.sb(f"{name}_low{p}", [P, 2 * KC, P], F32R, st) for p in range(2)]
            qTh = [c.sb(f"{name}_qTh{p}", [P, KC, P], F32R, st) for p in range(2)]
            kbh = [c.sb(f"{name}_kbh{p}", [P, KC, HG, P], F32R, st) for p in range(2)]
            kbl = [c.sb(f"{name}_kbl{p}", [P, KC, HG, P], F32R, st) for p in range(2)]
            s_m, s_lo = S("qk_masked"), S("qk_low")
        vx = [sb(f"vx{p}", [P, NH * P]) for p in range(2)]
        mx = sb("mx", [P, 2, HG, 2])
        df = sb("df", [P, 2, HG, P])
        pr = sb("pr", [P, 2, HG, P])
        pT = sb("pT", [P, 2, HG, P])
        es = sb("es", [P, NR // 2, P])
        ov = sb("ov", [P, NR // 2, P])
        rl = sb("rl", [P, NR // 2, P])
        oT = sb("oT", [P, NR // 2, P])
        n32 = sb("n32", [P, 4, 32]) if L1 else None
        psS = [ps(f"psS{p}", [P, HG, P]) for p in range(2)]
        psP = ps("psP", [P, HG, P])
        psO = [ps(f"psO{p}", [P, 4, P]) for p in range(2)]
        psT = ps("psT", [P, 4, P])
        psA = ps("psA", [P, 512])
        psV = ps("psV", [P, 512])
        s_ctx, s_pre = [S(f"ctx{p}") for p in range(2)], S("prepared")
        s_xt, s_xT, s_qk, s_v, s_vc = S("x_transposed"), S("xT_copied"), S("qk_made"), S("v_made"), S("v_copied")
        s_ch, s_n, s_qn = S("qk_chain"), S("qk_rstd"), S("qk_ready")
        s_qt, s_qT, s_kT, s_kb = S("qk_transposed"), S("qT_copied"), S("kT_copied"), S("keys_diagonal")
        s_s, s_mx, s_df, s_e = S("scores"), S("maxima"), S("shifted"), S("exps")
        s_z, s_pad = S("slots_zeroed"), S("context_zeroed")
        s_pt, s_pT, s_o = S("probs_transposed"), S("probs_T_copied"), S("out_made")
        s_oc = S("out_copied")
        s_rl, s_on, s_y, s_x = S("inverse_sums"), S("out_divided"), S("projected"), S("x_updated")
        CH = 5 if L1 else 3
        ND = 2 if L1 else 1
        NV = 4 if L1 else 2
        PRE = 2

        def slots(p, region_odd, half, seg):
            base = region_odd * HR * P + (half ^ region_odd) * HALF + seg * HR * HD
            stride = P + HD
            start = min(base, PER - HR * stride)
            a = vx[p][:].rearrange("p (r n) -> p r n", n=PER)[:, :, start:start + HR * stride]
            a = a.rearrange("p r (j c) -> p r j c", c=stride)
            return a[:, :, :, base - start:base - start + HD]

        def pe_A1(pe, b):
            wait(pe, ln.s_xn, b + 1)
            if L1:
                wait(pe, s_ch, (b - 1) * CH + 3)
            else:
                wait(pe, s_qn, b)
            for k in range(KC):
                last = nc.tensor.transpose(psA[:, k * P:(k + 1) * P], ln.xn[:, k * P:(k + 1) * P], c.ident[:])
            last.then_inc(s_xt, 1)

        def act_A1(act, b):
            wait(act, s_xt, b + 1)
            wait(act, s_qk, b)
            nc.scalar.copy(xT[:], psA[:, 0:KC * P].rearrange("p (k n) -> p k n", k=KC)).then_inc(s_xT, 1)

        def pe_A2(pe, b, p):
            wait(pe, s_xT, b + 1)
            wait(pe, s_ctx[p], (b - p) * (8 * ND) + 16 * ND)
            wq = w[name + "q"]
            mm = nc.tensor.matmul
            for k in range(KC):
                mm(psA[:, 0:DM], xT[:, k, :], wq[:, k, :], start=k == 0, stop=k == KC - 1 and not L1)
            if L1:
                mm(psA[:, 0:DM], c.ones_row[:], w["L1bq"][:], start=False, stop=True)
                mm(psA[:, DM:], ctx[:, p, 0, :], w["L1k"][:], start=True, stop=False)
                mm(psA[:, DM:], ctx[:, p, 1, :], w["L1d"][:, 0:DM], start=False, stop=False)
                mm(psA[:, DM:], c.sel_seg[:], w["L1bkv"][:, 0:DM], start=False, stop=True).then_inc(s_qk, 1)
            else:
                mm(psA[:, DM:], ctx[:, p, 0, :], w[name + "kv"][:, 0:DM], start=True, stop=True).then_inc(s_qk, 1)

        def pe_V(pe, b, p):
            wait(pe, s_vc, b * NV)
            wait(pe, s_x, b - 2)
            mm = nc.tensor.matmul
            if L1:
                mm(psV[:, 0:DM], ctx[:, p, 0, :], w["L1v"][:], start=True, stop=False)
                mm(psV[:, 0:DM], ctx[:, p, 1, :], w["L1d"][:, DM:], start=False, stop=False)
                mm(psV[:, 0:DM], c.sel_seg[:], w["L1bkv"][:, DM:], start=False, stop=True).then_inc(s_v, 1)
            else:
                mm(psV[:, 0:DM], ctx[:, p, 0, :], w[name + "kv"][:, DM:], start=True, stop=True).then_inc(s_v, 1)

        def act_V(act, b, p):
            wait(act, s_v, b + 1)
            wait(act, s_o, (b - 1) * G)
            vs = psV[:, 0:DM].rearrange("p (r o j d) -> p r o j d", o=2, j=HR, d=HD)
            for odd in range(2):
                if L1:
                    for i in range(2):
                        nc.scalar.activation(slots(p, odd, 0, i), vs[:, :, odd], ACT.Copy,
                                             scale=c.mask_seg[:, i:i + 1]).then_inc(s_vc, 1)
                else:
                    nc.scalar.copy(slots(p, odd, 0, 0), vs[:, :, odd]).then_inc(s_vc, 1)

        def dve_A2(dve, b):
            v = nc.vector
            wait(dve, s_qk, b + 1)
            if L1:
                wait(dve, s_qn, b)
            else:
                wait(dve, s_qt, b)

            def link(ins, n):
                ins.then_inc(s_ch, 1)
                dve.wait_ge(s_ch, b * CH + n)
            if L1:
                h3 = lambda a: a.rearrange("p (h d) -> p h d", d=HD)
                link(v.tensor_reduce(n32[:, 0, :], h3(psA[:]), AX.X, ALU.add), 1)
                link(v.tensor_scalar(n32[:, 1, :], n32[:, 0, :], 1.0 / HD, None, ALU.mult), 2)
                link(v.tensor_tensor(h3(t1[:]), h3(psA[:]), bc(n32[:, 1, :], 2, HD), ALU.subtract), 3)
                dve.wait_ge(s_sq, b + 1)
                link(v.tensor_reduce(n32[:, 2, :], h3(t2[:]), AX.X, ALU.add), 4)
                v.tensor_scalar(n32[:, 2, :], n32[:, 2, :], 1.0 / HD, 1e-6, ALU.mult, ALU.add).then_inc(s_ch, 1)
            else:
                f = lambda a: a.rearrange("p (h r) -> p h r", r=8)
                cb = bc(c.cos2[:, ds(b, 1), :].rearrange("p a r -> p (a r)"), 1, 64)
                v.tensor_tensor(f(t1[:]), f(psA[:]), cb, ALU.mult).then_inc(s_ch, 1)
                for i in range(2):
                    sbc = bc(c.sin2[:, ds(b, 1), i:8:2].rearrange("p a r -> p (a r)"), 1, 64)
                    last = v.tensor_tensor(f(t2[:])[:, :, i:8:2], f(psA[:])[:, :, 1 - i:8:2], sbc, ALU.mult)
                    last.then_inc(s_ch, 1)
                dve.wait_ge(s_ch, b * CH + 3)
                v.tensor_tensor(qk[:], t1[:], t2[:], ALU.add).then_inc(s_qn, 1)

        def act_square(act, b):
            if L1:
                wait(act, s_ch, b * CH + 3)
                nc.scalar.activation(t2[:], t1[:], ACT.Square).then_inc(s_sq, 1)
        s_sq = S("squares") if L1 else None

        def pool_A2(pool, b):
            if L1:
                wait(pool, s_ch, b * CH + 5)
                nc.gpsimd.tensor_tensor(n32[:, 3, :], n32[:, 2, :], c.neg_half[:], ALU.pow).then_inc(s_n, 1)

        def dve_A2b(dve, b):
            if L1:
                v = nc.vector
                s4 = lambda a: a.rearrange("p (s h d) -> p s h d", s=2, d=HD)
                wait(dve, s_n, b + 1)
                h3 = lambda a: a.rearrange("p (h d) -> p h d", d=HD)
                v.tensor_tensor(h3(t2[:]), h3(t1[:]), bc(n32[:, 3, :], 2, HD), ALU.mult).then_inc(s_nm, 1)
                dve.wait_ge(s_nm, b * 2 + 1)
                v.tensor_tensor(s4(t1[:]), s4(t2[:]), bc(w["L1nw"][:], 2, 16), ALU.mult).then_inc(s_nm, 1)
                dve.wait_ge(s_nm, b * 2 + 2)
                wait(dve, s_qt, b)
                v.tensor_tensor(s4(qk[:]), s4(t1[:]), bc(w["L1nb"][:], 2, 16), ALU.add).then_inc(s_qn, 1)
        s_nm = S("qk_norm_links")

        def pe_A3(pe, b):
            wait(pe, s_qn, b + 1)
            wait(pe, s_kT, b)
            for k in range(4):
                last = nc.tensor.transpose(psT[:, k, :], qk[:, k * P:(k + 1) * P], c.ident[:])
            last.then_inc(s_qt, 1)

        def act_A3(act, b, p):
            wait(act, s_qt, b + 1)
            if not L1:
                wait(act, s_lo, b)
                nc.scalar.copy(qkT[:], psT[:]).then_inc(s_kT, 1)
                return
            wait(act, s_s, (b - 1) * G)
            nc.scalar.copy(qT[p][:], psT[:, 0:KC, :]).then_inc(s_qT, 1)
            wait(act, s_kb, b * KC)
            nc.scalar.copy(kT[:], psT[:, KC:, :]).then_inc(s_kT, 1)

        def act_A3b(act, b, p):
            wait(act, s_m, b + 1)
            wait(act, s_s, (b - 1) * G)
            nc.scalar.copy(qTh[p][:], qkTm[:, 0:KC, :]).then_inc(s_qT, 1)

        def dve_A3(dve, b, p):
            v = nc.vector
            wait(dve, s_kT, b + 1)
            wait(dve, s_qT, b)
            wait(dve, s_kb, b * 2 * KC)
            wait(dve, s_lo, b)
            v.tensor_scalar(qkTm[:].bitcast(I32), qkT[:].bitcast(I32), HIGH_BITS, None, ALU.bitwise_and).then_inc(s_m, 1)
            wait(dve, s_m, b + 1)
            wait(dve, s_s, (b - 1) * G)
            v.tensor_tensor(low[p][:], qkT[:], qkTm[:], ALU.subtract).then_inc(s_lo, 1)

        def pool_A3(pool, b, p):
            if not L1:
                wait(pool, s_m, b + 1)
                wait(pool, s_lo, b + 1)
                wait(pool, s_s, (b - 1) * G)
                for k in range(KC):
                    for dst, src in ((kbh, qkTm[:]), (kbl, low[p][:].bitcast(F32))):
                        nc.gpsimd.tensor_tensor(dst[p][:, k], bc(src[:, KC + k, :], 1, HG), bc(mask[:], 2, P),
                                                ALU.mult).then_inc(s_kb, 1)
                return
            wait(pool, s_kT, b + 1)
            wait(pool, s_s, (b - 1) * G)
            for k in range(KC):
                nc.gpsimd.tensor_tensor(kbd[p][:, k], bc(kT[:, k, :], 1, HG), bc(mask[:], 2, P), ALU.mult).then_inc(s_kb, 1)

        def pe_S(pe, b, g, p):
            n = b * G + g
            if (g * RT) % P == 0:
                wait(pe, s_kb, b * KC + (g * RT) // P + 1 if L1 else b * 2 * KC + 2 * ((g * RT) // P + 1))
                wait(pe, s_qT, b + 1)
            wait(pe, s_df, (n - 1) * (2 if L1 else 1))
            k, r = (g * RT) // P, (g * RT) % P
            if L1:
                nc.tensor.matmul(psS[g % 2][:], qT[p][r:r + RT, k, :], kbd[p][r:r + RT, k], start=True, stop=True).then_inc(s_s, 1)
            else:
                for i, (a, z) in enumerate(((qTh, kbh), (low, kbh), (qTh, kbl))):
                    last = nc.tensor.matmul(psS[g % 2][:], a[p][r:r + RT, k, :], z[p][r:r + RT, k], start=i == 0, stop=i == 2)
                last.then_inc(s_s, 1)

        def dve_S(dve, b, g):
            n = b * G + g
            v = nc.vector
            wait(dve, s_s, n + 1)
            q = g % 2
            wait(dve, s_e, n - 1)
            if L1:
                v.tensor_reduce(mx[:, q, :, 0], psS[q][:, :, 0:SEG], AX.X, ALU.max).then_inc(s_mx, 1)
                v.tensor_reduce(mx[:, q, :, 1], psS[q][:, :, SEG:], AX.X, ALU.max).then_inc(s_mx, 1)
                dve.wait_ge(s_mx, n * 2 + 2)
                v.tensor_tensor(df[:, q, :, 0:SEG], psS[q][:, :, 0:SEG], bc(mx[:, q, :, 0], 2, SEG), ALU.subtract).then_inc(s_df, 1)
                v.tensor_tensor(df[:, q, :, SEG:], psS[q][:, :, SEG:], bc(mx[:, q, :, 1], 2, P - SEG), ALU.subtract).then_inc(s_df, 1)
            else:
                v.tensor_reduce(mx[:, q, :, 0], psS[q][:], AX.X, ALU.max).then_inc(s_mx, 1)
                dve.wait_ge(s_mx, n + 1)
                v.tensor_tensor(df[:, q], psS[q][:], bc(mx[:, q, :, 0], 2, P), ALU.subtract).then_inc(s_df, 1)

        def act_S(act, b, g):
            n = b * G + g
            wait(act, s_df, (n + 1) * (2 if L1 else 1))
            wait(act, s_pt, n - 1)
            nc.scalar.activation(pr[:, g % 2], df[:, g % 2], ACT.Exp, scale=SCALE).then_inc(s_e, 1)

        def pe_T(pe, b, g):
            n = b * G + g
            wait(pe, s_e, n + 1)
            wait(pe, s_pT, n)
            for h in range(HG):
                last = nc.tensor.transpose(psP[:, h, :], pr[:, g % 2, h, :], c.ident[:])
            last.then_inc(s_pt, 1)

        def act_T(act, b, g):
            n = b * G + g
            wait(act, s_pt, n + 1)
            wait(act, s_o, n - 1)
            nc.scalar.copy(pT[:, g % 2], psP[:]).then_inc(s_pT, 1)

        def pe_O(pe, b, g, p):
            n = b * G + g
            wait(pe, s_pT, n + 1)
            if g == 0:
                wait(pe, s_vc, (b + 1) * NV)
            i = g // (G // 2)
            if g == i * (G // 2):
                wait(pe, s_oc, (b * 2 + i - 1) * 4)
            for j in range(HG):
                h = g * HG + j
                last = nc.tensor.matmul(psO[i][:, (h // HR) % (NR // 2), :], vx[p][:, h * P:(h + 1) * P], pT[:, g % 2, j, :],
                                        start=h % HR == 0, stop=h % HR == HR - 1)
            last.then_inc(s_o, 1)

        def act_E1(act, b, i):
            R = NR // 4
            wait(act, s_o, b * G + (i + 1) * (G // 2))
            wait(act, s_on, b * 2 + i - 1)
            halves = (slice(0, HALF), slice(HALF, P))
            for odd, (a, z) in enumerate((halves, halves[::-1])):
                nc.scalar.copy(es[a, i * R:(i + 1) * R, :], psO[i][z, odd:NR // 2:2, :]).then_inc(s_oc, 1)
                nc.scalar.copy(ov[a, i * R:(i + 1) * R, :], psO[i][a, odd:NR // 2:2, :]).then_inc(s_oc, 1)

        def dve_E1(dve, b, i):
            v = nc.vector
            R = NR // 4
            wait(dve, s_oc, (b * 2 + i + 1) * 4)
            wait(dve, s_on, b * 2 + i)
            if i == 0:
                wait(dve, s_y, b)
            half = slice(i * R, (i + 1) * R)
            v.reciprocal(rl[:, half, :], es[:, half, :]).then_inc(s_rl, 1)
            wait(dve, s_rl, b * 2 + i + 1)
            v.tensor_tensor(oT[:, half, :], ov[:, half, :], rl[:, half, :], ALU.mult).then_inc(s_on, 1)

        def pe_E2(pe, b):
            wait(pe, s_on, b * 2 + 2)
            wait(pe, s_x, b)
            wait(pe, s_vc, (min(b + 3, B) if isinstance(b, int) else b + 3) * NV)
            ypart = psV[:, DM:]
            for k in range(NR // 2):
                nc.tensor.matmul(ypart, oT[:, k, :], w[name + "o"][:, k, :], start=k == 0, stop=False)
            nc.tensor.matmul(ypart, c.ones_row[:], w[name + "bo"][:], start=False, stop=True).then_inc(s_y, 1)

        def dve_E2(dve, b):
            wait(dve, s_y, b + 1)
            xb = c.x[:, ds(b, 1), :].rearrange("p a d -> p (a d)")
            nc.vector.tensor_tensor(xb, xb, psV[:, DM:], ALU.add).then_inc(s_x, 1)

        LEAD = 3 if L1 else 2
        A3, V, E2, A2 = (0, 1, 2, 0) if L1 else (0, 2, 3, 5)
        LN, A1 = (0, 3) if L1 else (3, 4)
        CHAIN = 1 if L1 else 6
        SQ = 1 if L1 else None

        def ahead(fn, eng, b, g, p, by):
            e, gg = divmod(g + by, G)
            if exists(b + e):
                fn(eng, b + e, gg, p ^ (e & 1))

        with nc.Block() as block:
            @block.sync
            def _(sp):
                def load(b, p):
                    src = c.dram["ctxT"][ds(b, 1)].rearrange("a p d -> p (a d)")
                    if L1:
                        sp.dma_start(ctx[:, p, 0, 0:SEG], src[:, 0:SEG]).then_inc(s_ctx[p], 16)
                        sp.dma_start(ctx[:, p, 1, SEG:], src[:, SEG:]).then_inc(s_ctx[p], 16)
                    else:
                        sp.dma_start(ctx[:, p, 0, :], src).then_inc(s_ctx[p], 16)
                if L1:
                    sp.wait_ge(s_pad, 1)
                for p in range(2):
                    load(p, p)
                with sp.Fori(0, (B - 2) // 2) as j:
                    for p in range(2):
                        wait(sp, s_v, j * 2 + p + 1)
                        load(j * 2 + p + 2, p)

            @block.tensor
            def _(pe):
                pe.wait_ge(c.s_late, c.n_late)
                pe_A1(pe, 0)
                pe_A2(pe, 0, 0)
                if not L1:
                    pe_A3(pe, 0)
                pe_V(pe, 0, 0)
                pe_A1(pe, 1)
                pe_A2(pe, 1, 1)
                if L1:
                    pe_A3(pe, 0)
                pe_S(pe, 0, 0, 0)
                pe_S(pe, 0, 1, 0)
                if L1:
                    pe_A1(pe, 2)
                pe.wait_ge(s_pre, PRE)

                def body(b, p):
                    for g in range(G):
                        ahead(pe_S, pe, b, g, p, 2)
                        pe_T(pe, b, g)
                        if not L1 and g == A3 and exists(b + 1):
                            pe_A3(pe, b + 1)
                        if g == V and exists(b + 1):
                            pe_V(pe, b + 1, p ^ 1)
                        if g == E2 and exists(b - 1):
                            pe_E2(pe, b - 1)
                        if g == A1 and exists(b + LEAD):
                            pe_A1(pe, b + LEAD)
                        ahead(pe_O, pe, b, g, p, -1)
                        if g == A2 and exists(b + 2):
                            pe_A2(pe, b + 2, p)
                        if L1 and g == A3 and exists(b + 1):
                            pe_A3(pe, b + 1)
                batch_schedule(body, pe.Fori)
                pe_O(pe, B - 1, G - 1, 1)
                pe_E2(pe, B - 1)

            @block.vector
            def _(dve):
                v = nc.vector
                if L1:
                    v.memset(ctx[:], 0.0).then_inc(s_pad, 1)
                dve.wait_ge(c.s_late, c.n_late)
                for b in range(2):
                    ln.dve_stats(dve, b)
                    ln.dve_apply(dve, b, s_xt, b)
                dve_A2(dve, 0)
                dve_A2b(dve, 0)
                if not L1:
                    dve_A3(dve, 0, 0)
                dve_A2(dve, 1)
                dve_S(dve, 0, 0)
                dve_S(dve, 0, 1)
                if L1:
                    ln.dve_stats(dve, 2)
                    ln.dve_apply(dve, 2, s_xt, 2)

                def body(b, p):
                    for g in range(G):
                        if g == 0 and exists(b + 1):
                            dve_A2b(dve, b + 1)
                        ahead(lambda e, bb, gg, pp: dve_S(e, bb, gg), dve, b, g, p, 2)
                        if not L1 and g == A3 + 1 and exists(b + 1):
                            dve_A3(dve, b + 1, 1 - p)
                        if g == LN and exists(b + LEAD):
                            ln.dve_stats(dve, b + LEAD)
                            ln.dve_apply(dve, b + LEAD, s_xt, b + LEAD)
                        if g == 1 and exists(b - 1):
                            dve_E1(dve, b - 1, 1)
                        if g == G // 2 + 1:
                            dve_E1(dve, b, 0)
                        if g == E2 and exists(b - 1):
                            dve_E2(dve, b - 1)
                        if g == CHAIN and exists(b + 2):
                            dve_A2(dve, b + 2)
                batch_schedule(body, dve.Fori)
                dve_E1(dve, B - 1, 1)
                dve_E2(dve, B - 1)

            @block.gpsimd
            def _(pool):
                pool.wait_ge(c.s_late, c.n_late)
                ln.pool_rstd(pool, 0)
                ln.pool_rstd(pool, 1)
                for p in range(2):
                    nc.gpsimd.memset(vx[p][:], 0.0).then_inc(s_z, 1)
                wait(pool, s_z, 2)
                for p in range(2):
                    for odd in range(2):
                        for i in range(2 if L1 else 1):
                            dst = slots(p, odd, 1, i)
                            if L1:
                                shape = list(dst.shape)
                                seg = c.mask_seg[:, i:i + 1].unsqueeze(2).unsqueeze(3).to_broadcast(shape)
                                last = nc.gpsimd.tensor_copy(dst, seg)
                            else:
                                last = nc.gpsimd.memset(dst, 1.0)
                    last.then_inc(s_pre, 1)
                pool_A2(pool, 0)
                pool_A3(pool, 0, 0)
                pool_A2(pool, 1)
                if L1:
                    ln.pool_rstd(pool, 2)

                def body(b, p):
                    if L1 and exists(b + LEAD):
                        ln.pool_rstd(pool, b + LEAD)
                    if exists(b + 1):
                        pool_A3(pool, b + 1, 1 - p)
                    if not L1 and exists(b + LEAD):
                        ln.pool_rstd(pool, b + LEAD)
                    if exists(b + 2):
                        pool_A2(pool, b + 2)
                batch_schedule(body, pool.Fori)

            @block.scalar
            def _(act):
                act_A1(act, 0)
                act_square(act, 0)
                if not L1:
                    act_A3(act, 0, 0)
                act_A1(act, 1)
                if not L1:
                    act_A3b(act, 0, 0)
                act.wait_ge(s_pre, PRE)
                act_V(act, 0, 0)
                if L1:
                    act_A3(act, 0, 0)
                act_square(act, 1)
                act_S(act, 0, 0)
                act_S(act, 0, 1)
                if L1:
                    act_A1(act, 2)

                def body(b, p):
                    for g in range(G):
                        act_T(act, b, g)
                        if not L1 and g == A3 and exists(b + 1):
                            act_A3(act, b + 1, 1 - p)
                        if not L1 and g == A3 + 2 and exists(b + 1):
                            act_A3b(act, b + 1, 1 - p)
                        if g == V and exists(b + 1):
                            act_V(act, b + 1, 1 - p)
                        if g == A1 and exists(b + LEAD):
                            act_A1(act, b + LEAD)
                        ahead(lambda e, bb, gg, pp: act_S(e, bb, gg), act, b, g, p, 2)
                        if L1 and g == A3 and exists(b + 1):
                            act_A3(act, b + 1, 1 - p)
                        if g == SQ and exists(b + 2):
                            act_square(act, b + 2)
                        if g == 0 and exists(b - 1):
                            act_E1(act, b - 1, 1)
                        if g == G // 2:
                            act_E1(act, b, 0)
                batch_schedule(body, act.Fori)
                act_E1(act, B - 1, 1)


def rotation_tables(c):
    nc = c.nc
    FREQ = (1.0, 0.01)
    c.cos2 = c.sb("cos2", [P, B, 8])
    c.sin2 = c.sb("sin2", [P, B, 8])
    with ExitStack() as st:
        ang = c.sb("rt_ang", [P, B * 4], F32, st)
        kk = c.sb("rt_k", [P, B * 4], F32, st)
        kr = c.sb("rt_kr", [P, B * 4], F32, st)
        red = [c.sb(f"rt_red{i}", [P, B * 4], F32, st) for i in range(4)]
        ab = c.sb("rt_abs", [P, B * 4], F32, st)
        sn = c.sb("rt_sin", [P, B * 4], F32, st)
        cs = c.sb("rt_cos", [P, B * 4], F32, st)
        half_pi = c.sb("rt_half_pi", [P, 1], F32, st)
        over, over_stack = c.passing_over()
        s_ch, s_red, s_act = c.sem("rt_chain"), c.sem("rt_reduced"), c.sem("rt_functions")
        with nc.Block() as block:
            @block.gpsimd
            def _(pool):
                for s in over:
                    pool.sem_clear(s)

            @block.vector
            def _(dve):
                v = nc.vector
                n = 0

                def link(ins):
                    nonlocal n
                    n += 1
                    ins.then_inc(s_ch, 1)
                    dve.wait_ge(s_ch, n)
                v.memset(half_pi[:], 1.5707963267948966).then_inc(s_red, 1)
                dve.wait_ge(c.s_late, c.n_late)
                pos = c.pos[:].rearrange("p b a -> p (b a)")
                a3 = ang[:].rearrange("p (q f) -> p q f", f=2)
                for i, f in enumerate(FREQ):
                    link(v.tensor_scalar(a3[:, :, i], pos, f, None, ALU.mult))
                link(v.tensor_scalar(kk[:], ang[:], 0.15915494309189535, MAGIC, ALU.mult, ALU.add))
                link(v.tensor_scalar(kr[:], kk[:], -MAGIC, None, ALU.add))
                src = ang
                for i, part in enumerate(TWO_PI):
                    link(v.scalar_tensor_tensor(red[i][:], kr[:], -part, src[:], ALU.mult, ALU.add))
                    src = red[i]
                v.tensor_scalar(red[3][:], src[:], PI_LOW, -PI_LOW, ALU.min, ALU.max).then_inc(s_red, 1)
                dve.wait_ge(s_act, 3)
                for i, sign in ((0, -1.0), (1, 1.0)):
                    s8 = c.sin2[:].rearrange("p b (r i) -> p (b r) i", i=2)
                    c8 = c.cos2[:].rearrange("p b (r i) -> p (b r) i", i=2)
                    v.tensor_scalar(s8[:, :, i], sn[:], sign, None, ALU.mult)
                    v.tensor_copy(c8[:, :, i], cs[:])

            @block.scalar
            def _(act):
                act.wait_ge(s_red, 2)
                nc.scalar.activation(sn[:], red[3][:], ACT.Sin).then_inc(s_act, 1)
                nc.scalar.activation(ab[:], red[3][:], ACT.Abs).then_inc(s_act, 1)
                act.wait_ge(s_act, 2)
                nc.scalar.activation(cs[:], ab[:], ACT.Sin, bias=half_pi[:], scale=-1.0).then_inc(s_act, 1)
        over_stack.close()


def moe(c, name, E, TOP, EX, chunks, downs, shared=False):
    nc, d = c.nc, c.dram
    pack = d[name + "_pack"]
    U, WP = pack.shape[0], pack.shape[2]
    FT = chunks[-1][0] + chunks[-1][1]
    NCH = len(chunks)
    ES = E + (1 if shared else 0)
    BP = 2 * EX
    with ExitStack() as st:
        sb = lambda n, shape, dt=F32: c.sb(f"{name}moe_{n}", shape, dt, st)
        ps = lambda n, shape: c.ps(f"{name}moe_{n}", shape, F32, st)
        S = lambda n: c.sem(f"{name}moe_{n}")
        norm = GroupNorm(c, f"{name}moe", st)
        wr = sb("router", [P, KC, E])
        bias = sb("bias", [P, E])
        xb = [sb(f"xb{p}", [P, KC, P]) for p in range(2)]
        lg = sb("lg", [P, B, E])
        val = sb("val", [P, B, E])
        key = sb("key", [P, B, E])
        tmp = sb("tmp", [P, B, E])
        col = sb("col", [P, B])
        rank = sb("rank", [P, B, E])
        cw = sb("cw", [P, ES, B])
        cmp_ = sb("cmp", [P, B, E, E])
        wt = [sb(f"w{p}", [P, WP]) for p in range(2)]
        wm = sb("wm", [P, WP])
        wh = [sb(f"wh{p}", [P, WP], F32R) for p in range(2)]
        wl = [sb(f"wl{p}", [P, WP], F32R) for p in range(2)]
        xm = [sb(f"xm{p}", [P, KC, P]) for p in range(2)]
        xh = sb("xh", [P, KC, B * P], F32R)
        xl = sb("xl", [P, KC, B * P], F32R)
        cwe = [sb(f"cwe{p}", [P, EX, B]) for p in range(2)]
        sg = [sb(f"sg{p}", [P, 512]) for p in range(2)]
        hf = [sb(f"hf{p}", [P, 512]) for p in range(2)]
        hm = [sb(f"hm{p}", [P, 512]) for p in range(2)]
        hh = [[sb(f"hh{p}_{i}", [P, 512], F32R) for i in range(NCH)] for p in range(2)]
        hl = [[sb(f"hl{p}_{i}", [P, 512], F32R) for i in range(NCH)] for p in range(2)]
        psG = [ps(f"psG{p}", [P, 512]) for p in range(2)]
        psU = [ps(f"psU{p}", [P, 512]) for p in range(2)]
        psY = [ps(f"psY{p}", [P, 2, DM]) for p in range(4)]
        s_r, s_w = S("router_loaded"), [S(f"weights_loaded{p}") for p in range(2)]
        s_xt, s_xb, s_lg, s_lc = S("x_transposed"), S("xb_copied"), S("logits_made"), S("logits_copied")
        s_ch, s_d, s_e, s_cw, s_ce = (S("gate_chain"), S("gate_shifted"), S("gate_exps"),
                                      S("gates_done"), S("unit_gates"))
        s_g, s_u, s_sg, s_h, s_y, s_x = (S("gate_made"), S("up_made"), S("silu_done"), S("hidden_done"),
                                         S("down_made"), S("x_added"))

        s_z = S("comparisons_zeroed")
        s_wm, s_wh, s_wl = S("weights_masked"), S("weights_high"), S("weights_low")
        s_xm, s_xh, s_xl = S("x_masked"), S("x_high"), S("x_low")
        s_hm, s_hh, s_hl = S("hidden_masked"), S("hidden_high"), S("hidden_low")

        def gate_w(ww, k, ch):
            o, m = chunks[ch]
            return ww[:, k * FT + o:k * FT + o + m]

        def up_w(ww, k, ch):
            o, m = chunks[ch]
            return ww[:, (KC + k) * FT + o:(KC + k) * FT + o + m]

        def down_w(ww, ch):
            return ww[:, 2 * KC * FT + ch * DM:2 * KC * FT + (ch + 1) * DM]

        def dve_split(dve, u, p):
            wait(dve, s_w[p], (u - p) * 8 + 16)
            wait(dve, s_wh, u)
            wait(dve, s_wl, u)
            nc.vector.tensor_scalar(wm[:].bitcast(I32), wt[p][:].bitcast(I32), HIGH_BITS, None, ALU.bitwise_and).then_inc(s_wm, 1)

        def act_split(act, u, p):
            wait(act, s_wm, u + 1)
            wait(act, s_y, (u - 1) * (NG * BP))
            nc.scalar.copy(wh[p][:], wm[:]).then_inc(s_wh, 1)

        def pool_split(pool, u, p):
            wait(pool, s_wm, u + 1)
            wait(pool, s_y, (u - 1) * (NG * BP))
            nc.gpsimd.tensor_tensor(wl[p][:], wt[p][:], wm[:], ALU.subtract).then_inc(s_wl, 1)

        def units(body, loop):
            body(0, 0, True)
            body(1, 1, True)
            with loop(1, (U - 1) // 2) as j:
                body(j * 2, 0, True)
                body(j * 2 + 1, 1, True)
            for u in range((U - 1) // 2 * 2, U):
                body(u, u % 2, u < U - 1)

        def steps(u, p, more):
            for q in range(NG):
                yield q, ((u, q + 1, p) if q < NG - 1 else (u + 1, 0, 1 - p) if more else None)

        with nc.Block() as block:
            @block.sync
            def _(sp):
                sp.dma_start(wr[:], d[name + "_router"].rearrange("(k p) e -> p k e", p=P)).then_inc(s_r, 16)
                if shared:
                    sp.dma_start(bias[:], d[name + "_bias"].rearrange("(o e) -> o e", o=1).to_broadcast([P, E])).then_inc(s_r, 16)
                for p in range(2):
                    sp.dma_start(wt[p][:], pack[p]).then_inc(s_w[p], 16)

                def load(u, p):
                    wait(sp, s_wl, u - 1)
                    sp.dma_start(wt[p][:], pack[ds(u, 1)].rearrange("a p n -> p (a n)")).then_inc(s_w[p], 16)
                with sp.Fori(1, U // 2) as j:
                    load(j * 2, 0)
                    load(j * 2 + 1, 1)
                if U % 2:
                    load(U - 1, 0)

            @block.tensor
            def _(pe):
                pe.wait_ge(s_r, 16 + 16 * shared)

                def transposes(i, p):
                    wait(pe, norm.s_xn, i + 1)
                    wait(pe, s_xb, i - 1)
                    for k in range(KC):
                        last = nc.tensor.transpose(psG[p][:, k * P:(k + 1) * P], norm.xn[p][:, k * P:(k + 1) * P], c.ident[:])
                    last.then_inc(s_xt, 1)

                def logits(i, p):
                    wait(pe, s_xb, i + 1)
                    wait(pe, s_lc, i - 1)
                    for k in range(KC):
                        last = nc.tensor.matmul(psU[p][:, 0:E], xb[p][:, k, :], wr[:, k, :], start=k == 0, stop=k == KC - 1)
                    last.then_inc(s_lg, 1)
                transposes(0, 0)
                transposes(1, 1)
                logits(0, 0)

                def pair(j):
                    transposes(j * 2, 0)
                    logits(j * 2 - 1, 1)
                    transposes(j * 2 + 1, 1)
                    logits(j * 2, 0)
                pair(1)
                with pe.Fori(2, B // 2) as j:
                    pair(j)
                logits(B - 1, 1)
                pe.wait_ge(s_xh, B)
                pe.wait_ge(s_xl, B)
                pe.wait_ge(s_lc, B)

                def gate_up(u, q, p):
                    if q == 0:
                        wait(pe, s_wh, u + 1)
                        wait(pe, s_wl, u + 1)
                    for ch in range(NCH):
                        m = (u * NG + q) * NCH + ch
                        i, rows = (q * NCH + ch) % 2, chunks[ch][1]
                        wait(pe, s_h, m - 1)
                        for ww, dst, s in ((gate_w, psG, s_g), (up_w, psU, s_u)):
                            parts = [(k, a, b) for k in range(KC) for a, b in ((wh, xh), (wl, xh), (wh, xl))]
                            for j, (k, a, b) in enumerate(parts):
                                last = nc.tensor.matmul(dst[i][0:rows, :], ww(a[p], k, ch), b[:, k, q * 512:(q + 1) * 512],
                                                        start=j == 0, stop=j == len(parts) - 1)
                            last.then_inc(s, 1)

                def down(u, q, p):
                    n = u * NG + q
                    wait(pe, s_hh, (n + 1) * NCH)
                    wait(pe, s_hl, (n + 1) * NCH)
                    for j in range(BP):
                        r = n * BP + j
                        wait(pe, s_x, (r - 3) * 2)
                        for i in range(2):
                            t, e = 2 * (j // EX) + i, j % EX
                            parts = [(d3, a, b) for d3 in downs[e] for a, b in ((hh, wh), (hl, wh), (hh, wl))]
                            for k, ((ch, r0, rn), a, b) in enumerate(parts):
                                last = nc.tensor.matmul(psY[(q * BP + j) % 4][:, i, :],
                                                        a[q % 2][ch][r0:r0 + rn, t * P:(t + 1) * P],
                                                        down_w(b[p], ch)[r0:r0 + rn, :],
                                                        start=k == 0, stop=k == len(parts) - 1)
                        last.then_inc(s_y, 1)
                gate_up(0, 0, 0)

                def unit(u, p, more):
                    for q, nxt in steps(u, p, more):
                        if nxt:
                            gate_up(*nxt)
                        down(u, q, p)
                units(unit, pe.Fori)

            @block.vector
            def _(dve):
                v = nc.vector
                if shared:
                    v.memset(cw[:, E:, :], 1.0).then_inc(s_cw, 1)

                def mask_x(i, p):
                    wait(dve, s_xb, i + 1)
                    wait(dve, s_xl, i - 1)
                    wait(dve, s_xh, i - 1)
                    v.tensor_scalar(xm[p][:].bitcast(I32), xb[p][:].bitcast(I32), HIGH_BITS, None, ALU.bitwise_and).then_inc(s_xm, 1)

                norm.dve_stats(dve, 0)

                def group(g, more):
                    if more:
                        norm.dve_stats(dve, g + 1)
                    for t in range(norm.N):
                        norm.dve_apply(dve, g, t, s_xt)
                        if t or not isinstance(g, int) or g:
                            mask_x(g * norm.N + t - 1, (t - 1) % 2)
                    if isinstance(g, int) and not g:
                        dve_split(dve, 0, 0)
                norm.groups(group, dve.Fori)
                mask_x(B - 1, 1)

                dve.wait_ge(s_lc, B)
                n = 0

                def link(ins):
                    nonlocal n
                    n += 1
                    ins.then_inc(s_ch, 1)
                    dve.wait_ge(s_ch, n)
                if shared:
                    dve.wait_ge(s_e, 1)
                    link(v.tensor_scalar(tmp[:], key[:], 1.0, None, ALU.add))
                    link(v.reciprocal(val[:], tmp[:]))
                    dve.wait_ge(s_r, 32)
                    link(v.tensor_tensor(key[:], val[:], bc(bias[:], 1, B), ALU.add))
                    ranked = key
                else:
                    link(v.tensor_reduce(col[:], lg[:], AX.X, ALU.max))
                    v.tensor_tensor(tmp[:], lg[:], bc(col[:], 2, E), ALU.subtract).then_inc(s_d, 1)
                    dve.wait_ge(s_e, 1)
                    ranked = lg
                    if name == "L1":
                        link(v.tensor_reduce(col[:], key[:], AX.X, ALU.add))
                        link(v.reciprocal(col[:], col[:]))
                        link(v.tensor_tensor(val[:], key[:], bc(col[:], 2, E), ALU.mult))
                        ranked = val
                dve.wait_ge(s_z, 1)
                for j in range(E):
                    kj = ranked[:, :, j]
                    if j > 0:
                        last = v.tensor_tensor(cmp_[:, :, 0:j, j], bc(kj, 2, j), ranked[:, :, 0:j], ALU.is_gt)
                    if j < E - 1:
                        last = v.tensor_tensor(cmp_[:, :, j + 1:, j], bc(kj, 2, E - 1 - j), ranked[:, :, j + 1:], ALU.is_ge)
                link(last)
                link(v.tensor_reduce(rank[:], cmp_[:], AX.X, ALU.add))
                link(v.tensor_scalar(rank[:], rank[:], float(TOP), None, ALU.is_lt))
                vals = key if name == "L0" else val
                cwt = cw[:, 0:E, :].rearrange("p e b -> p b e")
                if name == "L1":
                    v.tensor_tensor(cwt, vals[:], rank[:], ALU.mult).then_inc(s_cw, 1)
                else:
                    link(v.tensor_tensor(tmp[:], vals[:], rank[:], ALU.mult))
                    link(v.tensor_reduce(col[:], tmp[:], AX.X, ALU.add))
                    link(v.reciprocal(col[:], col[:]))
                    v.tensor_tensor(cwt, tmp[:], bc(col[:], 2, E), ALU.mult).then_inc(s_cw, 1)

                def hidden(u, q, p):
                    nn = u * NG + q
                    for ch in range(NCH):
                        m = nn * NCH + ch
                        i, rows = (q * NCH + ch) % 2, chunks[ch][1]
                        wait(dve, s_u, m + 1)
                        wait(dve, s_sg, m + 1)
                        wait(dve, s_hl, m - 1)
                        v.tensor_tensor(hf[i][0:rows, :], sg[i][0:rows, :], psU[i][0:rows, :], ALU.mult).then_inc(s_h, 1)
                        wait(dve, s_h, m + 1)
                        wait(dve, s_hh, m - 1)
                        v.tensor_scalar(hm[i][0:rows, :].bitcast(I32), hf[i][0:rows, :].bitcast(I32),
                                        HIGH_BITS, None, ALU.bitwise_and).then_inc(s_hm, 1)

                def add(u, q, p):
                    nn = u * NG + q
                    if q == 0:
                        wait(dve, s_ce, u + 1)
                    for j in range(BP):
                        r = nn * BP + j
                        wait(dve, s_y, r + 1)
                        for i in range(2):
                            t, e = 4 * q + 2 * (j // EX) + i, j % EX
                            if i == 0 and (e or j == 0):
                                wait(dve, s_x, r * 2)
                            v.scalar_tensor_tensor(c.x[:, t, :], psY[(q * BP + j) % 4][:, i, :],
                                                   cwe[p][:, e, t:t + 1], c.x[:, t, :], ALU.mult, ALU.add).then_inc(s_x, 1)
                hidden(0, 0, 0)

                def unit(u, p, more):
                    for q, nxt in steps(u, p, more):
                        if nxt:
                            hidden(*nxt)
                        if q == 0 and more:
                            dve_split(dve, u + 1, 1 - p)
                        add(u, q, p)
                units(unit, dve.Fori)

            @block.gpsimd
            def _(pool):
                def split_x(i, p):
                    wait(pool, s_xm, i + 1)
                    nc.gpsimd.tensor_tensor(xl[:, :, ds(i * P, P)], xb[p][:], xm[p][:], ALU.subtract).then_inc(s_xl, 1)
                norm.pool_rstd(pool, 0)

                def group(g, more):
                    if more:
                        norm.pool_rstd(pool, g + 1)
                    for t in range(norm.N):
                        if t or not isinstance(g, int) or g:
                            split_x(g * norm.N + t - 1, (t - 1) % 2)
                    if isinstance(g, int) and not g:
                        nc.gpsimd.memset(cmp_[:], 0.0).then_inc(s_z, 1)
                        pool_split(pool, 0, 0)
                norm.groups(group, pool.Fori)
                split_x(B - 1, 1)
                pool.wait_ge(s_cw, 1 + shared)

                def gates(u, p):
                    wait(pool, s_x, (u - 1) * (NG * BP * 2))
                    nc.gpsimd.tensor_copy(cwe[p][:], cw[:, ds(u * EX, EX), :]).then_inc(s_ce, 1)
                gates(0, 0)

                def low(u, q, p):
                    nn = u * NG + q
                    for ch in range(NCH):
                        m = nn * NCH + ch
                        i, rows = (q * NCH + ch) % 2, chunks[ch][1]
                        wait(pool, s_hm, m + 1)
                        wait(pool, s_y, (nn - 1) * BP)
                        nc.gpsimd.tensor_tensor(hl[q % 2][ch][0:rows, :], hf[i][0:rows, :], hm[i][0:rows, :],
                                                ALU.subtract).then_inc(s_hl, 1)
                low(0, 0, 0)

                def unit(u, p, more):
                    for q, nxt in steps(u, p, more):
                        if nxt:
                            low(*nxt)
                        if q == 0 and more:
                            pool_split(pool, u + 1, 1 - p)
                        if q == 1 and more:
                            gates(u + 1, 1 - p)
                units(unit, pool.Fori)

            @block.scalar
            def _(act):
                def copy_x(i, p):
                    wait(act, s_xt, i + 1)
                    wait(act, s_lg, i - 1)
                    wait(act, s_xl, i - 1)
                    nc.scalar.copy(xb[p][:], psG[p][:, 0:DM].rearrange("p (k n) -> p k n", k=KC)).then_inc(s_xb, 1)

                def copy_rest(i, p):
                    wait(act, s_xm, i + 1)
                    nc.scalar.copy(xh[:, :, ds(i * P, P)], xm[p][:]).then_inc(s_xh, 1)
                    wait(act, s_lg, i + 1)
                    nc.scalar.copy(lg[:, ds(i, 1), :], psU[p][:, 0:E].rearrange("p (a e) -> p a e", a=1)).then_inc(s_lc, 1)
                copy_x(0, 0)

                def pair(j):
                    copy_x(j * 2 - 1, 1)
                    copy_rest(j * 2 - 2, 0)
                    copy_x(j * 2, 0)
                    copy_rest(j * 2 - 1, 1)
                pair(1)
                with act.Fori(2, B // 2) as j:
                    pair(j)
                copy_x(B - 1, 1)
                copy_rest(B - 2, 0)
                copy_rest(B - 1, 1)
                act_split(act, 0, 0)
                if shared:
                    act.wait_ge(s_lc, B)
                    nc.scalar.activation(key[:], lg[:], ACT.Exp, scale=-1.0).then_inc(s_e, 1)
                else:
                    act.wait_ge(s_d, 1)
                    nc.scalar.activation(key[:], tmp[:], ACT.Exp).then_inc(s_e, 1)

                def silu(u, q, p):
                    nn = u * NG + q
                    for step in range(NCH + 1):
                        if step < NCH:
                            m, i, rows = nn * NCH + step, (q * NCH + step) % 2, chunks[step][1]
                            wait(act, s_g, m + 1)
                            wait(act, s_h, m - 1)
                            nc.scalar.activation(sg[i][0:rows, :], psG[i][0:rows, :], ACT.Silu).then_inc(s_sg, 1)
                        if step > 0:
                            ch = step - 1
                            m, i, rows = nn * NCH + ch, (q * NCH + ch) % 2, chunks[ch][1]
                            wait(act, s_hm, m + 1)
                            wait(act, s_y, (nn - 1) * BP)
                            nc.scalar.copy(hh[q % 2][ch][0:rows, :], hm[i][0:rows, :]).then_inc(s_hh, 1)
                silu(0, 0, 0)

                def unit(u, p, more):
                    for q, nxt in steps(u, p, more):
                        if nxt:
                            silu(*nxt)
                        if q == 0 and more:
                            act_split(act, u + 1, 1 - p)
                units(unit, act.Fori)



def quantized_linear(c):
    nc, w = c.nc, c.w
    with ExitStack() as st:
        sb = lambda n, shape, dt=F32: c.sb(f"q8_{n}", shape, dt, st)
        S = lambda n: c.sem("q8_" + n)
        norm = GroupNorm(c, "q8", st)
        wb = sb("wb", [P, KC, DM], BF16)
        am = sb("am", [P, 2])
        sc = [sb(f"sc{p}", [P, 1]) for p in range(2)]
        isc = sb("isc", [P, 2])
        r1 = sb("r1", [P, DM])
        r2 = sb("r2", [P, DM])
        xq = [sb(f"xq{p}", [P, DM], BF16) for p in range(2)]
        xqT = [sb(f"xqT{p}", [P, KC, P], BF16) for p in range(2)]
        y1 = [sb(f"y1{p}", [P, DM]) for p in range(2)]
        y2 = sb("y2", [P, DM], F16)
        psT = [c.ps(f"q8_psT{p}", [P, KC, P], BF16, st) for p in range(2)]
        psY = [c.ps(f"q8_psY{p}", [P, 512], F32, st) for p in range(2)]
        s_w, s_ch, s_xq, s_xt, s_xT, s_acc, s_y, s_x = (S("weights"), S("chain"), S("quantized"), S("transposed"),
                                                        S("transposed_copied"), S("accumulated"), S("scaled"), S("x_added"))
        CH = 5
        s_yb = S("biased")

        with nc.Block() as block:
            @block.vector
            def _(dve):
                v = nc.vector
                dve.wait_ge(c.s_late, c.n_late)
                v.tensor_copy(wb[:].rearrange("p k n -> p (k n)"),
                              w["fq8"][:].rearrange("p k n -> p (k n)").bitcast(I8)).then_inc(s_w, 1)

                def front(g, t):
                    i, p = g * norm.N + t, t % 2
                    norm.dve_apply(dve, g, t, s_xq)

                    def link(ins, k):
                        ins.then_inc(s_ch, 1)
                        dve.wait_ge(s_ch, i * CH + k)
                    dve.wait_ge(norm.s_xn, i + 1)
                    link(v.tensor_reduce(am[:, 0:1], norm.xn[p][:], AX.X, ALU.max, apply_absolute_value=True), 1)
                    wait(dve, s_y, i - 1)
                    link(v.tensor_scalar(sc[p][:], am[:, 0:1], 1e-7, 1.0 / 127.0, ALU.max, ALU.mult), 2)
                    link(v.reciprocal(isc[:, 0:1], sc[p][:]), 3)
                    link(v.tensor_scalar(r1[:], norm.xn[p][:], isc[:, 0:1], MAGIC, ALU.mult, ALU.add), 4)
                    link(v.tensor_scalar(r2[:], r1[:], -MAGIC, 127.0, ALU.add, ALU.min), 5)
                    wait(dve, s_xt, i - 1)
                    v.tensor_scalar(xq[p][:], r2[:], -128.0, None, ALU.max).then_inc(s_xq, 1)

                def back(i, p):
                    wait(dve, s_acc, i + 1)
                    wait(dve, s_yb, i - 1)
                    v.scalar_tensor_tensor(y1[p][:], psY[p][:, 0:DM], sc[p][:], w["fsc"][:], ALU.mult, ALU.mult).then_inc(s_y, 1)
                norm.dve_stats(dve, 0)

                def group(g, more):
                    if more:
                        norm.dve_stats(dve, g + 1)
                    for t in range(norm.N):
                        if t > 1 or not isinstance(g, int) or g:
                            back(g * norm.N + t - 2, t % 2)
                        front(g, t)
                norm.groups(group, dve.Fori)
                back(B - 2, 0)
                back(B - 1, 1)

            @block.gpsimd
            def _(pool):
                def finish(i, p):
                    wait(pool, s_y, i + 1)
                    wait(pool, s_x, i)
                    nc.gpsimd.tensor_tensor(y2[:], y1[p][:], w["fb"][:], ALU.add).then_inc(s_yb, 1)
                    wait(pool, s_yb, i + 1)
                    xi = c.x[:, ds(i, 1), :].rearrange("p a d -> p (a d)")
                    nc.gpsimd.tensor_tensor(xi, xi, y2[:], ALU.add).then_inc(s_x, 1)
                norm.pool_rstd(pool, 0)

                def group(g, more):
                    if more:
                        norm.pool_rstd(pool, g + 1)
                    for t in range(norm.N):
                        if t > 2 or not isinstance(g, int) or g:
                            finish(g * norm.N + t - 3, (t - 3) % 2)
                norm.groups(group, pool.Fori)
                for i in range(B - 3, B):
                    finish(i, i % 2)

            def pairs(body, loop):
                for p in range(2):
                    body(p, p)
                with loop(1, B // 2) as j:
                    for p in range(2):
                        body(j * 2 + p, p)

            @block.tensor
            def _(pe):
                pe.wait_ge(s_w, 1)
                pe.wait_ge(c.s_late, c.n_late)

                def tile(i, p):
                    wait(pe, s_xq, i + 1)
                    wait(pe, s_xT, i - 1)
                    for k in range(KC):
                        last = nc.tensor.transpose(psT[p][:, k, :], xq[p][:, k * P:(k + 1) * P], c.ident_b[:])
                    last.then_inc(s_xt, 1)
                    wait(pe, s_xT, i + 1)
                    wait(pe, s_y, i - 1)
                    for k in range(KC):
                        last = nc.tensor.matmul(psY[p][:, 0:DM], xqT[p][:, k, :], wb[:, k, :], start=k == 0, stop=k == KC - 1)
                    last.then_inc(s_acc, 1)
                pairs(tile, pe.Fori)

            @block.scalar
            def _(act):
                def tile(i, p):
                    wait(act, s_xt, i + 1)
                    wait(act, s_acc, i - 1)
                    nc.scalar.copy(xqT[p][:], psT[p][:]).then_inc(s_xT, 1)
                pairs(tile, act.Fori)


def store(c, out):
    s_out = c.sem("stored")
    with c.nc.Block() as block:
        @block.sync
        def _(sp):
            sp.wait_ge(c.s_late, c.n_late)
            sp.dma_start(out.rearrange("b p d -> p b d"), c.x[:]).then_inc(s_out, 16)
            sp.wait_ge(s_out, 16)


STOP = 8


def build(nc, dram, out):
    with ExitStack() as stack:
        c = Core(nc, dram, stack)
        load_everything_small(c)
        whole = [(0, P)]
        rest = 176 - P
        parts = [
            lambda: (l0_attention(c), c.layer0.close()),
            lambda: moe(c, "L0", 8, 2, 1, whole, [[(0, 0, P)]]),
            lambda: small_attention(c, "L1"),
            lambda: moe(c, "L1", 16, 6, 2, [(0, P), (P, P), (2 * P, 64 + rest)],
                        [[(0, 0, P), (2, 0, rest)], [(1, 0, P), (2, 64, rest)]]),
            lambda: (rotation_tables(c), small_attention(c, "L2")),
            lambda: quantized_linear(c),
            lambda: small_attention(c, "L3"),
            lambda: moe(c, "L3", 16, 4, 1, whole, [[(0, 0, P)]], shared=True),
        ]
        for part in parts[:STOP]:
            part()
        store(c, out)
        c.passing.close()


_SHAPE = (B, P, DM)


def kernel(**inputs):
    import numpy as np
    import concourse.bacc as bacc
    from concourse.bass_utils import run_bass_kernel_spmd

    a = {k: np.asarray(v) for k, v in inputs.items()}

    def packed(g, u, dn):
        n = g.shape[0]
        cut = lambda m: m.reshape(n, KC, P, m.shape[2]).transpose(0, 2, 1, 3).reshape(n, P, -1)
        return np.concatenate([cut(g), cut(u), dn.reshape(n, P, -1)], axis=2)

    t = lambda m: m.transpose(0, 2, 1)
    d = {k: a[k] for k in a if "_xattn_" in k or k in ("x", "fside_BxSx2_0", "L2_ffn_w_scale", "L2_ffn_bias")}
    d["ctxT"] = t(a["ctx_1024"])
    d["L2_ffn_weight"] = np.ascontiguousarray(a["L2_ffn_weight"].T).view(np.int32)
    wq = a["L0_xattn_Wq"].reshape(KC, P, 4, 512).transpose(1, 2, 0, 3).reshape(P, 4, 1024)
    wk, wv = (a["L0_xattn_" + n].reshape(P, 4, 512) for n in ("Wk", "Wv"))
    wo = a["L0_xattn_Wo"].reshape(4, 4, P, DM).transpose(2, 0, 1, 3).reshape(P, 4, 1024)
    d["L0_attn"] = np.concatenate([wq, wk, wv, wo], axis=2)
    d["L0_router"] = a["L0_ffn_router_w"].T
    d["L0_pack"] = packed(a["L0_ffn_w1"], a["L0_ffn_w2"], a["L0_ffn_w3"])
    d["L1_router"] = a["L1_ffn_gate_w"].T

    def pairs(m):
        m = m.reshape(8, 2, DM, 176)
        gap = np.zeros((8, DM, 16), m.dtype)
        return np.concatenate([m[:, 0, :, :P], m[:, 1, :, :P], m[:, 0, :, P:], gap, m[:, 1, :, P:]], axis=2)
    dn = pairs(a["L1_ffn_w_down"])
    dn = np.concatenate([dn, np.zeros((8, DM, 16), dn.dtype)], axis=2)
    dn = dn.reshape(8, DM, 3, P).transpose(0, 3, 2, 1)
    d["L1_pack"] = packed(pairs(t(a["L1_ffn_w_gate"])), pairs(t(a["L1_ffn_w_up"])), dn)
    heads = np.concatenate([a["L1_xattn_Wk"], a["L1_xattn_Wv"]], axis=1).reshape(CD, 16, 2, 16)
    biases = np.concatenate([a["L1_xattn_bk"], a["L1_xattn_bv"]]).reshape(16, 2, 16)
    for i, n in enumerate(("L1_k", "L1_v")):
        d[n], d[n + "_bias"] = heads[:, :, i].reshape(CD, DM), biases[:, i].reshape(DM)
    wo = a["L1_xattn_Wo"].reshape(8, 1, 32, DM)
    d["L1_o"] = np.concatenate([wo, wo], axis=1).reshape(2 * DM, DM)
    d["L3_router"] = a["L3_ffn_gate_w"].T
    d["L3_bias"] = a["L3_ffn_expert_bias"]
    both = lambda e, s: np.concatenate([t(a["L3_ffn_" + e]), t(a["L3_ffn_" + s][None])])
    d["L3_pack"] = packed(both("w_gate", "sw_gate"), both("w_up", "sw_up"), both("w_down", "sw_down"))
    p = np.arange(P)
    f = np.float32
    d["c_ident"] = np.eye(P, dtype=f)
    d["c_neg_half"] = np.full((P, 32), -0.5, f)
    d["c_ones"] = np.ones((1, P), f)
    d["c_mask8"] = ((p[:, None] // 8) % 4 == np.arange(4)).astype(f)
    d["c_mask16"] = ((p[:, None] // 16) % 4 == np.arange(4)).astype(f)
    seg = np.stack([p < P - 16, p >= P - 16], axis=1).astype(f)
    d["c_mask_seg"] = seg
    d["c_sel_seg"] = seg.T

    nc = bacc.Bacc("TRN2", target_bir_lowering=False, num_devices=1)
    arrays, dram = {}, {}
    for name, m in d.items():
        m = np.ascontiguousarray(m)
        arrays["in_" + name] = m
        dram[name] = nc.dram_tensor("in_" + name, m.shape, mybir.dt.from_np(m.dtype), kind="ExternalInput").ap()
    out = nc.dram_tensor("out", _SHAPE, F32, kind="ExternalOutput").ap()
    build(nc, dram, out)
    r = run_bass_kernel_spmd(nc, [arrays], core_ids=[0])
    return r.results[0]["out"]
```
